# Optimizing a Trainium2 kernel written in Bass

```python
import numpy as np
import jax
import jax.numpy as jnp

def _softmax(x, axis=-1):
    return jax.nn.softmax(x, axis=axis)

def _gelu(x):
    return jax.nn.gelu(x, approximate=True)

def _silu(x):
    return jax.nn.silu(x)

def _sigmoid(x):
    return jax.nn.sigmoid(x)

def _layernorm(x, axis=-1, eps=1e-05):
    m = jnp.mean(x, axis=axis, keepdims=True)
    v = jnp.var(x, axis=axis, keepdims=True)
    return (x - m) / jnp.sqrt(v + eps)

def _scatter_add(tgt, idx, src, axis=0):
    return tgt.at[idx].add(src)

def _segment_sum(src, seg, n):
    return jax.ops.segment_sum(src, seg, n)
kernel_name = 'mk_gnn_ffn_d4_gnn_r64_ac729c'

def setup_inputs(seed: int=0):
    np.random.seed(seed)
    _w = jnp.asarray

    def _rec_inputs():
        import jax
        import jax.numpy as jnp
        _gk = jax.random.key(seed)
        x = -0.000125 + 0.9999 * jax.random.normal(jax.random.fold_in(_gk, 1), (1024, 512), jnp.float32)
        _s = jax.random.randint(jax.random.fold_in(_gk, 2), (8192,), 0, 1024, jnp.int32)
        _d = jax.random.randint(jax.random.fold_in(_gk, 3), (8192,), 0, 1024, jnp.int32)
        _loop = jnp.arange(1024, dtype=jnp.int32)
        src = jnp.concatenate([_s, _d, _loop])
        dst = jnp.concatenate([_d, _s, _loop])
        _o = jnp.argsort(dst, stable=True)
        src = src[_o]
        dst = dst[_o]
        edge_attr_20 = jax.random.uniform(jax.random.fold_in(_gk, 12), (17408, 20), jnp.float32, 0.0, 0.999999)
        edge_attr_3 = -0.0005747 + 0.998114 * jax.random.normal(jax.random.fold_in(_gk, 13), (17408, 3), jnp.float32)
        edge_type_4 = jax.random.randint(jax.random.fold_in(_gk, 15), (17408,), 0, 4, jnp.int32)
        edge_weight = jax.random.uniform(jax.random.fold_in(_gk, 16), (17408,), jnp.float32, 0.0, 0.999998)
        return (x, src, dst, edge_attr_20, edge_attr_3, edge_type_4, edge_weight)
    x, src, dst, edge_attr_20, edge_attr_3, edge_type_4, edge_weight = _rec_inputs()

    def _L0_gnn_setup():
        import jax, jax.numpy as jnp
        import numpy as np
        N_NODES = 1024
        N_EDGES = 8192
        FEAT_DIM = 512
        EMBED_DIM = 512
        key = jax.random.key(seed)
        k1, k2, k3, k4, k5 = jax.random.split(key, 5)
        x = jax.random.normal(k1, (N_NODES, FEAT_DIM), dtype=jnp.float32)
        limit = float(np.sqrt(6.0 / (EMBED_DIM + FEAT_DIM)))
        weight = jax.random.uniform(k2, (EMBED_DIM, FEAT_DIM), dtype=jnp.float32, minval=-limit, maxval=limit)
        row = jax.random.randint(k3, (N_EDGES,), 0, N_NODES, dtype=jnp.int64)
        col = jax.random.randint(k4, (N_EDGES,), 0, N_NODES, dtype=jnp.int64)
        vals = jax.random.uniform(k5, (N_EDGES,), dtype=jnp.float32)
        return {'x': x, 'weight': weight, 'row': row, 'col': col, 'vals': vals}
    _L0_gnn_all = _L0_gnn_setup()
    _L0_gnn_in = {k: v for k, v in _L0_gnn_all.items() if k in ('weight',)}
    del _L0_gnn_all

    def _L0_ffn_setup():
        import jax, jax.numpy as jnp
        import numpy as np
        from jax import lax
        N_HEADS = 8
        D_KEYS = 128
        HALF = D_KEYS // 2
        N_KEYS = 256
        TOP_K = 8
        D_MODEL = 512

        def _forward(queries, Wq, bq, keys, w_down, w_up):
            N, T, D = queries.shape
            x = queries.reshape(-1, D)
            q = (x @ Wq + bq).reshape(-1, N_HEADS, D_KEYS)
            q1, q2 = (q[..., :HALF], q[..., HALF:])
            s1 = jnp.einsum('bhc,hnc->bhn', q1, keys[:, 0])
            s2 = jnp.einsum('bhc,hnc->bhn', q2, keys[:, 1])
            s1t, i1 = lax.top_k(s1, TOP_K)
            s2t, i2 = lax.top_k(s2, TOP_K)
            all_scores = (s1t[..., :, None] + s2t[..., None, :]).reshape(-1, N_HEADS, TOP_K * TOP_K)
            all_idx = (i1[..., :, None] * N_KEYS + i2[..., None, :]).reshape(-1, N_HEADS, TOP_K * TOP_K)
            scores, best = lax.top_k(all_scores, TOP_K)
            indices = jnp.take_along_axis(all_idx, best, axis=-1)
            w_d = w_down[indices]
            w_u = w_up[indices]
            inner = jnp.einsum('bd,bhkd->bhk', x, w_d)
            vals = jax.nn.relu(inner) * jax.nn.softmax(scores, axis=-1)
            out = jnp.einsum('bhk,bhkd->bd', vals, w_u)
            return out.reshape(N, T, D)
        key = jax.random.key(seed)
        ks = jax.random.split(key, 6)
        N, T = (2, 1024)
        queries = jax.random.normal(ks[0], (N, T, D_MODEL), dtype=jnp.float32)
        Wq = jax.random.normal(ks[1], (D_MODEL, N_HEADS * D_KEYS), dtype=jnp.float32) / np.sqrt(D_MODEL)
        bq = jnp.zeros((N_HEADS * D_KEYS,), dtype=jnp.float32)
        bound = 1.0 / np.sqrt(HALF)
        keys = jax.random.uniform(ks[2], (N_HEADS, 2, N_KEYS, HALF), dtype=jnp.float32, minval=-bound, maxval=bound)
        w_down = jax.random.normal(ks[3], (N_KEYS * N_KEYS, D_MODEL), dtype=jnp.float32) * 0.02
        w_up = jax.random.normal(ks[4], (N_KEYS * N_KEYS, D_MODEL), dtype=jnp.float32) * 0.02
        return {'queries': queries, 'Wq': Wq, 'bq': bq, 'keys': keys, 'w_down': w_down, 'w_up': w_up}
    _L0_ffn_all = _L0_ffn_setup()
    _L0_ffn_in = {k: v for k, v in _L0_ffn_all.items() if k in ('Wq', 'bq', 'keys', 'w_down', 'w_up')}
    del _L0_ffn_all

    def _L1_gnn_setup():
        import jax, jax.numpy as jnp
        import numpy as np
        DIM = 512
        NUM_REL = 4
        N_NODES = 50000
        N_EDGES = 2500

        def _layer_norm(x, g, b, eps=1e-05):
            mu = jnp.mean(x, axis=-1, keepdims=True)
            var = jnp.mean((x - mu) ** 2, axis=-1, keepdims=True)
            return (x - mu) * jax.lax.rsqrt(var + eps) * g + b
        key = jax.random.key(seed)
        ks = jax.random.split(key, 16)
        s = 1.0 / np.sqrt(DIM)
        inp = {'x': jax.random.normal(ks[0], (N_NODES, DIM), jnp.float32), 'edge_index': jax.random.randint(ks[1], (2, N_EDGES), 0, N_NODES, jnp.int32), 'edge_type': jax.random.randint(ks[2], (N_EDGES,), 0, NUM_REL, jnp.int32), 'edge_weight': jax.random.uniform(ks[3], (N_EDGES,), jnp.float32), 'W_self': jax.random.uniform(ks[4], (DIM, DIM), jnp.float32, -s, s), 'b_self': jnp.zeros((DIM,), jnp.float32), 'W_rel': jax.random.uniform(ks[5], (NUM_REL, DIM, DIM), jnp.float32, -s, s), 'b_rel': jnp.zeros((NUM_REL, DIM), jnp.float32), 'ln1_g': jnp.ones((DIM,), jnp.float32), 'ln1_b': jnp.zeros((DIM,), jnp.float32), 'ln2_g': jnp.ones((DIM,), jnp.float32), 'ln2_b': jnp.zeros((DIM,), jnp.float32), 'W_ffn1': jax.random.uniform(ks[6], (DIM, 2 * DIM), jnp.float32, -s, s), 'b_ffn1': jnp.zeros((2 * DIM,), jnp.float32), 'W_ffn2': jax.random.uniform(ks[7], (2 * DIM, DIM), jnp.float32, -1.0 / np.sqrt(2 * DIM), 1.0 / np.sqrt(2 * DIM)), 'b_ffn2': jnp.zeros((DIM,), jnp.float32)}
        return inp
    _L1_gnn_all = _L1_gnn_setup()
    _L1_gnn_in = {k: v for k, v in _L1_gnn_all.items() if k in ('W_self', 'b_self', 'W_rel', 'b_rel', 'ln1_g', 'ln1_b', 'ln2_g', 'ln2_b', 'W_ffn1', 'b_ffn1', 'W_ffn2', 'b_ffn2')}
    del _L1_gnn_all

    def _L1_ffn_setup():
        import jax, jax.numpy as jnp
        import numpy as np
        import math
        B, T, D = (4, 128, 512)
        E, K, F = (8, 2, 32)
        CAP_FACTOR = 1.25
        key = jax.random.key(seed)
        ks = jax.random.split(key, 4)
        return {'x': jax.random.normal(ks[0], (B, T, D), jnp.float32), 'gate_w': jax.random.normal(ks[1], (E, D), jnp.float32) * 0.01, 'w1': jax.random.normal(ks[2], (E, D, F), jnp.float32) * (1.0 / np.sqrt(D)), 'b1': jnp.zeros((E, F), jnp.float32), 'w2': jax.random.normal(ks[3], (E, F, D), jnp.float32) * (1.0 / np.sqrt(F)), 'b2': jnp.zeros((E, D), jnp.float32)}
    _L1_ffn_all = _L1_ffn_setup()
    _L1_ffn_in = {k: v for k, v in _L1_ffn_all.items() if k in ('gate_w', 'w1', 'b1', 'w2', 'b2')}
    del _L1_ffn_all

    def _L2_gnn_setup():
        import jax, jax.numpy as jnp
        import numpy as np
        N_ATOMS = 5000
        N_EDGES = 50000
        C = 128
        F = 128
        N_RBF = 20
        LOG2 = float(np.log(2.0))
        Y0 = float(1.0 / np.sqrt(4.0 * np.pi))
        Y1_SCALE = float(np.sqrt(3.0 / (4.0 * np.pi)))

        def shifted_softplus(x):
            return jax.nn.softplus(x) - LOG2

        def _forward(x, idx_i, idx_j, f_ij, rcut_ij, r_ij, W_in2f_s, W_in2f_v, Wf1, bf1, Wf2, bf2, W1_s, W1_v, W2_s, W2_v):
            n = x.shape[0]
            e = r_ij.shape[0]
            xs = x[:, :C] @ (W_in2f_s / np.sqrt(C))
            xv = jnp.einsum('nci,cf->nfi', x[:, C:].reshape(n, C, 3), W_in2f_v) / np.sqrt(C)
            sj = xs[idx_j]
            vj = xv[idx_j]
            u = r_ij / jnp.linalg.norm(r_ij, axis=-1, keepdims=True)
            Yv = Y1_SCALE * u
            o0a = sj * Y0
            o0b = jnp.einsum('efi,ei->ef', vj, Yv) / np.sqrt(3.0)
            s2 = jnp.stack([o0a, o0b], axis=-1).reshape(e, 2 * F)
            ova = sj[:, :, None] * Yv[:, None, :]
            ovb = vj * Y0
            v2 = jnp.stack([ova, ovb], axis=2)
            w1 = jnp.cross(vj, Yv[:, None, :]) / np.sqrt(2.0)
            ax, ay, az = (vj[..., 0], vj[..., 1], vj[..., 2])
            bx, by, bz = (Yv[:, None, 0], Yv[:, None, 1], Yv[:, None, 2])
            t = jnp.stack([(ax * by + ay * bx) / np.sqrt(2.0), (ay * bz + az * by) / np.sqrt(2.0), (2.0 * az * bz - ax * bx - ay * by) / np.sqrt(6.0), (az * bx + ax * bz) / np.sqrt(2.0), (ax * bx - ay * by) / np.sqrt(2.0)], axis=-1)
            h = shifted_softplus(f_ij @ Wf1 + bf1)
            W = (h @ Wf2 + bf2) * rcut_ij[:, None]
            m_s = s2 * W[:, :2 * F]
            m_v = (v2.reshape(e, 2 * F, 3) * W[:, 2 * F:4 * F, None]).reshape(e, 6 * F)
            m_w = (w1 * W[:, 4 * F:5 * F, None]).reshape(e, 3 * F)
            m_t = (t * W[:, 5 * F:6 * F, None]).reshape(e, 5 * F)
            x_ij = jnp.concatenate([m_s, m_v, m_w, m_t], axis=1)
            agg = jax.ops.segment_sum(x_ij, idx_i, num_segments=n)
            S = agg[:, :2 * F] @ (W1_s / np.sqrt(2 * F))
            V = jnp.einsum('nmi,mc->nci', agg[:, 2 * F:8 * F].reshape(n, 2 * F, 3), W1_v) / np.sqrt(2 * F)
            S = shifted_softplus(S)
            S = S @ (W2_s / np.sqrt(C))
            V = jnp.einsum('nci,cd->ndi', V, W2_v) / np.sqrt(C)
            return jnp.concatenate([S, V.reshape(n, 3 * C)], axis=1)
        key = jax.random.key(seed)
        ks = jax.random.split(key, 16)
        f32 = jnp.float32
        x = jax.random.normal(ks[0], (N_ATOMS, 4 * C), f32)
        idx_i = jnp.sort(jax.random.randint(ks[1], (N_EDGES,), 0, N_ATOMS))
        idx_j = jax.random.randint(ks[2], (N_EDGES,), 0, N_ATOMS)
        f_ij = jax.random.uniform(ks[3], (N_EDGES, N_RBF), f32)
        rcut_ij = jax.random.uniform(ks[4], (N_EDGES,), f32)
        r_ij = jax.random.normal(ks[5], (N_EDGES, 3), f32)
        W_in2f_s = jax.random.normal(ks[6], (C, F), f32)
        W_in2f_v = jax.random.normal(ks[7], (C, F), f32)
        Wf1 = jax.random.normal(ks[8], (N_RBF, F), f32) / np.sqrt(N_RBF)
        bf1 = 0.1 * jax.random.normal(ks[9], (F,), f32)
        Wf2 = jax.random.normal(ks[10], (F, 6 * F), f32) / np.sqrt(F)
        bf2 = 0.1 * jax.random.normal(ks[11], (6 * F,), f32)
        W1_s = jax.random.normal(ks[12], (2 * F, C), f32)
        W1_v = jax.random.normal(ks[13], (2 * F, C), f32)
        W2_s = jax.random.normal(ks[14], (C, C), f32)
        W2_v = jax.random.normal(ks[15], (C, C), f32)
        return dict(x=x, idx_i=idx_i, idx_j=idx_j, f_ij=f_ij, rcut_ij=rcut_ij, r_ij=r_ij, W_in2f_s=W_in2f_s, W_in2f_v=W_in2f_v, Wf1=Wf1, bf1=bf1, Wf2=Wf2, bf2=bf2, W1_s=W1_s, W1_v=W1_v, W2_s=W2_s, W2_v=W2_v)
    _L2_gnn_all = _L2_gnn_setup()
    _L2_gnn_in = {k: v for k, v in _L2_gnn_all.items() if k in ('W_in2f_s', 'W_in2f_v', 'Wf1', 'bf1', 'Wf2', 'bf2', 'W1_s', 'W1_v', 'W2_s', 'W2_v')}
    del _L2_gnn_all

    def _L2_ffn_setup():
        import jax, jax.numpy as jnp
        import numpy as np
        B, T, D = (4, 128, 512)
        E, F, CAP = (8, 32, 64)
        key = jax.random.key(seed)
        ks = jax.random.split(key, 6)
        s = 0.02
        return {'x': jax.random.normal(ks[0], (B, T, D), dtype=jnp.float32), 'Wr': jax.random.normal(ks[1], (D, E), dtype=jnp.float32) * s, 'W1': jax.random.normal(ks[2], (E, D, F), dtype=jnp.float32) * s, 'b1': jax.random.normal(ks[3], (E, F), dtype=jnp.float32) * s, 'W2': jax.random.normal(ks[4], (E, F, D), dtype=jnp.float32) * s, 'b2': jax.random.normal(ks[5], (E, D), dtype=jnp.float32) * s}
    _L2_ffn_all = _L2_ffn_setup()
    _L2_ffn_in = {k: v for k, v in _L2_ffn_all.items() if k in ('Wr', 'W1', 'b1', 'W2', 'b2')}
    del _L2_ffn_all

    def _L3_gnn_setup():
        import jax, jax.numpy as jnp
        import numpy as np
        N_NODES = 10000
        N_EDGES = 2500
        D_IN = 512
        D_OUT = 512
        key = jax.random.key(seed)
        k1, k2, k3, k4, k5 = jax.random.split(key, 5)
        feature = jax.random.normal(k1, (N_NODES, D_IN), dtype=jnp.float32)
        src = jax.random.randint(k2, (N_EDGES,), 0, N_NODES, dtype=jnp.int64)
        dst = jax.random.randint(k3, (N_EDGES,), 0, N_NODES, dtype=jnp.int64)
        W = jax.random.normal(k4, (2 * D_IN, D_OUT), dtype=jnp.float32) * (1.0 / np.sqrt(2 * D_IN))
        b = jax.random.normal(k5, (D_OUT,), dtype=jnp.float32) * 0.01
        return {'feature': feature, 'src': src, 'dst': dst, 'W': W, 'b': b}
    _L3_gnn_all = _L3_gnn_setup()
    _L3_gnn_in = {k: v for k, v in _L3_gnn_all.items() if k in ('W', 'b')}
    del _L3_gnn_all

    def _L3_ffn_setup():
        import jax, jax.numpy as jnp
        import numpy as np
        B, S, D, E, O = (1024, 256, 512, 16, 512)
        key = jax.random.key(seed)
        k_x, k_wg, k_bg, k_we, k_be = jax.random.split(key, 5)
        scale_g = 1.0 / np.sqrt(D)
        scale_e = 1.0 / np.sqrt(D)
        return {'x': jax.random.normal(k_x, (B, S, D), dtype=jnp.float32), 'Wg': jax.random.uniform(k_wg, (D, E), jnp.float32, -scale_g, scale_g), 'bg': jax.random.uniform(k_bg, (E,), jnp.float32, -scale_g, scale_g), 'We': jax.random.uniform(k_we, (E, D, O), jnp.float32, -scale_e, scale_e), 'be': jax.random.uniform(k_be, (E, O), jnp.float32, -scale_e, scale_e)}
    _L3_ffn_all = _L3_ffn_setup()
    _L3_ffn_in = {k: v for k, v in _L3_ffn_all.items() if k in ('Wg', 'bg', 'We', 'be')}
    del _L3_ffn_all
    return {'x': x, 'src': src, 'dst': dst, 'edge_attr_20': edge_attr_20, 'edge_attr_3': edge_attr_3, 'edge_type_4': edge_type_4, 'edge_weight': edge_weight, 'L0_gnn_weight': _L0_gnn_in['weight'], 'L0_ffn_Wq': _L0_ffn_in['Wq'], 'L0_ffn_bq': _L0_ffn_in['bq'], 'L0_ffn_keys': _L0_ffn_in['keys'], 'L0_ffn_w_down': _L0_ffn_in['w_down'], 'L0_ffn_w_up': _L0_ffn_in['w_up'], 'L1_gnn_W_self': _L1_gnn_in['W_self'], 'L1_gnn_b_self': _L1_gnn_in['b_self'], 'L1_gnn_W_rel': _L1_gnn_in['W_rel'], 'L1_gnn_b_rel': _L1_gnn_in['b_rel'], 'L1_gnn_ln1_g': _L1_gnn_in['ln1_g'], 'L1_gnn_ln1_b': _L1_gnn_in['ln1_b'], 'L1_gnn_ln2_g': _L1_gnn_in['ln2_g'], 'L1_gnn_ln2_b': _L1_gnn_in['ln2_b'], 'L1_gnn_W_ffn1': _L1_gnn_in['W_ffn1'], 'L1_gnn_b_ffn1': _L1_gnn_in['b_ffn1'], 'L1_gnn_W_ffn2': _L1_gnn_in['W_ffn2'], 'L1_gnn_b_ffn2': _L1_gnn_in['b_ffn2'], 'L1_ffn_gate_w': _L1_ffn_in['gate_w'], 'L1_ffn_w1': _L1_ffn_in['w1'], 'L1_ffn_b1': _L1_ffn_in['b1'], 'L1_ffn_w2': _L1_ffn_in['w2'], 'L1_ffn_b2': _L1_ffn_in['b2'], 'L2_gnn_W_in2f_s': _L2_gnn_in['W_in2f_s'], 'L2_gnn_W_in2f_v': _L2_gnn_in['W_in2f_v'], 'L2_gnn_Wf1': _L2_gnn_in['Wf1'], 'L2_gnn_bf1': _L2_gnn_in['bf1'], 'L2_gnn_Wf2': _L2_gnn_in['Wf2'], 'L2_gnn_bf2': _L2_gnn_in['bf2'], 'L2_gnn_W1_s': _L2_gnn_in['W1_s'], 'L2_gnn_W1_v': _L2_gnn_in['W1_v'], 'L2_gnn_W2_s': _L2_gnn_in['W2_s'], 'L2_gnn_W2_v': _L2_gnn_in['W2_v'], 'L2_ffn_Wr': _L2_ffn_in['Wr'], 'L2_ffn_W1': _L2_ffn_in['W1'], 'L2_ffn_b1': _L2_ffn_in['b1'], 'L2_ffn_W2': _L2_ffn_in['W2'], 'L2_ffn_b2': _L2_ffn_in['b2'], 'L3_gnn_W': _L3_gnn_in['W'], 'L3_gnn_b': _L3_gnn_in['b'], 'L3_ffn_Wg': _L3_ffn_in['Wg'], 'L3_ffn_bg': _L3_ffn_in['bg'], 'L3_ffn_We': _L3_ffn_in['We'], 'L3_ffn_be': _L3_ffn_in['be']}

def reference(x, src, dst, edge_attr_20, edge_attr_3, edge_type_4, edge_weight, L0_gnn_weight, L0_ffn_Wq, L0_ffn_bq, L0_ffn_keys, L0_ffn_w_down, L0_ffn_w_up, L1_gnn_W_self, L1_gnn_b_self, L1_gnn_W_rel, L1_gnn_b_rel, L1_gnn_ln1_g, L1_gnn_ln1_b, L1_gnn_ln2_g, L1_gnn_ln2_b, L1_gnn_W_ffn1, L1_gnn_b_ffn1, L1_gnn_W_ffn2, L1_gnn_b_ffn2, L1_ffn_gate_w, L1_ffn_w1, L1_ffn_b1, L1_ffn_w2, L1_ffn_b2, L2_gnn_W_in2f_s, L2_gnn_W_in2f_v, L2_gnn_Wf1, L2_gnn_bf1, L2_gnn_Wf2, L2_gnn_bf2, L2_gnn_W1_s, L2_gnn_W1_v, L2_gnn_W2_s, L2_gnn_W2_v, L2_ffn_Wr, L2_ffn_W1, L2_ffn_b1, L2_ffn_W2, L2_ffn_b2, L3_gnn_W, L3_gnn_b, L3_ffn_Wg, L3_ffn_bg, L3_ffn_We, L3_ffn_be):
    import jax
    import jax.numpy as jnp

    def _L0_gnn_ref(x, weight, row, col, vals):
        import jax, jax.numpy as jnp
        import numpy as np
        N_NODES = 1024
        N_EDGES = 8192
        FEAT_DIM = 512
        EMBED_DIM = 512
        h = jnp.einsum('nf,ef->ne', x, weight)
        msgs = vals[:, None] * h[col]
        out = jax.ops.segment_sum(msgs, row, num_segments=N_NODES)
        return out

    def _L0_ffn_ref(queries, Wq, bq, keys, w_down, w_up):
        import jax, jax.numpy as jnp
        import numpy as np
        from jax import lax
        N_HEADS = 8
        D_KEYS = 128
        HALF = D_KEYS // 2
        N_KEYS = 256
        TOP_K = 8
        D_MODEL = 512

        def _forward(queries, Wq, bq, keys, w_down, w_up):
            N, T, D = queries.shape
            x = queries.reshape(-1, D)
            q = (x @ Wq + bq).reshape(-1, N_HEADS, D_KEYS)
            q1, q2 = (q[..., :HALF], q[..., HALF:])
            s1 = jnp.einsum('bhc,hnc->bhn', q1, keys[:, 0])
            s2 = jnp.einsum('bhc,hnc->bhn', q2, keys[:, 1])
            s1t, i1 = lax.top_k(s1, TOP_K)
            s2t, i2 = lax.top_k(s2, TOP_K)
            all_scores = (s1t[..., :, None] + s2t[..., None, :]).reshape(-1, N_HEADS, TOP_K * TOP_K)
            all_idx = (i1[..., :, None] * N_KEYS + i2[..., None, :]).reshape(-1, N_HEADS, TOP_K * TOP_K)
            scores, best = lax.top_k(all_scores, TOP_K)
            indices = jnp.take_along_axis(all_idx, best, axis=-1)
            w_d = w_down[indices]
            w_u = w_up[indices]
            inner = jnp.einsum('bd,bhkd->bhk', x, w_d)
            vals = jax.nn.relu(inner) * jax.nn.softmax(scores, axis=-1)
            out = jnp.einsum('bhk,bhkd->bd', vals, w_u)
            return out.reshape(N, T, D)
        return _forward(queries, Wq, bq, keys, w_down, w_up)

    def _L1_gnn_ref(x, edge_index, edge_type, edge_weight, W_self, b_self, W_rel, b_rel, ln1_g, ln1_b, ln2_g, ln2_b, W_ffn1, b_ffn1, W_ffn2, b_ffn2):
        import jax, jax.numpy as jnp
        import numpy as np
        DIM = 512
        NUM_REL = 4
        N_NODES = 50000
        N_EDGES = 2500

        def _layer_norm(x, g, b, eps=1e-05):
            mu = jnp.mean(x, axis=-1, keepdims=True)
            var = jnp.mean((x - mu) ** 2, axis=-1, keepdims=True)
            return (x - mu) * jax.lax.rsqrt(var + eps) * g + b
        n = x.shape[0]
        src, dst = (edge_index[0], edge_index[1])
        xs = x[src]
        total_msg = jnp.zeros_like(xs)
        for r in range(NUM_REL):
            w_r = jnp.where(edge_type == r, edge_weight, 0.0)
            total_msg = total_msg + (xs @ W_rel[r] + b_rel[r]) * w_r[:, None]
        agg = jax.ops.segment_sum(total_msg, dst, num_segments=n)
        deg = jax.ops.segment_sum(edge_weight, dst, num_segments=n)
        agg = agg / jnp.maximum(deg, 1.0)[:, None]
        h = x @ W_self + b_self + agg
        x1 = _layer_norm(x + h, ln1_g, ln1_b)
        ffn = jax.nn.gelu(x1 @ W_ffn1 + b_ffn1, approximate=False) @ W_ffn2 + b_ffn2
        out = _layer_norm(x1 + ffn, ln2_g, ln2_b)
        return out

    def _L1_ffn_ref(x, gate_w, w1, b1, w2, b2):
        import jax, jax.numpy as jnp
        import numpy as np
        import math
        B, T, D = (4, 128, 512)
        E, K, F = (8, 2, 32)
        CAP_FACTOR = 1.25
        Bx, Tx, Dx = x.shape
        N = Bx * Tx
        C = math.ceil(CAP_FACTOR * N / E)
        xf = x.reshape(N, Dx)
        probs = jax.nn.softmax(xf @ gate_w.T, axis=-1)
        topk_vals, topk_idx = jax.lax.top_k(probs, K)
        topk_vals = topk_vals / topk_vals.sum(-1, keepdims=True)
        flat_e = topk_idx.reshape(N * K)
        onehot = jax.nn.one_hot(flat_e, E, dtype=jnp.int32)
        pos = jnp.cumsum(onehot, axis=0)[jnp.arange(N * K), flat_e] - 1
        keep = pos < C
        pos_safe = jnp.where(keep, pos, C)
        token_ids = jnp.repeat(jnp.arange(N), K)
        buf = jnp.zeros((E, C + 1, Dx), x.dtype).at[flat_e, pos_safe].set(xf[token_ids])
        expert_in = buf[:, :C]
        h = jax.nn.gelu(jnp.einsum('ecd,edf->ecf', expert_in, w1) + b1[:, None, :], approximate=False)
        expert_out = jnp.einsum('ecf,efd->ecd', h, w2) + b2[:, None, :]
        gathered = expert_out[flat_e, jnp.minimum(pos_safe, C - 1)]
        w = (topk_vals.reshape(N * K) * keep).astype(x.dtype)
        out = (gathered * w[:, None]).reshape(N, K, Dx).sum(axis=1)
        return out.reshape(Bx, Tx, Dx)

    def _L2_gnn_ref(x, idx_i, idx_j, f_ij, rcut_ij, r_ij, W_in2f_s, W_in2f_v, Wf1, bf1, Wf2, bf2, W1_s, W1_v, W2_s, W2_v):
        import jax, jax.numpy as jnp
        import numpy as np
        N_ATOMS = 5000
        N_EDGES = 50000
        C = 128
        F = 128
        N_RBF = 20
        LOG2 = float(np.log(2.0))
        Y0 = float(1.0 / np.sqrt(4.0 * np.pi))
        Y1_SCALE = float(np.sqrt(3.0 / (4.0 * np.pi)))

        def shifted_softplus(x):
            return jax.nn.softplus(x) - LOG2

        def _forward(x, idx_i, idx_j, f_ij, rcut_ij, r_ij, W_in2f_s, W_in2f_v, Wf1, bf1, Wf2, bf2, W1_s, W1_v, W2_s, W2_v):
            n = x.shape[0]
            e = r_ij.shape[0]
            xs = x[:, :C] @ (W_in2f_s / np.sqrt(C))
            xv = jnp.einsum('nci,cf->nfi', x[:, C:].reshape(n, C, 3), W_in2f_v) / np.sqrt(C)
            sj = xs[idx_j]
            vj = xv[idx_j]
            u = r_ij / jnp.linalg.norm(r_ij, axis=-1, keepdims=True)
            Yv = Y1_SCALE * u
            o0a = sj * Y0
            o0b = jnp.einsum('efi,ei->ef', vj, Yv) / np.sqrt(3.0)
            s2 = jnp.stack([o0a, o0b], axis=-1).reshape(e, 2 * F)
            ova = sj[:, :, None] * Yv[:, None, :]
            ovb = vj * Y0
            v2 = jnp.stack([ova, ovb], axis=2)
            w1 = jnp.cross(vj, Yv[:, None, :]) / np.sqrt(2.0)
            ax, ay, az = (vj[..., 0], vj[..., 1], vj[..., 2])
            bx, by, bz = (Yv[:, None, 0], Yv[:, None, 1], Yv[:, None, 2])
            t = jnp.stack([(ax * by + ay * bx) / np.sqrt(2.0), (ay * bz + az * by) / np.sqrt(2.0), (2.0 * az * bz - ax * bx - ay * by) / np.sqrt(6.0), (az * bx + ax * bz) / np.sqrt(2.0), (ax * bx - ay * by) / np.sqrt(2.0)], axis=-1)
            h = shifted_softplus(f_ij @ Wf1 + bf1)
            W = (h @ Wf2 + bf2) * rcut_ij[:, None]
            m_s = s2 * W[:, :2 * F]
            m_v = (v2.reshape(e, 2 * F, 3) * W[:, 2 * F:4 * F, None]).reshape(e, 6 * F)
            m_w = (w1 * W[:, 4 * F:5 * F, None]).reshape(e, 3 * F)
            m_t = (t * W[:, 5 * F:6 * F, None]).reshape(e, 5 * F)
            x_ij = jnp.concatenate([m_s, m_v, m_w, m_t], axis=1)
            agg = jax.ops.segment_sum(x_ij, idx_i, num_segments=n)
            S = agg[:, :2 * F] @ (W1_s / np.sqrt(2 * F))
            V = jnp.einsum('nmi,mc->nci', agg[:, 2 * F:8 * F].reshape(n, 2 * F, 3), W1_v) / np.sqrt(2 * F)
            S = shifted_softplus(S)
            S = S @ (W2_s / np.sqrt(C))
            V = jnp.einsum('nci,cd->ndi', V, W2_v) / np.sqrt(C)
            return jnp.concatenate([S, V.reshape(n, 3 * C)], axis=1)
        return _forward(x, idx_i, idx_j, f_ij, rcut_ij, r_ij, W_in2f_s, W_in2f_v, Wf1, bf1, Wf2, bf2, W1_s, W1_v, W2_s, W2_v)

    def _L2_ffn_ref(x, Wr, W1, b1, W2, b2):
        import jax, jax.numpy as jnp
        import numpy as np
        B, T, D = (4, 128, 512)
        E, F, CAP = (8, 32, 64)
        Bb, Tt, Dd = x.shape
        N = Bb * Tt
        C = min(CAP, N)
        x_flat = x.reshape(N, Dd)
        logits = x_flat @ Wr
        probs = jax.nn.softmax(logits, axis=0)
        vals, idx = jax.lax.top_k(probs.T, C)
        selected = x_flat[idx]
        h = jax.nn.gelu(jnp.einsum('ecd,edf->ecf', selected, W1) + b1[:, None, :], approximate=False)
        out_e = jnp.einsum('ecf,efd->ecd', h, W2) + b2[:, None, :]
        weighted = vals[..., None] * out_e
        output = jnp.zeros_like(x_flat).at[idx.reshape(-1)].add(weighted.reshape(-1, Dd))
        return output.reshape(Bb, Tt, Dd)

    def _L3_gnn_ref(feature, src, dst, W, b):
        import jax, jax.numpy as jnp
        import numpy as np
        N_NODES = 10000
        N_EDGES = 2500
        D_IN = 512
        D_OUT = 512
        n = feature.shape[0]
        neigh = jax.ops.segment_sum(feature[src], dst, num_segments=n)
        degs = jax.ops.segment_sum(jnp.ones_like(dst, dtype=feature.dtype), dst, num_segments=n)
        hk_neigh = neigh / jnp.maximum(degs, 1.0)[:, None]
        hk = jnp.concatenate([feature, hk_neigh], axis=-1) @ W + b
        return jax.nn.relu(hk)

    def _L3_ffn_ref(x, Wg, bg, We, be):
        import jax, jax.numpy as jnp
        import numpy as np
        B, S, D, E, O = (1024, 256, 512, 16, 512)
        scores = jax.nn.softmax(jnp.mean(x, axis=1) @ Wg + bg, axis=-1)
        idx = jnp.argmax(scores, axis=-1)
        gate = jnp.take_along_axis(scores, idx[:, None], axis=-1)
        W_sel = We[idx]
        b_sel = be[idx]
        y = jnp.einsum('bsd,bdo->bso', x, W_sel) + b_sel[:, None, :]
        return gate[:, :, None] * y
    edge_index = jnp.stack([src, dst])
    x = x + _L0_gnn_ref(_layernorm(x, axis=-1), L0_gnn_weight, src, dst, edge_weight)
    x = x + _L0_ffn_ref(_layernorm(x, axis=-1)[None], L0_ffn_Wq, L0_ffn_bq, L0_ffn_keys, L0_ffn_w_down, L0_ffn_w_up)[0]
    x = x + _L1_gnn_ref(_layernorm(x, axis=-1), edge_index, edge_type_4, edge_weight, L1_gnn_W_self, L1_gnn_b_self, L1_gnn_W_rel, L1_gnn_b_rel, L1_gnn_ln1_g, L1_gnn_ln1_b, L1_gnn_ln2_g, L1_gnn_ln2_b, L1_gnn_W_ffn1, L1_gnn_b_ffn1, L1_gnn_W_ffn2, L1_gnn_b_ffn2)
    x = x + _L1_ffn_ref(_layernorm(x, axis=-1)[None], L1_ffn_gate_w, L1_ffn_w1, L1_ffn_b1, L1_ffn_w2, L1_ffn_b2)[0]
    x = x + _L2_gnn_ref(_layernorm(x, axis=-1), src, dst, edge_attr_20, edge_weight, edge_attr_3, L2_gnn_W_in2f_s, L2_gnn_W_in2f_v, L2_gnn_Wf1, L2_gnn_bf1, L2_gnn_Wf2, L2_gnn_bf2, L2_gnn_W1_s, L2_gnn_W1_v, L2_gnn_W2_s, L2_gnn_W2_v)
    x = x + _L2_ffn_ref(_layernorm(x, axis=-1)[None], L2_ffn_Wr, L2_ffn_W1, L2_ffn_b1, L2_ffn_W2, L2_ffn_b2)[0]
    x = x + _L3_gnn_ref(_layernorm(x, axis=-1), src, dst, L3_gnn_W, L3_gnn_b)
    x = x + _L3_ffn_ref(_layernorm(x, axis=-1)[None], L3_ffn_Wg, L3_ffn_bg, L3_ffn_We, L3_ffn_be)[0]
    return x

_drawn_inputs = setup_inputs


def setup_inputs(seed=0):
    import zlib

    import numpy as np

    out = dict(_drawn_inputs(seed))
    spreads = {'L0_ffn_bq': (0.0, 0.8),
     'L1_gnn_b_self': (0.0, 0.272),
     'L1_gnn_b_rel': (0.0, 0.415),
     'L1_gnn_ln1_g': (1.0, 0.2),
     'L1_gnn_ln1_b': (0.0, 0.1),
     'L1_gnn_ln2_g': (1.0, 0.2),
     'L1_gnn_ln2_b': (0.0, 0.1),
     'L1_gnn_b_ffn1': (0.0, 0.504),
     'L1_gnn_b_ffn2': (0.0, 0.1),
     'L1_ffn_b1': (0.0, 0.8),
     'L1_ffn_b2': (0.0, 0.568)}
    factors = {'L0_ffn_Wq': 8.0,
     'L0_ffn_keys': 7.52,
     'L0_ffn_w_down': 8.0,
     'L0_ffn_w_up': 8.0,
     'L2_gnn_bf1': 5.77,
     'L2_gnn_bf2': 3.231,
     'L2_gnn_W1_s': 3.481,
     'L2_gnn_W2_s': 3.468,
     'L2_ffn_Wr': 8.0,
     'L2_ffn_W1': 26.635,
     'L2_ffn_b1': 200.0,
     'L2_ffn_W2': 22.174,
     'L2_ffn_b2': 200.0,
     'L3_gnn_b': 36.529,
     'L3_ffn_Wg': 5.564,
     'L3_ffn_bg': 8.0,
     'L3_ffn_We': 5.566,
     'L3_ffn_be': 64.0}
    for name, (base, spread) in spreads.items():
        noise = np.random.default_rng([zlib.crc32(name.encode()), seed]).standard_normal(out[name].shape)
        drawn = base * np.exp(spread * noise) if base else spread * noise
        out[name] = jnp.asarray(drawn.astype(out[name].dtype))
    for name, factor in factors.items():
        out[name] = (out[name] * factor).astype(out[name].dtype)
    return out
```

```python
from contextlib import ExitStack
import math

import concourse.bass as bass
from concourse import mybir

F32 = mybir.dt.float32
I32 = mybir.dt.int32
U32 = mybir.dt.uint32
ALU = mybir.AluOpType
ACT = mybir.ActivationFunctionType
AX_X = mybir.AxisListType.X

P = 128
N = 1024
D = 512
NT = N // P
DC = D // P
E = 17408
EP = E // P
CH = EP + NT
SLOTS = CH * P
RS = 32
RD = 4
S_RBF, S_R, S_W, S_LO, S_OTHER = 0, 20, 23, 24, 25
D_W, D_LO, D_OTHER, D_TYPED = 0, 1, 2, 3
RBF = 20
EPS = 1e-5
ROWS = 16
RING = 8
LEAD = 4


class Stage:

    def __init__(self, nc, tag):
        self.nc, self.tag, self.ctx, self.sems = nc, tag, ExitStack(), []

    def __enter__(self):
        return self

    def __exit__(self, *e):
        self.ctx.close()
        if self.sems:
            self.nc.clear_and_free_semaphores(self.sems)
            self.nc.all_engine_barrier(sem_only=True)
        return False

    def sb(self, name, shape, dt=F32):
        return self.ctx.enter_context(self.nc.sbuf_tensor(f"{self.tag}_{name}", shape, dt))

    def ps(self, name, shape=(P, D)):
        return self.ctx.enter_context(self.nc.psum_tensor(f"{self.tag}_{name}", list(shape), F32))

    def sem(self, name):
        self.sems.append(self.nc.alloc_semaphore(f"{self.tag}_{name}"))
        return self.sems[-1]


class Landings:

    def __init__(self, ctx, nc):
        self.sems = [ctx.enter_context(nc.semaphore(f"landed{k}")) for k in range(ROWS)]
        self.counts = [0] * ROWS

    def take(self, transfers):
        pairs = [(self.sems[k], self.counts[k]) for k in range(len(transfers))]
        for k, n in enumerate(transfers):
            self.counts[k] += 16 * n
        return pairs


class Shared:

    def __init__(self, nc, ctx):
        def sb(name, shape, dt=F32):
            return ctx.enter_context(nc.sbuf_tensor(name, shape, dt))

        def dram(name, shape):
            return nc.dram_tensor(name, shape, F32, kind="Internal").ap()

        self.X = sb("X", [P, NT, D])
        self.XL = sb("XL", [P, NT, D])
        self.XLT = None
        self.ident = sb("ident", [P, P])
        self.ones = sb("ones", [P, P])
        self.before = sb("before", [P, P])
        self.spread = sb("spread", [8, 256])
        self.iota = sb("iota", [P, 144])
        self.eps = sb("eps", [P, 1])
        self.rec_s = sb("rec_s", [P, CH, RS])
        self.rec_d = sb("rec_d", [P, CH, RD])
        self.tile_of = sb("tile_of", [P, 2, CH])
        self.tile_row = sb("tile_row", [1, 2, CH], I32)
        self.by_src = dram("by_src", [SLOTS, RS])
        self.by_dst = dram("by_dst", [SLOTS, RD])
        self.rows = dram("rows", [4 * N, D])
        self.landings = Landings(ctx, nc)



def load_nodes(nc, c, x):
    with Stage(nc, "setup") as s:
        loaded, filled, made = s.sem("loaded"), s.sem("filled"), s.sem("made")
        bounded = s.sem("bounded")
        with nc.Block() as block:
            @block.sync
            def _(sp):
                sp.dma_start(c.X[:, :, :], x.rearrange("(t p) d -> p t d", p=P)).then_inc(loaded, 16)
                sp.wait_ge(loaded, 16)

            @block.vector
            def _(dve):
                dve.memset(c.eps[:], EPS)
                dve.memset(c.ones[:], 1.0).then_inc(filled, 1)
                dve.memset(c.ident[:], 0.0).then_inc(filled, 1)
                dve.memset(c.spread[:], 1.0).then_inc(filled, 1)

            @block.gpsimd
            def _(pool):
                pool.iota(c.iota[:], [[1, 144]], base=0, channel_multiplier=0,
                          allow_small_or_imprecise_dtypes=True).then_inc(made, 1)
                pool.wait_ge(filled, 3)
                pool.affine_select(out=c.ident[:], in_=c.ident[:], compare_op=ALU.not_equal, fill=1.0,
                                   base=0, pattern=[[-1, P]], channel_multiplier=1).then_inc(made, 1)
                pool.affine_select(out=c.before[:], in_=c.ones[:], compare_op=ALU.is_gt, fill=0.0,
                                   base=0, pattern=[[1, P]], channel_multiplier=-1).then_inc(made, 1)
                pool.affine_select(out=c.spread[:], in_=c.spread[:], compare_op=ALU.is_ge, fill=0.0,
                                   base=0, pattern=[[1, 256]], channel_multiplier=-32).then_inc(bounded, 1)
                pool.wait_ge(bounded, 1)
                pool.affine_select(out=c.spread[:], in_=c.spread[:], compare_op=ALU.is_ge, fill=0.0,
                                   base=31, pattern=[[-1, 256]], channel_multiplier=32).then_inc(made, 1)



def bin_edges(nc, c, a):
    with Stage(nc, "bin") as s:
        keys = s.sb("keys", [P, 2, EP], I32)
        typ = s.sb("typ", [P, EP], I32)
        tile_i = s.sb("tile_i", [P, 2, EP], I32)
        low_i = s.sb("low_i", [P, 2, EP], I32)
        tile_f = s.sb("tile_f", [P, 2, EP])
        zeros = s.sb("zeros", [P, EP])
        member = s.sb("member", [P, 2, NT, EP])
        rank = s.sb("rank", [P, 2, NT, EP])
        slot_f = s.sb("slot_f", [P, 2, EP])
        slot = s.sb("slot", [P, 2, EP], I32)
        total = s.sb("total", [P, 2 * NT])
        count_f = s.sb("count_f", [P, 2 * NT])
        count_i = s.sb("count_i", [P, 2 * NT], I32)
        chunks = s.sb("chunks", [P, 2, NT])
        ends = s.sb("ends", [P, 2, NT])
        shift = s.sb("shift", [P, 2, NT])
        tmap = s.sb("tmap", [P, 2, CH])
        rec_s = s.sb("rec_s", [P, EP, RS])
        rec_d = s.sb("rec_d", [P, EP, RD])
        pad_s = s.sb("pad_s", [P, CH, RS])
        pad_d = s.sb("pad_d", [P, CH, RD])
        earlier, all_of = s.ps("earlier", [P, 2 * NT]), s.ps("all_of", [P, 2 * NT])
        keys_in, fields_in, padded = s.sem("keys_in"), s.sem("fields_in"), s.sem("padded")
        chain, counted, summed, ready = s.sem("chain"), s.sem("counted"), s.sem("summed"), s.sem("ready")
        reloaded, cleared, scattered_ok = s.sem("reloaded"), s.sem("cleared"), s.sem("scattered_ok")
        (scattered, base), = c.landings.take([2 * EP])
        with nc.Block() as block:
            @block.sync
            def _(sp):
                sp.dma_start(keys[:, 0, :], a["src"].rearrange("(p c) -> p c", p=P)).then_inc(keys_in, 16)
                sp.dma_start(keys[:, 1, :], a["dst"].rearrange("(p c) -> p c", p=P)).then_inc(keys_in, 16)
                sp.dma_start(typ[:], a["edge_type_4"].rearrange("(p c) -> p c", p=P)).then_inc(keys_in, 16)
                sp.dma_start(rec_s[:, :, S_RBF:S_RBF + RBF],
                             a["edge_attr_20"].rearrange("(p c) f -> p c f", p=P)).then_inc(fields_in, 16)
                sp.dma_start(rec_s[:, :, S_R:S_R + 3],
                             a["edge_attr_3"].rearrange("(p c) f -> p c f", p=P)).then_inc(fields_in, 16)
                sp.dma_start(tile_f[:, 0, :], a["edge_weight"].rearrange("(p c) -> p c", p=P)).then_inc(fields_in, 16)
                sp.wait_ge(cleared, 1)
                sp.dma_start(c.by_src.rearrange("(c p) f -> p c f", p=P), pad_s[:]).then_inc(padded, 16)
                sp.dma_start(c.by_dst.rearrange("(c p) f -> p c f", p=P), pad_d[:]).then_inc(padded, 16)
                sp.wait_ge(scattered_ok, 1)
                sp.dma_start(c.rec_s[:], c.by_src.rearrange("(c p) f -> p c f", p=P)).then_inc(reloaded, 16)
                sp.dma_start(c.rec_d[:], c.by_dst.rearrange("(c p) f -> p c f", p=P)).then_inc(reloaded, 16)
                sp.wait_ge(reloaded, 32)

            @block.vector
            def _(dve):
                links = [0]

                def link(ins):
                    links[0] += 1
                    ins.then_inc(chain, 1)
                    dve.wait_ge(chain, links[0])

                dve.memset(zeros[:], 0.0)
                dve.memset(rec_s[:, :, S_OTHER + 1:RS], 0.0)
                dve.memset(pad_d[:], 0.0)
                link(dve.memset(pad_s[:], 0.0))
                dve.memset(pad_s[:, :, S_R:S_R + 3], 1.0)
                dve.memset(pad_s[:, :, S_LO:S_LO + 1], -1.0)
                link(dve.memset(pad_d[:, :, D_LO:D_LO + 1], -1.0))
                dve.sem_inc(cleared, 1)
                dve.wait_ge(fields_in, 48)
                dve.wait_ge(keys_in, 48)
                dve.tensor_copy(rec_s[:, :, S_W], tile_f[:, 0, :])
                dve.tensor_copy(rec_d[:, :, D_W], tile_f[:, 0, :])
                dve.tensor_copy(rec_s[:, :, S_OTHER].bitcast(I32), keys[:, 1, :])
                dve.tensor_copy(rec_d[:, :, D_OTHER].bitcast(I32), keys[:, 0, :])
                dve.tensor_scalar(tile_i[:], keys[:], 7, None, ALU.logical_shift_right)
                link(dve.tensor_scalar(low_i[:], keys[:], P - 1, None, ALU.bitwise_and))
                dve.scalar_tensor_tensor(out=rec_d[:, :, D_TYPED].bitcast(I32), in0=typ[:], scalar=float(N),
                                         in1=keys[:, 0, :], op0=ALU.mult, op1=ALU.add)
                dve.tensor_copy(rec_s[:, :, S_LO], low_i[:, 0, :])
                dve.tensor_copy(rec_d[:, :, D_LO], low_i[:, 1, :])
                link(dve.tensor_copy(tile_f[:], tile_i[:]))
                for b in range(NT):
                    last = dve.tensor_scalar(member[:, :, b, :], tile_f[:], float(b), None, ALU.is_equal)
                link(last)
                for k in range(2):
                    for b in range(NT):
                        last = dve.tensor_tensor_scan(rank[:, k, b, :], zeros[:], member[:, k, b, :], 0.0,
                                                      ALU.add, ALU.add)
                link(last)
                dve.tensor_copy(total[:], rank[:, :, :, EP - 1].rearrange("p k b -> p (k b)")).then_inc(counted, 1)
                dve.wait_ge(summed, 1)
                link(dve.tensor_scalar(count_f[:], all_of[:], float(P - 1), None, ALU.add))
                link(dve.tensor_copy(count_i[:], count_f[:]))
                link(dve.tensor_scalar(count_i[:], count_i[:], 7, None, ALU.logical_shift_right))
                link(dve.tensor_copy(chunks[:].rearrange("p k b -> p (k b)"), count_i[:]))
                for k in range(2):
                    last = dve.tensor_tensor_scan(ends[:, k, :], zeros[:, 0:NT], chunks[:, k, :], 0.0,
                                                  ALU.add, ALU.add)
                link(last)
                link(dve.tensor_tensor(shift[:], ends[:], chunks[:], ALU.subtract))
                link(dve.tensor_scalar(shift[:], shift[:], float(P), -1.0, ALU.mult, ALU.add))
                link(dve.tensor_tensor(shift[:].rearrange("p k b -> p (k b)"),
                                       shift[:].rearrange("p k b -> p (k b)"), earlier[:], ALU.add))
                for k in range(2):
                    for b in range(NT):
                        last = dve.scalar_tensor_tensor(out=rank[:, k, b, :], in0=rank[:, k, b, :],
                                                        scalar=shift[:, k, b:b + 1], in1=member[:, k, b, :],
                                                        op0=ALU.add, op1=ALU.mult)
                link(last)
                for k in range(2):
                    last = dve.tensor_reduce(slot_f[:, k, :], rank[:, k, :, :].rearrange("p b e -> p e b"),
                                             AX_X, ALU.add)
                link(last)
                dve.tensor_copy(slot[:], slot_f[:]).then_inc(ready, 1)
                for b in range(NT):
                    for k in range(2):
                        if b == 0:
                            last = dve.tensor_scalar(tmap[:, k, :], c.iota[:, 0:CH], ends[:, k, b:b + 1], None,
                                                     ALU.is_ge)
                        else:
                            last = dve.scalar_tensor_tensor(out=tmap[:, k, :], in0=c.iota[:, 0:CH],
                                                            scalar=ends[:, k, b:b + 1], in1=tmap[:, k, :],
                                                            op0=ALU.is_ge, op1=ALU.add)
                    link(last)
                link(dve.tensor_scalar(c.tile_of[:], tmap[:], float(NT - 1), None, ALU.min))
                dve.tensor_copy(c.tile_row[:], c.tile_of[0:1, :, :])

            @block.tensor
            def _(pe):
                pe.wait_ge(counted, 1)
                pe.matmul(earlier[:], c.before[:], total[:], start=True, stop=True)
                pe.matmul(all_of[:], c.ones[:], total[:], start=True, stop=True).then_inc(summed, 1)

            @block.gpsimd
            def _(pool):
                pool.wait_ge(ready, 1)
                pool.wait_ge(padded, 32)
                for i in range(EP):
                    pool.indirect_dma_start(c.by_src, bass.IndirectOffsetOnAxis(ap=slot[:, 0, i:i + 1], axis=0),
                                            rec_s[:, i, :], None).then_inc(scattered, 16)
                    pool.indirect_dma_start(c.by_dst, bass.IndirectOffsetOnAxis(ap=slot[:, 1, i:i + 1], axis=0),
                                            rec_d[:, i, :], None).then_inc(scattered, 16)
                pool.wait_ge(scattered, base + 2 * EP * 16)
                pool.sem_inc(scattered_ok, 1)



def norm(nc, c, tag, src, dst, affine=None, turned=None, columns=None, rows=None, residual=False):
    columns = columns or [slice(k * P, (k + 1) * P) for k in range(DC)]
    with Stage(nc, tag) as s:
        stats = s.sb("stats", [P, NT, 6])
        mv = s.sb("mv", [P, NT, 2])
        dev = s.sb("dev", [P, NT])
        rdev = s.sb("rdev", [P, NT])
        gains = s.sb("gains", [P, 2, D]) if affine else None
        turn = [s.ps(f"turn{k}") for k in range(2)]
        stat, moment, rooted, inverted, centred, scaled, shifted, added = (s.sem(n) for n in (
            "stat", "moment", "rooted", "inverted", "centred", "scaled", "shifted", "added"))
        turned_ok, taken, stored, gains_in = s.sem("turned"), s.sem("taken"), s.sem("stored"), s.sem("gains_in")
        final = shifted if affine else centred
        with nc.Block() as block:
            @block.sync
            def _(sp):
                if affine:
                    for k in range(2):
                        sp.dma_start(gains[:, k, :], affine[k].partition_broadcast(P)).then_inc(gains_in, 16)
                if rows is not None:
                    for t in range(NT):
                        sp.wait_ge(final, t + 1)
                        sp.dma_start(rows[t * P:(t + 1) * P, :], dst[:, t, :]).then_inc(stored, 16)
                    sp.wait_ge(stored, 16 * NT)

            @block.vector
            def _(dve):
                for t in range(NT):
                    dve.bn_stats(stats[:, t, :], src[:, t, :]).then_inc(stat, 1)
                for t in range(NT):
                    dve.wait_ge(stat, t + 1)
                    dve.bn_aggr(mv[:, t, :], stats[:, t, :]).then_inc(moment, 1)
                dve.wait_ge(rooted, 1)
                dve.reciprocal(rdev[:], dev[:]).then_inc(inverted, 1)
                dve.wait_ge(inverted, 1)
                for t in range(NT):
                    dve.tensor_scalar(dst[:, t, :], src[:, t, :], mv[:, t, 0:1], rdev[:, t:t + 1],
                                      ALU.subtract, ALU.mult).then_inc(centred, 1)
                if affine:
                    dve.wait_ge(gains_in, 32)
                    for t in range(NT):
                        dve.wait_ge(centred, t + 1)
                        dve.tensor_tensor(dst[:, t, :], dst[:, t, :], gains[:, 0, :], ALU.mult).then_inc(scaled, 1)
                    for t in range(NT):
                        dve.wait_ge(scaled, t + 1)
                        dve.tensor_tensor(dst[:, t, :], dst[:, t, :], gains[:, 1, :], ALU.add).then_inc(shifted, 1)
                if residual:
                    for t in range(NT):
                        dve.wait_ge(final, t + 1)
                        dve.tensor_tensor(c.X[:, t, :], c.X[:, t, :], dst[:, t, :], ALU.add).then_inc(added, 1)

            @block.scalar
            def _(act):
                act.wait_ge(moment, NT)
                act.activation(dev[:], mv[:, :, 1], ACT.Sqrt, bias=c.eps[:]).then_inc(rooted, 1)
                if turned is not None:
                    for t in range(NT):
                        act.wait_ge(turned_ok, t + 1)
                        act.copy(turned[:, :, t * P:(t + 1) * P],
                                 turn[t % 2][:, :].rearrange("p (k n) -> p k n", k=DC)).then_inc(taken, 1)

            @block.tensor
            def _(pe):
                if turned is not None:
                    for t in range(NT):
                        pe.wait_ge(final, t + 1)
                        if t >= 2:
                            pe.wait_ge(taken, t - 1)
                        for k, cols in enumerate(columns):
                            last = pe.transpose(turn[t % 2][:, k * P:(k + 1) * P], dst[:, t, cols], c.ident[:])
                        last.then_inc(turned_ok, 1)



def node_tables(nc, c, tag, weights, biases, table):
    R = weights.shape[0]
    with Stage(nc, tag) as s:
        w = s.sb("w", [P, R, DC, D])
        bias = s.sb("bias", [P, R, D]) if biases is not None else None
        row = [s.sb(f"row{k}", [P, D]) for k in range(4)]
        out = [s.ps(f"out{k}") for k in range(4)]
        w_in, product, biased = s.sem("w_in"), s.sem("product"), s.sem("biased")
        stored = [s.sem(f"stored{k}") for k in range(4)]
        work = [(r, t) for r in range(R) for t in range(NT)]
        with nc.Block() as block:
            @block.sync
            def _(sp):
                for r in range(R):
                    sp.dma_start(w[:, r], weights[r].rearrange("(k p) d -> p k d", p=P)).then_inc(w_in, 16)
                    if biases is not None:
                        sp.dma_start(bias[:, r, :], biases[r].partition_broadcast(P)).then_inc(w_in, 16)
                for i, (r, t) in enumerate(work):
                    sp.wait_ge(biased, i + 1)
                    sp.dma_start(table[(r * NT + t) * P:(r * NT + t + 1) * P, :], row[i % 4][:])\
                        .then_inc(stored[i % 4], 16)
                for k in range(4):
                    sp.wait_ge(stored[k], 16 * (len(work) // 4))

            @block.tensor
            def _(pe):
                pe.wait_ge(w_in, 16 * R * (2 if biases is not None else 1))
                for i, (r, t) in enumerate(work):
                    if i >= 4:
                        pe.wait_ge(biased, i - 3)
                    for k in range(DC):
                        last = pe.matmul(out[i % 4][:], c.XLT[:, k, t * P:(t + 1) * P], w[:, r, k, :],
                                         start=k == 0, stop=k == DC - 1)
                    last.then_inc(product, 1)

            @block.vector
            def _(dve):
                for i, (r, t) in enumerate(work):
                    dve.wait_ge(product, i + 1)
                    if i >= 4:
                        dve.wait_ge(stored[i % 4], 16 * (i // 4))
                    if biases is not None:
                        dve.tensor_tensor(row[i % 4][:], out[i % 4][:], bias[:, r, :], ALU.add).then_inc(biased, 1)
                    else:
                        dve.tensor_copy(row[i % 4][:], out[i % 4][:]).then_inc(biased, 1)



def aggregate(nc, c, tag, order, rec, index, lo, weight, table, total, degree=None, clear=False):
    with Stage(nc, tag) as s:
        at = [s.sb(f"at{h}", [P, LEAD], I32) for h in range(RING // LEAD)]
        rows = [s.sb(f"rows{j}", [P, D]) for j in range(RING)]
        hot = [s.sb(f"hot{j}", [P, P]) for j in range(RING)]
        part = [s.ps(f"part{j}") for j in range(LEAD)]
        deg = s.ps("deg", [P, CH]) if degree is not None else None
        scratch = s.sb("scratch", [P, CH]) if degree is not None else None
        landed = c.landings.take([CH // RING] * RING)
        placed, marked, summed, added = s.sem("placed"), s.sem("marked"), s.sem("summed"), s.sem("added")
        issued, chain = s.sem("issued"), s.sem("chain")
        flat = total[:, :, :].rearrange("p t d -> p (t d)")
        LOOPS = CH // RING
        with nc.Block() as block:
            @block.gpsimd
            def _(pool):
                with pool.Fori(0, LOOPS) as i:
                    for h in range(RING // LEAD):
                        first = i * RING + h * LEAD
                        pool.wait_ge(summed, first + LEAD)
                        pool.tensor_copy(at[h][:], rec[:, bass.ds(first, LEAD), index].bitcast(I32))\
                            .then_inc(placed, 1)
                        pool.wait_ge(placed, i * (RING // LEAD) + h + 1)
                        pool.sem_inc(issued, 1)
                        for j in range(h * LEAD, (h + 1) * LEAD):
                            k = j - h * LEAD
                            pool.indirect_dma_start(rows[j][:], None, table,
                                                    bass.IndirectOffsetOnAxis(ap=at[h][:, k:k + 1], axis=0))\
                                .then_inc(landed[j][0], 16)

            @block.vector
            def _(dve):
                dve.sem_inc(summed, RING)
                if clear:
                    dve.memset(flat, 0.0).then_inc(added, LEAD)
                else:
                    dve.sem_inc(added, LEAD)

                def one_hot(chunk, j):
                    dve.wait_ge(summed, chunk + 1)
                    low = rec[:, bass.ds(chunk, 1), lo:lo + 1].rearrange("p a b -> p (a b)")
                    if weight is None:
                        dve.tensor_scalar(hot[j][:], c.iota[:, 0:P], low, None, ALU.is_equal).then_inc(marked, 1)
                    else:
                        w = rec[:, bass.ds(chunk, 1), weight:weight + 1].rearrange("p a b -> p (a b)")
                        dve.tensor_scalar(hot[j][:], c.iota[:, 0:P], low, w,
                                          ALU.is_equal, ALU.mult).then_inc(marked, 1)

                def add(chunk, j):
                    tile = dve.value_load(c.tile_row[0:1, order, bass.ds(chunk, 1)], min_val=0, max_val=NT - 1)
                    dve.wait_ge(summed, RING + chunk + 1)
                    dve.wait_ge(added, LEAD + chunk)
                    there = flat[:, bass.ds(tile * D, D)]
                    dve.tensor_tensor(there, there, part[j % LEAD][:], ALU.add).then_inc(added, 1)

                for j in range(LEAD):
                    one_hot(j, j)
                with dve.Fori(0, LOOPS - 1) as i:
                    for j in range(RING):
                        one_hot(i * RING + j + LEAD, (j + LEAD) % RING)
                        add(i * RING + j, j)
                for j in range(RING):
                    chunk = (LOOPS - 1) * RING + j
                    if chunk + LEAD < CH:
                        one_hot(chunk + LEAD, (j + LEAD) % RING)
                    add(chunk, j)
                if degree is not None:
                    dve.wait_ge(summed, RING + CH)
                    for t in range(NT):
                        dve.scalar_tensor_tensor(out=scratch[:], in0=c.tile_of[:, order, :], scalar=float(t),
                                                 in1=deg[:], op0=ALU.is_equal, op1=ALU.mult).then_inc(chain, 1)
                        dve.wait_ge(chain, 2 * t + 1)
                        dve.tensor_reduce(degree[:, t:t + 1], scratch[:], AX_X, ALU.add).then_inc(chain, 1)
                        dve.wait_ge(chain, 2 * t + 2)

            @block.tensor
            def _(pe):
                with pe.Fori(0, LOOPS) as i:
                    for j in range(RING):
                        chunk = i * RING + j
                        pe.wait_ge(marked, chunk + 1)
                        pe.wait_ge(added, chunk + 1)
                        if degree is not None:
                            pe.matmul(deg[:, bass.ds(chunk, 1)], hot[j][:], c.ones[:, 0:1], start=True, stop=True)
                        pe.wait_ge(landed[j][0], landed[j][1] + (i + 1) * 16)
                        pe.matmul(part[j % LEAD][:], hot[j][:], rows[j][:], start=True, stop=True)\
                            .then_inc(summed, 1)



def relation_update(nc, c, a, agg, degree, mixed):
    with Stage(nc, "l1u") as s:
        w = s.sb("w", [P, DC, D])
        bias = s.sb("bias", [P, D])
        rdeg = s.sb("rdeg", [P, NT])
        out = [s.ps(f"out{k}") for k in range(4)]
        w_in, product, read, scaled, summed, chain = (s.sem(n) for n in (
            "w_in", "product", "read", "scaled", "summed", "chain"))
        with nc.Block() as block:
            @block.sync
            def _(sp):
                sp.dma_start(w[:], a["L1_gnn_W_self"].rearrange("(k p) d -> p k d", p=P)).then_inc(w_in, 16)
                sp.dma_start(bias[:], a["L1_gnn_b_self"].partition_broadcast(P)).then_inc(w_in, 16)

            @block.tensor
            def _(pe):
                pe.wait_ge(w_in, 32)
                for t in range(NT):
                    if t >= 4:
                        pe.wait_ge(read, t - 3)
                    for k in range(DC):
                        last = pe.matmul(out[t % 4][:], c.XLT[:, k, t * P:(t + 1) * P], w[:, k, :],
                                         start=k == 0, stop=k == DC - 1)
                    last.then_inc(product, 1)

            @block.vector
            def _(dve):
                dve.tensor_scalar(rdeg[:], degree[:], 1.0, None, ALU.max).then_inc(chain, 1)
                dve.wait_ge(chain, 1)
                dve.reciprocal(rdeg[:], rdeg[:]).then_inc(chain, 1)
                dve.wait_ge(chain, 2)
                dve.wait_ge(w_in, 32)
                for t in range(NT):
                    dve.wait_ge(product, t + 1)
                    dve.tensor_tensor(mixed[:, t, :], out[t % 4][:], bias[:], ALU.add).then_inc(read, 1)
                    dve.wait_ge(read, t + 1)
                    dve.scalar_tensor_tensor(out=mixed[:, t, :], in0=agg[:, t, :], scalar=rdeg[:, t:t + 1],
                                             in1=mixed[:, t, :], op0=ALU.mult, op1=ALU.add).then_inc(scaled, 1)
                    dve.wait_ge(scaled, t + 1)
                    dve.tensor_tensor(mixed[:, t, :], mixed[:, t, :], c.XL[:, t, :], ALU.add).then_inc(summed, 1)


def relation_mlp(nc, c, a, x1, x1t, out_sum):
    HC = 2 * D // P
    with Stage(nc, "l1m") as s:
        w1 = s.sb("w1", [P, DC, 2 * D])
        w2 = s.sb("w2", [P, HC, D])
        b1 = s.sb("b1", [P, HC])
        b2 = s.sb("b2", [P, D])
        hid = s.sb("hid", [P, HC, N])
        up = [s.ps(f"up{k}") for k in range(4)]
        down = [s.ps(f"down{k}") for k in range(4)]
        w1_in, w2_in, upped, active, downed, read, summed = (s.sem(n) for n in (
            "w1_in", "w2_in", "upped", "active", "downed", "read", "summed"))
        work = [(h, n) for h in range(HC) for n in range(2)]
        with nc.Block() as block:
            @block.sync
            def _(sp):
                sp.dma_start(w1[:], a["L1_gnn_W_ffn1"].rearrange("(k p) d -> p k d", p=P)).then_inc(w1_in, 16)
                sp.dma_start(b1[:], a["L1_gnn_b_ffn1_t"]).then_inc(w1_in, 16)
                sp.dma_start(w2[:], a["L1_gnn_W_ffn2"].rearrange("(k p) d -> p k d", p=P)).then_inc(w2_in, 16)
                sp.dma_start(b2[:], a["L1_gnn_b_ffn2"].partition_broadcast(P)).then_inc(w2_in, 16)

            @block.tensor
            def _(pe):
                pe.wait_ge(w1_in, 32)
                for i, (h, n) in enumerate(work):
                    if i >= 4:
                        pe.wait_ge(active, i - 3)
                    for k in range(DC):
                        last = pe.matmul(up[i % 4][:], w1[:, k, h * P:(h + 1) * P], x1t[:, k, n * D:(n + 1) * D],
                                         start=k == 0, stop=k == DC - 1)
                    last.then_inc(upped, 1)
                pe.wait_ge(w2_in, 32)
                pe.wait_ge(active, len(work))
                for t in range(NT):
                    if t >= 4:
                        pe.wait_ge(read, t - 3)
                    for h in range(HC):
                        last = pe.matmul(down[t % 4][:], hid[:, h, t * P:(t + 1) * P], w2[:, h, :],
                                         start=h == 0, stop=h == HC - 1)
                    last.then_inc(downed, 1)

            @block.scalar
            def _(act):
                act.wait_ge(w1_in, 32)
                for i, (h, n) in enumerate(work):
                    act.wait_ge(upped, i + 1)
                    act.activation(hid[:, h, n * D:(n + 1) * D], up[i % 4][:], ACT.Gelu,
                                   bias=b1[:, h:h + 1]).then_inc(active, 1)

            @block.vector
            def _(dve):
                dve.wait_ge(w2_in, 32)
                for t in range(NT):
                    dve.wait_ge(downed, t + 1)
                    dve.tensor_tensor(out_sum[:, t, :], down[t % 4][:], b2[:], ALU.add).then_inc(read, 1)
                    dve.wait_ge(read, t + 1)
                    dve.tensor_tensor(out_sum[:, t, :], out_sum[:, t, :], x1[:, t, :], ALU.add).then_inc(summed, 1)


def expert_mix(nc, c, tag, gate_t, w1_d, b1_d, w2_d, b2_d):
    with Stage(nc, tag) as s:
        w1 = s.sb("w1", [P, DC, 256])
        b1 = s.sb("b1", [P, 2])
        w2 = s.sb("w2", [P, 2, D])
        b2 = s.sb("b2", [8, D])
        hid = s.sb("hid", [P, 2, N])
        up = [s.ps(f"up{k}") for k in range(4)]
        wide = [s.ps(f"wide{k}") for k in range(4)]
        w_in, upped, active, gated, downed, added = (s.sem(n) for n in (
            "w_in", "upped", "active", "gated", "downed", "added"))
        work = [(h, n) for h in range(2) for n in range(2)]
        with nc.Block() as block:
            @block.sync
            def _(sp):
                sp.dma_start(w1[:], w1_d.rearrange("(k p) d -> p k d", p=P)).then_inc(w_in, 16)
                sp.dma_start(b1[:], b1_d).then_inc(w_in, 16)
                sp.dma_start(w2[:], w2_d.rearrange("(k p) d -> p k d", p=P)).then_inc(w_in, 16)
                sp.dma_start(b2[:], b2_d).then_inc(w_in, 16)

            @block.tensor
            def _(pe):
                pe.wait_ge(w_in, 64)
                for i, (h, n) in enumerate(work):
                    pe.matmul(wide[i][:], c.spread[:, h * P:(h + 1) * P], gate_t[:, n * D:(n + 1) * D],
                              start=True, stop=True)
                    for k in range(DC):
                        last = pe.matmul(up[i][:], w1[:, k, h * P:(h + 1) * P], c.XLT[:, k, n * D:(n + 1) * D],
                                         start=k == 0, stop=k == DC - 1)
                    last.then_inc(upped, 1)
                pe.wait_ge(gated, 4)
                for t in range(NT):
                    if t >= 4:
                        pe.wait_ge(added, t - 3)
                    for h in range(2):
                        pe.matmul(up[t % 4][:], hid[:, h, t * P:(t + 1) * P], w2[:, h, :], start=h == 0, stop=False)
                    pe.matmul(up[t % 4][:], gate_t[:, t * P:(t + 1) * P], b2[:], start=False, stop=True)\
                        .then_inc(downed, 1)

            @block.scalar
            def _(act):
                act.wait_ge(w_in, 64)
                for i, (h, n) in enumerate(work):
                    act.wait_ge(upped, i + 1)
                    act.activation(hid[:, h, n * D:(n + 1) * D], up[i][:], ACT.Gelu,
                                   bias=b1[:, h:h + 1]).then_inc(active, 1)

            @block.vector
            def _(dve):
                for i, (h, n) in enumerate(work):
                    dve.wait_ge(active, i + 1)
                    part = hid[:, h, n * D:(n + 1) * D]
                    dve.tensor_tensor(part, part, wide[i][:], ALU.mult).then_inc(gated, 1)
                for t in range(NT):
                    dve.wait_ge(downed, t + 1)
                    dve.tensor_tensor(c.X[:, t, :], c.X[:, t, :], up[t % 4][:], ALU.add).then_inc(added, 1)


def capacity_gates(nc, c, a, gate_t):
    NE, CAP = 8, math.ceil(1.25 * N / 8)
    with Stage(nc, "cg") as s:
        w = s.sb("w", [P, DC, NE])
        top = s.sb("top", [P, NT])
        probs = s.sb("probs", [P, NT, NE])
        sums = s.sb("sums", [P, NT])
        best = s.sb("best", [P, NT, NE])
        best_at = s.sb("best_at", [P, NT, NE], U32)
        at = s.sb("at", [P, NT, 2])
        pick = s.sb("pick", [P, 2, NT, NE])
        taken = s.sb("taken", [P, NT, NE])
        place = s.sb("place", [P, NT, NE])
        carry = s.sb("carry", [P, NT, NE])
        gate = s.sb("gate", [P, NT, NE])
        logits, earlier, all_of = (s.ps(n, [P, NT * NE]) for n in ("logits", "earlier", "all_of"))
        turn = [s.ps(f"turn{k}", [NE, D]) for k in range(2)]
        w_in, scored, cut, raised, chosen, counted, gates, turned, chain = (s.sem(n) for n in (
            "w_in", "scored", "cut", "raised", "chosen", "counted", "gates", "turned", "chain"))
        kept = s.sem("kept")

        def flat(t):
            return t[:].rearrange("p t e -> p (t e)")

        def over(t):
            return t.unsqueeze(2).to_broadcast([P, NT, NE])

        with nc.Block() as block:
            @block.sync
            def _(sp):
                sp.dma_start(w[:], a["L1_ffn_gate_w_t"].rearrange("(k p) d -> p k d", p=P)).then_inc(w_in, 16)

            @block.tensor
            def _(pe):
                pe.wait_ge(w_in, 16)
                for t in range(NT):
                    for k in range(DC):
                        last = pe.matmul(logits[:, t * NE:(t + 1) * NE], c.XLT[:, k, t * P:(t + 1) * P], w[:, k, :],
                                         start=k == 0, stop=k == DC - 1)
                last.then_inc(scored, 1)
                pe.wait_ge(chosen, 1)
                pe.matmul(earlier[:], c.before[:], flat(taken), start=True, stop=True)
                pe.matmul(all_of[:], c.ones[:], flat(taken), start=True, stop=True).then_inc(counted, 1)
                pe.wait_ge(gates, 1)
                for t in range(NT):
                    last = pe.transpose(turn[t // 4][:, (t % 4) * P:(t % 4 + 1) * P], gate[:, t, :], c.ident[:])
                last.then_inc(turned, 1)

            @block.scalar
            def _(act):
                act.wait_ge(cut, 1)
                act.activation(probs[:], probs[:], ACT.Exp).then_inc(raised, 1)

            @block.vector
            def _(dve):
                links = [0]

                def link(ins):
                    links[0] += 1
                    ins.then_inc(chain, 1)
                    dve.wait_ge(chain, links[0])

                scores = logits[:].rearrange("p (t e) -> p t e", e=NE)
                dve.wait_ge(scored, 1)
                link(dve.tensor_reduce(top[:], scores, AX_X, ALU.max))
                dve.tensor_tensor(probs[:], scores, over(top[:]), ALU.subtract).then_inc(cut, 1)
                dve.wait_ge(raised, 1)
                link(dve.tensor_reduce(sums[:], probs[:], AX_X, ALU.add))
                link(dve.reciprocal(sums[:], sums[:]))
                link(dve.tensor_tensor(probs[:], probs[:], over(sums[:]), ALU.mult))
                for t in range(NT):
                    last = dve.max(best[:, t, :], probs[:, t, :])
                link(last)
                for t in range(NT):
                    last = dve.max_index(best_at[:, t, :], best[:, t, :], probs[:, t, :])
                link(last)
                link(dve.tensor_copy(at[:], best_at[:, :, 0:2]))
                for k in range(2):
                    last = dve.tensor_tensor(pick[:, k], c.iota[:, 0:NE].unsqueeze(1).to_broadcast([P, NT, NE]),
                                             over(at[:, :, k]), ALU.is_equal)
                link(last)
                dve.tensor_tensor(taken[:], pick[:, 0], pick[:, 1], ALU.add).then_inc(chosen, 1)
                link(dve.tensor_tensor(sums[:], best[:, :, 0], best[:, :, 1], ALU.add))
                link(dve.reciprocal(sums[:], sums[:]))
                dve.wait_ge(chosen, 1)
                link(dve.tensor_tensor(gate[:], taken[:], probs[:], ALU.mult))
                link(dve.tensor_tensor(gate[:], gate[:], over(sums[:]), ALU.mult))
                link(dve.memset(carry[:, 0, :], 0.0))
                dve.wait_ge(counted, 1)
                totals = all_of[:].rearrange("p (t e) -> p t e", e=NE)
                for t in range(1, NT):
                    link(dve.tensor_tensor(carry[:, t, :], carry[:, t - 1, :], totals[:, t - 1, :], ALU.add))
                link(dve.tensor_tensor(flat(place), flat(carry), earlier[:], ALU.add))
                dve.scalar_tensor_tensor(out=flat(gate), in0=flat(place), scalar=float(CAP), in1=flat(gate),
                                         op0=ALU.is_lt, op1=ALU.mult).then_inc(gates, 1)
                dve.wait_ge(turned, 1)
                for k in range(2):
                    dve.tensor_copy(gate_t[:, k * D:(k + 1) * D], turn[k][:]).then_inc(kept, 1)


def choice_gates(nc, c, a, gate_t):
    NE, CAP = 8, 64
    with Stage(nc, "eg") as s:
        w = s.sb("w", [P, DC, NE])
        top = s.sb("top", [NE, 1])
        sums = s.sb("sums", [NE, 1])
        probs = s.sb("probs", [NE, N])
        left = s.sb("left", [NE, N])
        best = s.sb("best", [NE, CAP])
        logits = s.ps("logits", [NE, N])
        w_in, scored, cut, raised, chain = (s.sem(n) for n in ("w_in", "scored", "cut", "raised", "chain"))
        with nc.Block() as block:
            @block.sync
            def _(sp):
                sp.dma_start(w[:], a["L2_ffn_Wr"].rearrange("(k p) d -> p k d", p=P)).then_inc(w_in, 16)

            @block.tensor
            def _(pe):
                pe.wait_ge(w_in, 16)
                for n in range(2):
                    for k in range(DC):
                        last = pe.matmul(logits[:, n * D:(n + 1) * D], w[:, k, :], c.XLT[:, k, n * D:(n + 1) * D],
                                         start=k == 0, stop=k == DC - 1)
                last.then_inc(scored, 1)

            @block.scalar
            def _(act):
                act.wait_ge(cut, 1)
                act.activation(probs[:], logits[:], ACT.Exp, bias=top[:]).then_inc(raised, 1)

            @block.vector
            def _(dve):
                links = [0]

                def link(ins):
                    links[0] += 1
                    ins.then_inc(chain, 1)
                    dve.wait_ge(chain, links[0])

                dve.wait_ge(scored, 1)
                link(dve.tensor_reduce(top[:], logits[:], AX_X, ALU.max))
                dve.tensor_scalar(top[:], top[:], -1.0, None, ALU.mult).then_inc(cut, 1)
                dve.wait_ge(raised, 1)
                link(dve.tensor_reduce(sums[:], probs[:], AX_X, ALU.add))
                link(dve.reciprocal(sums[:], sums[:]))
                link(dve.tensor_scalar(probs[:], probs[:], sums[:], None, ALU.mult))
                for k in range(CAP // 8):
                    now = probs if k == 0 else left
                    link(dve.max(best[:, 8 * k:8 * k + 8], now[:]))
                    link(dve.match_replace(left[:], best[:, 8 * k:8 * k + 8], now[:], -1.0))
                link(dve.scalar_tensor_tensor(out=gate_t[:], in0=left[:], scalar=0.0, in1=probs[:],
                                              op0=ALU.is_lt, op1=ALU.mult))


def sage_update(nc, c, a, agg, degree):
    with Stage(nc, "l3u") as s:
        w = s.sb("w", [P, 2 * DC, D])
        bias = s.sb("bias", [P, D])
        rdeg = s.sb("rdeg", [P, NT])
        agg_t = s.sb("agg_t", [P, DC, N])
        turn = [s.ps(f"turn{k}") for k in range(2)]
        out = [s.ps(f"out{k}") for k in range(4)]
        w_in, mean, turned, taken, product, biased, clipped, chain = (s.sem(n) for n in (
            "w_in", "mean", "turned", "taken", "product", "biased", "clipped", "chain"))
        with nc.Block() as block:
            @block.sync
            def _(sp):
                sp.dma_start(w[:], a["L3_gnn_W"].rearrange("(k p) d -> p k d", p=P)).then_inc(w_in, 16)
                sp.dma_start(bias[:], a["L3_gnn_b"].partition_broadcast(P)).then_inc(w_in, 16)

            @block.tensor
            def _(pe):
                for t in range(NT):
                    pe.wait_ge(mean, t + 1)
                    if t >= 2:
                        pe.wait_ge(taken, t - 1)
                    for k in range(DC):
                        last = pe.transpose(turn[t % 2][:, k * P:(k + 1) * P], agg[:, t, k * P:(k + 1) * P], c.ident[:])
                    last.then_inc(turned, 1)
                pe.wait_ge(w_in, 32)
                for t in range(NT):
                    pe.wait_ge(taken, t + 1)
                    if t >= 4:
                        pe.wait_ge(biased, t - 3)
                    for k in range(2 * DC):
                        left = c.XLT if k < DC else agg_t
                        last = pe.matmul(out[t % 4][:], left[:, k % DC, t * P:(t + 1) * P], w[:, k, :],
                                         start=k == 0, stop=k == 2 * DC - 1)
                    last.then_inc(product, 1)

            @block.scalar
            def _(act):
                for t in range(NT):
                    act.wait_ge(turned, t + 1)
                    act.copy(agg_t[:, :, t * P:(t + 1) * P],
                             turn[t % 2][:, :].rearrange("p (k n) -> p k n", k=DC)).then_inc(taken, 1)

            @block.vector
            def _(dve):
                dve.tensor_scalar(rdeg[:], degree[:], 1.0, None, ALU.max).then_inc(chain, 1)
                dve.wait_ge(chain, 1)
                dve.reciprocal(rdeg[:], rdeg[:]).then_inc(chain, 1)
                dve.wait_ge(chain, 2)
                for t in range(NT):
                    dve.tensor_scalar(agg[:, t, :], agg[:, t, :], rdeg[:, t:t + 1], None, ALU.mult).then_inc(mean, 1)
                dve.wait_ge(w_in, 32)
                for t in range(NT):
                    dve.wait_ge(product, t + 1)
                    dve.wait_ge(turned, t + 1)
                    dve.tensor_tensor(agg[:, t, :], out[t % 4][:], bias[:], ALU.add).then_inc(biased, 1)
                    dve.wait_ge(biased, t + 1)
                    dve.scalar_tensor_tensor(out=c.X[:, t, :], in0=agg[:, t, :], scalar=0.0, in1=c.X[:, t, :],
                                             op0=ALU.max, op1=ALU.add).then_inc(clipped, 1)


def one_expert(nc, c, a):
    NE = 16
    with Stage(nc, "l3e") as s:
        wg = s.sb("wg", [P, DC, NE])
        bg = s.sb("bg", [P, NE])
        mean = s.sb("mean", [P, DC])
        mean_w = s.sb("mean_w", [P, DC, P])
        scores = s.sb("scores", [P, NE])
        top = s.sb("top", [P, 8])
        top_at = s.sb("top_at", [P, 8], U32)
        low = s.sb("low", [P, 1])
        raised_s = s.sb("raised_s", [P, NE])
        sums = s.sb("sums", [P, 1])
        gate = s.sb("gate", [P, 1])
        which = s.sb("which", [P, 1])
        line = s.sb("line", [P, DC])
        row_f = s.sb("row_f", [P, DC])
        row_i = s.sb("row_i", [P, DC], I32)
        which_i = s.sb("which_i", [P, 1], I32)
        w = s.sb("w", [P, DC, D])
        bias = s.sb("bias", [P, D])
        logits = s.ps("logits", [P, NE])
        out = [s.ps(f"out{k}") for k in range(4)]
        (w_in, base), = c.landings.take([DC + 1])
        g_in, spread, scored, cut, raised, picked, lined, product, biased, added, chain = (s.sem(n) for n in (
            "g_in", "spread", "scored", "cut", "raised", "picked", "lined", "product", "biased", "added",
            "chain"))
        with nc.Block() as block:
            @block.sync
            def _(sp):
                sp.dma_start(wg[:], a["L3_ffn_Wg"].rearrange("(k p) d -> p k d", p=P)).then_inc(g_in, 16)
                sp.dma_start(bg[:], a["L3_ffn_bg"].partition_broadcast(P)).then_inc(g_in, 16)

            @block.gpsimd
            def _(pool):
                pool.iota(line[:], [[P, DC]], base=0, channel_multiplier=1,
                          allow_small_or_imprecise_dtypes=True).then_inc(lined, 1)
                pool.wait_ge(picked, 1)
                for k in range(DC):
                    pool.indirect_dma_start(w[:, k, :], None, a["L3_ffn_We_rows"],
                                            bass.IndirectOffsetOnAxis(ap=row_i[:, k:k + 1], axis=0)).then_inc(w_in, 16)
                pool.indirect_dma_start(bias[:], None, a["L3_ffn_be"],
                                        bass.IndirectOffsetOnAxis(ap=which_i[:], axis=0)).then_inc(w_in, 16)

            @block.tensor
            def _(pe):
                pe.wait_ge(g_in, 32)
                pe.wait_ge(spread, 1)
                for k in range(DC):
                    last = pe.matmul(logits[:], mean_w[:, k, :], wg[:, k, :], start=k == 0, stop=k == DC - 1)
                last.then_inc(scored, 1)
                pe.wait_ge(w_in, base + 16 * (DC + 1))
                for t in range(NT):
                    if t >= 4:
                        pe.wait_ge(biased, t - 3)
                    for k in range(DC):
                        last = pe.matmul(out[t % 4][:], c.XLT[:, k, t * P:(t + 1) * P], w[:, k, :],
                                         start=k == 0, stop=k == DC - 1)
                    last.then_inc(product, 1)

            @block.scalar
            def _(act):
                act.wait_ge(cut, 1)
                act.activation(raised_s[:], scores[:], ACT.Exp, bias=low[:]).then_inc(raised, 1)

            @block.vector
            def _(dve):
                links = [0]

                def link(ins):
                    links[0] += 1
                    ins.then_inc(chain, 1)
                    dve.wait_ge(chain, links[0])

                link(dve.tensor_reduce(mean[:], c.XLT[:], AX_X, ALU.add))
                link(dve.tensor_scalar(mean[:], mean[:], 1.0 / N, None, ALU.mult))
                dve.tensor_copy(mean_w[:], mean[:].unsqueeze(2).to_broadcast([P, DC, P])).then_inc(spread, 1)
                dve.wait_ge(scored, 1)
                link(dve.tensor_tensor(scores[:], logits[:], bg[:], ALU.add))
                link(dve.max(top[:], scores[:]))
                dve.tensor_scalar(low[:], top[:, 0:1], -1.0, None, ALU.mult).then_inc(cut, 1)
                link(dve.max_index(top_at[:], top[:], scores[:]))
                link(dve.tensor_copy(which[:], top_at[:, 0:1]))
                dve.wait_ge(lined, 1)
                dve.tensor_copy(which_i[:], which[:])
                link(dve.tensor_scalar(which[:], which[:], float(D), None, ALU.mult))
                link(dve.tensor_scalar(row_f[:], line[:], which[:], None, ALU.add))
                dve.tensor_copy(row_i[:], row_f[:]).then_inc(picked, 1)
                dve.wait_ge(raised, 1)
                link(dve.tensor_reduce(sums[:], raised_s[:], AX_X, ALU.add))
                link(dve.reciprocal(gate[:], sums[:]))
                dve.wait_ge(w_in, base + 16 * (DC + 1))
                for t in range(NT):
                    dve.wait_ge(product, t + 1)
                    dve.tensor_tensor(c.XL[:, t, :], out[t % 4][:], bias[:], ALU.add).then_inc(biased, 1)
                    dve.wait_ge(biased, t + 1)
                    dve.scalar_tensor_tensor(out=c.X[:, t, :], in0=c.XL[:, t, :], scalar=gate[:], in1=c.X[:, t, :],
                                             op0=ALU.mult, op1=ALU.add).then_inc(added, 1)



HEADS, NKEYS, TOPK = 8, 256, 8
BANKS = 4


def memory_queries(nc, c, a, q):
    with Stage(nc, "m0q") as s:
        w = s.sb("w", [P, DC, HEADS * P])
        bias = s.sb("bias", [P, HEADS])
        out = [s.ps(f"out{k}") for k in range(4)]
        w_in, product, biased = s.sem("w_in"), s.sem("product"), s.sem("biased")
        work = [(h, n) for h in range(HEADS) for n in range(2)]
        with nc.Block() as block:
            @block.sync
            def _(sp):
                sp.dma_start(w[:], a["L0_ffn_Wq"].rearrange("(k p) d -> p k d", p=P)).then_inc(w_in, 16)
                sp.dma_start(bias[:], a["L0_ffn_bq_t"]).then_inc(w_in, 16)

            @block.tensor
            def _(pe):
                pe.wait_ge(w_in, 32)
                for i, (h, n) in enumerate(work):
                    if i >= 4:
                        pe.wait_ge(biased, i - 3)
                    for k in range(DC):
                        last = pe.matmul(out[i % 4][:], w[:, k, h * P:(h + 1) * P], c.XLT[:, k, n * D:(n + 1) * D],
                                         start=k == 0, stop=k == DC - 1)
                    last.then_inc(product, 1)

            @block.scalar
            def _(act):
                act.wait_ge(w_in, 32)
                for i, (h, n) in enumerate(work):
                    act.wait_ge(product, i + 1)
                    act.activation(q[:, h, n * D:(n + 1) * D], out[i % 4][:], ACT.Identity,
                                   bias=bias[:, h:h + 1]).then_inc(biased, 1)


def memory_lookup(nc, c, a, q):
    with Stage(nc, "m0") as s:
        keys = s.sb("keys", [P, HEADS, NKEYS])
        query = [s.sb(f"query{k}", [P, P]) for k in range(BANKS)]
        vals = s.sb("best", [P, HEADS, 2, TOPK])
        vals_at = s.sb("best_at", [P, HEADS, 2, TOPK], U32)
        key_no = s.sb("key_no", [P, HEADS, 2, TOPK])
        pairs = s.sb("pairs", [P, HEADS, TOPK, TOPK])
        score = s.sb("score", [P, HEADS, TOPK])
        pair_at = s.sb("pair_at", [P, HEADS, TOPK], U32)
        half_at = s.sb("half_at", [P, 2, HEADS * TOPK], U32)
        half_no = s.sb("half_no", [P, 2, HEADS * TOPK])
        same = s.sb("same", [P, 2, HEADS * TOPK, TOPK])
        chosen = s.sb("chosen", [P, 2, HEADS * TOPK])
        memory = [s.sb(f"memory{u}", [P, HEADS * TOPK], I32) for u in range(2)]
        share = [s.sb(f"share{u}", [P, HEADS, TOPK]) for u in range(2)]
        norms = s.sb("norms", [P, HEADS])
        rows = [s.sb(f"rows{k}", [P, 2 * D]) for k in range(ROWS)]
        inner = [s.sb(f"inner{k}", [P, TOPK]) for k in range(2)]
        value = [s.sb(f"value{k}", [P, TOPK]) for k in range(2)]
        diag = [s.sb(f"diag{k}", [P, P]) for k in range(ROWS)]
        scores = [s.ps(f"scores{k}") for k in range(BANKS)]
        out = [s.ps(f"out{u}") for u in range(2)]
        keys_in, queried, scored, maxed, ranked = (s.sem(n) for n in ("keys_in", "queried", "scored", "maxed", "ranked"))
        steps, indexed, issued, shifted, raised = (s.sem(n) for n in ("steps", "indexed", "issued", "shifted", "raised"))
        dotted, valued, spread, used, added = (s.sem(n) for n in ("dotted", "valued", "spread", "used", "added"))
        waited = s.sem("waited")
        landed = c.landings.take([NT * HEADS * TOPK // ROWS] * ROWS)
        STEPS = 15
        PAIRS = HEADS // 2

        def bank(h, k):
            return scores[h % BANKS // 2 * 2 + k][:, h % 2 * NKEYS:(h % 2 + 1) * NKEYS]

        def over_tiles(engine, tile, before=None):
            with engine.Fori(0, NT // 2 - 1) as i:
                for u in range(2):
                    tile(i * 2 + u, u, True)
            tile(NT - 2, 0, True)
            tile(NT - 1, 1, False)

        with nc.Block() as block:
            @block.sync
            def _(sp):
                sp.dma_start(keys[:], a["L0_ffn_keys_t"]).then_inc(keys_in, 16)

            @block.scalar
            def _(act):
                def place_queries(T, p):
                    act.wait_ge(scored, T * PAIRS + p + 1)
                    for h in (2 * p, 2 * p + 1):
                        act.copy(query[h % BANKS][:], q[:, h, bass.ds(T * P, P)]).then_inc(queried, 1)

                def raise_scores(T):
                    act.wait_ge(shifted, T + 1)
                    act.activation(score[:], score[:], ACT.Exp).then_inc(raised, 1)

                def spread_values(T, h):
                    act.wait_ge(valued, T * HEADS + h + 1)
                    act.wait_ge(used, (T * HEADS + h) * TOPK + TOPK)
                    for k in range(TOPK):
                        act.mul(diag[h % 2 * TOPK + k][:], c.ident[:], value[h % 2][:, k:k + 1]).then_inc(spread, 1)

                def tile(T, u, more):
                    for h in range(HEADS):
                        if more and h < PAIRS:
                            place_queries(T + 1, h)
                        spread_values(T, h)
                        if more and h == HEADS // 2:
                            raise_scores(T + 1)

                for p in range(PAIRS):
                    place_queries(0, p)
                raise_scores(0)
                over_tiles(act, tile)

            @block.tensor
            def _(pe):
                def score_pair(T, p):
                    pe.wait_ge(queried, (T * PAIRS + p + 1) * 2)
                    pe.wait_ge(ranked, T * PAIRS + p + 1)
                    for h in (2 * p, 2 * p + 1):
                        for k in range(2):
                            half = slice(k * 64, (k + 1) * 64)
                            last = pe.matmul(bank(h, k), query[h % BANKS][half, :],
                                             keys[half, h, :], start=True, stop=True)
                    last.then_inc(scored, 1)

                def sum_up(T, u, h):
                    if h == 0:
                        pe.wait_ge(added, T + 1)
                    for k in range(TOPK):
                        pe.wait_ge(spread, ROWS + (T * HEADS + h) * TOPK + k + 1)
                        slot = h % 2 * TOPK + k
                        pe.matmul(out[u][:], diag[slot][:], rows[slot][:, D:2 * D],
                                  start=h == 0 and k == 0, stop=h == HEADS - 1 and k == TOPK - 1).then_inc(used, 1)

                def tile(T, u, more):
                    for h in range(HEADS):
                        if more and h < PAIRS:
                            score_pair(T + 1, h)
                        sum_up(T, u, h)

                pe.wait_ge(keys_in, 16)
                for p in range(PAIRS):
                    score_pair(0, p)
                over_tiles(pe, tile)

            @block.gpsimd
            def _(pool):
                def tile(T, u, more):
                    pool.wait_ge(indexed, T + 1)
                    pool.sem_inc(issued, 1)
                    for h in range(HEADS):
                        for half in range(2):
                            first = half * TOPK // 2
                            pool.wait_ge(used, (T * HEADS + h) * TOPK + first + TOPK // 2)
                            pool.sem_inc(issued, 1)
                            for k in range(first, first + TOPK // 2):
                                slot = h % 2 * TOPK + k
                                pool.indirect_dma_start(
                                    rows[slot][:], None, a["L0_ffn_w_rows"],
                                    bass.IndirectOffsetOnAxis(ap=memory[u][:, h * TOPK + k:h * TOPK + k + 1], axis=0))\
                                    .then_inc(landed[slot][0], 16)

                over_tiles(pool, tile)

            @block.vector
            def _(dve):
                dve.sem_inc(scored, 2)
                dve.sem_inc(ranked, 2)
                dve.sem_inc(spread, ROWS)
                dve.sem_inc(used, ROWS)
                dve.sem_inc(added, 2)

                def rank(T, p):
                    heads = [(h, k) for h in (2 * p, 2 * p + 1) for k in range(2)]
                    dve.wait_ge(scored, 2 + T * PAIRS + p + 1)
                    dve.sem_inc(waited, 1)
                    for h, k in heads:
                        last = dve.max(vals[:, h, k, :], bank(h, k))
                    last.then_inc(maxed, 1)
                    dve.wait_ge(maxed, T * PAIRS + p + 1)
                    dve.sem_inc(waited, 1)
                    for h, k in heads:
                        last = dve.max_index(vals_at[:, h, k, :], vals[:, h, k, :], bank(h, k))
                    last.then_inc(ranked, 1)

                def choose(T, u):
                    done = [0]

                    def link(ins):
                        done[0] += 1
                        ins.then_inc(steps, 1)
                        dve.wait_ge(steps, T * STEPS + done[0])

                    full = [P, HEADS, TOPK, TOPK]
                    dve.wait_ge(ranked, 2 + (T + 1) * PAIRS)
                    dve.tensor_copy(key_no[:], vals_at[:])
                    link(dve.tensor_tensor(pairs[:], vals[:, :, 0, :].unsqueeze(3).to_broadcast(full),
                                           vals[:, :, 1, :].unsqueeze(2).to_broadcast(full), ALU.add))
                    dve.sem_inc(waited, 1)
                    for h in range(HEADS):
                        last = dve.max(score[:, h, :], pairs[:, h].rearrange("p a b -> p (a b)"))
                    link(last)
                    dve.sem_inc(waited, 1)
                    for h in range(HEADS):
                        last = dve.max_index(pair_at[:, h, :], score[:, h, :], pairs[:, h].rearrange("p a b -> p (a b)"))
                    link(last)
                    at = pair_at[:].rearrange("p h k -> p (h k)")
                    dve.tensor_scalar(half_at[:, 0, :], at, 3, None, ALU.logical_shift_right)
                    link(dve.tensor_scalar(half_at[:, 1, :], at, TOPK - 1, None, ALU.bitwise_and))
                    link(dve.tensor_copy(norms[:], score[:, :, 0]))
                    dve.tensor_tensor(score[:], score[:], norms[:].unsqueeze(2).to_broadcast([P, HEADS, TOPK]),
                                      ALU.subtract).then_inc(shifted, 1)
                    link(dve.tensor_copy(half_no[:], half_at[:]))
                    wide = [P, 2 * HEADS * TOPK, TOPK]
                    link(dve.tensor_tensor(same[:].rearrange("p a n m -> p (a n) m"),
                                           c.iota[:, 0:TOPK].unsqueeze(1).to_broadcast(wide),
                                           half_no[:].rearrange("p a n -> p (a n)").unsqueeze(2).to_broadcast(wide),
                                           ALU.is_equal))
                    for k in range(2):
                        part = same[:, k].rearrange("p (h n) m -> p h n m", h=HEADS)
                        last = dve.tensor_tensor(part, part, key_no[:, :, k, :].unsqueeze(2).to_broadcast(full), ALU.mult)
                    link(last)
                    link(dve.tensor_reduce(chosen[:], same[:], AX_X, ALU.add))
                    dve.scalar_tensor_tensor(out=memory[u][:], in0=chosen[:, 0, :], scalar=float(NKEYS),
                                             in1=chosen[:, 1, :], op0=ALU.mult, op1=ALU.add).then_inc(indexed, 1)
                    for _ in range(STEPS - 4 - done[0]):
                        dve.sem_inc(steps, 1)
                        done[0] += 1

                def softmax(T, u):
                    def link(n, ins):
                        ins.then_inc(steps, 1)
                        dve.wait_ge(steps, T * STEPS + n)

                    dve.wait_ge(raised, T + 1)
                    link(STEPS - 3, dve.tensor_reduce(norms[:], score[:], AX_X, ALU.add))
                    link(STEPS - 2, dve.reciprocal(norms[:], norms[:]))
                    link(STEPS - 1, dve.tensor_tensor(share[u][:], score[:],
                                                      norms[:].unsqueeze(2).to_broadcast([P, HEADS, TOPK]), ALU.mult))
                    dve.sem_inc(steps, 1)

                def weigh(T, u, h):
                    for k in range(TOPK):
                        slot = h % 2 * TOPK + k
                        dve.wait_ge(landed[slot][0], landed[slot][1] + (T * (HEADS // 2) + h // 2 + 1) * 16)
                        last = dve.scalar_tensor_tensor(out=rows[slot][:, 0:D], in0=c.XL[:, bass.ds(T, 1), :]
                                                        .rearrange("p a d -> p (a d)"), scalar=1.0,
                                                        in1=rows[slot][:, 0:D], op0=ALU.mult, op1=ALU.mult,
                                                        accum_out=inner[h % 2][:, k:k + 1])
                    last.then_inc(dotted, 1)
                    dve.wait_ge(dotted, T * HEADS + h + 1)
                    dve.wait_ge(spread, (T * HEADS + h) * TOPK + TOPK - 7)
                    dve.scalar_tensor_tensor(out=value[h % 2][:], in0=inner[h % 2][:], scalar=0.0,
                                             in1=share[u][:, h, :], op0=ALU.max, op1=ALU.mult).then_inc(valued, 1)

                def add(T, u):
                    dve.wait_ge(used, ROWS + (T + 1) * HEADS * TOPK)
                    there = c.X[:, bass.ds(T, 1), :].rearrange("p a d -> p (a d)")
                    dve.tensor_tensor(there, there, out[u][:], ALU.add).then_inc(added, 1)

                def tile(T, u, more):
                    for h in range(HEADS):
                        if more and h < PAIRS:
                            rank(T + 1, h)
                        if more and h == HEADS // 2:
                            choose(T + 1, 1 - u)
                        weigh(T, u, h)
                        if more and h == HEADS // 2:
                            softmax(T + 1, 1 - u)
                    add(T, u)

                for p in range(PAIRS):
                    rank(0, p)
                choose(0, 0)
                softmax(0, 0)
                over_tiles(dve, tile)



LOG2 = math.log(2.0)
Y0 = 1.0 / math.sqrt(4.0 * math.pi)
Y1 = math.sqrt(3.0 / (4.0 * math.pi))
QUAD = 4


def vector_node_rows(nc, c, a):
    with Stage(nc, "t0") as s:
        w = s.sb("w", [P, 2, P])
        row = [s.sb(f"row{k}", [P, D]) for k in range(4)]
        out = [s.ps(f"out{k}") for k in range(4)]
        w_in, product, scaled = s.sem("w_in"), s.sem("product"), s.sem("scaled")
        stored = [s.sem(f"stored{k}") for k in range(4)]
        with nc.Block() as block:
            @block.sync
            def _(sp):
                sp.dma_start(w[:, 0, :], a["L2_gnn_W_in2f_s"]).then_inc(w_in, 16)
                sp.dma_start(w[:, 1, :], a["L2_gnn_W_in2f_v"]).then_inc(w_in, 16)
                for t in range(NT):
                    sp.wait_ge(scaled, t + 1)
                    sp.dma_start(c.rows[t * P:(t + 1) * P, :], row[t % 4][:]).then_inc(stored[t % 4], 16)
                for k in range(4):
                    sp.wait_ge(stored[k], 16 * (NT // 4))

            @block.tensor
            def _(pe):
                pe.wait_ge(w_in, 32)
                for t in range(NT):
                    if t >= 4:
                        pe.wait_ge(scaled, t - 3)
                    for k in range(DC):
                        last = pe.matmul(out[t % 4][:, k * P:(k + 1) * P], c.XLT[:, k, t * P:(t + 1) * P],
                                         w[:, min(k, 1), :], start=True, stop=True)
                    last.then_inc(product, 1)

            @block.scalar
            def _(act):
                for t in range(NT):
                    act.wait_ge(product, t + 1)
                    if t >= 4:
                        act.wait_ge(stored[t % 4], 16 * (t // 4))
                    act.mul(row[t % 4][:], out[t % 4][:], 1.0 / math.sqrt(P)).then_inc(scaled, 1)


def directions(nc, c, unit):
    with Stage(nc, "t1") as s:
        square = s.sb("square", [P, CH, 3])
        length = s.sb("length", [P, CH])
        squared, rooted, chain, done = s.sem("squared"), s.sem("rooted"), s.sem("chain"), s.sem("done")
        r = c.rec_s[:, :, S_R:S_R + 3]
        with nc.Block() as block:
            @block.scalar
            def _(act):
                act.wait_ge(squared, 1)
                act.sqrt(length[:], length[:]).then_inc(rooted, 1)

            @block.vector
            def _(dve):
                dve.tensor_tensor(square[:], r, r, ALU.mult).then_inc(chain, 1)
                dve.wait_ge(chain, 1)
                dve.tensor_reduce(length[:], square[:], AX_X, ALU.add).then_inc(squared, 1)
                dve.wait_ge(rooted, 1)
                dve.reciprocal(length[:], length[:]).then_inc(chain, 1)
                dve.wait_ge(chain, 2)
                dve.tensor_tensor(unit[:], r, length[:].unsqueeze(2).to_broadcast([P, CH, 3]), ALU.mult)\
                    .then_inc(done, 1)


def vector_messages(nc, c, a, unit, total):
    Q, SA, SB, VA, VB = (k * P for k in (0, 1, 2, 3, 6))
    QUADS = CH // QUAD
    with Stage(nc, "t2") as s:
        wf1 = s.sb("wf1", [RBF, P])
        bf1 = s.sb("bf1", [P, 1])
        wf2 = s.sb("wf2", [P, D])
        bf2 = s.sb("bf2", [P, D])
        attr = [s.sb(f"attr{k}", [P, QUAD, RBF]) for k in range(2)]
        attr_t = s.sb("attr_t", [RBF, D])
        size = s.sb("size", [P, D])
        above = s.sb("above", [P, D])
        hid = [s.sb(f"hid{k}", [P, D]) for k in range(2)]
        at = [s.sb(f"at{h}", [P, QUAD], I32) for h in range(2)]
        rows = [s.sb(f"rows{j}", [P, D]) for j in range(RING)]
        hot = [s.sb(f"hot{j}", [P, P]) for j in range(2)]
        filt = [s.sb(f"filt{j}", [P, D]) for j in range(2)]
        along = [s.sb(f"along{j}", [P, P]) for j in range(2)]
        mess = [s.sb(f"mess{j}", [P, 9 * P]) for j in range(2)]
        turn, pre = s.ps("turn"), s.ps("pre")
        fps = [s.ps(f"fps{j}") for j in range(2)]
        part = [s.ps(f"part{j}", [P, 2 * D]) for j in range(2)]
        w_in, attr_ok, turned, attr_t_ok, pre_ok, sized, logged, aboved, hid_ok = (s.sem(n) for n in (
            "w_in", "attr_ok", "turned", "attr_t_ok", "pre_ok", "sized", "logged", "aboved", "hid_ok"))
        placed, issued, marked, filtered, biased = (s.sem(n) for n in (
            "placed", "issued", "marked", "filtered", "biased"))
        landed = c.landings.take([CH // RING] * RING)
        dots, mixed, scaled, outer, pushed, summed, added, raised = (s.sem(n) for n in (
            "dots", "mixed", "scaled", "outer", "pushed", "summed", "added", "raised"))
        flat = total[:, :, :].rearrange("p t d -> p (t d)")

        def over_quads(engine, quad):
            with engine.Fori(0, QUADS // 2 - 1) as i:
                for u in range(2):
                    quad(i * 2 + u, u, True)
            quad(QUADS - 2, 0, True)
            quad(QUADS - 1, 1, False)

        with nc.Block() as block:
            @block.sync
            def _(sp):
                sp.dma_start(wf1[:], a["L2_gnn_Wf1"]).then_inc(w_in, 16)
                sp.dma_start(bf1[:], a["L2_gnn_bf1_t"]).then_inc(w_in, 16)
                sp.dma_start(wf2[:], a["L2_gnn_Wf2_t"]).then_inc(w_in, 16)
                sp.dma_start(bf2[:], a["L2_gnn_bf2_t"].partition_broadcast(P)).then_inc(w_in, 16)

            @block.gpsimd
            def _(pool):
                with pool.Fori(0, CH // RING) as i:
                    for h in range(RING // QUAD):
                        first = i * RING + h * QUAD
                        pool.wait_ge(summed, first + QUAD)
                        pool.tensor_copy(at[h][:], c.rec_s[:, bass.ds(first, QUAD), S_OTHER].bitcast(I32))\
                            .then_inc(placed, 1)
                        pool.wait_ge(placed, i * (RING // QUAD) + h + 1)
                        pool.sem_inc(issued, 1)
                        for j in range(h * QUAD, (h + 1) * QUAD):
                            k = j - h * QUAD
                            pool.indirect_dma_start(rows[j][:], None, c.rows[0:N, :],
                                                    bass.IndirectOffsetOnAxis(ap=at[h][:, k:k + 1], axis=0))\
                                .then_inc(landed[j][0], 16)

            @block.scalar
            def _(act):
                def attributes(g, u):
                    act.wait_ge(turned, g + 1)
                    act.copy(attr[u][:], c.rec_s[:, bass.ds(g * QUAD, QUAD), S_RBF:S_RBF + RBF]).then_inc(attr_ok, 1)

                def hidden(g):
                    act.wait_ge(turned, 2 + g + 1)
                    act.copy(attr_t[:], turn[0:RBF, :]).then_inc(attr_t_ok, 1)
                    act.wait_ge(pre_ok, g + 1)
                    act.wait_ge(hid_ok, g + 1)
                    act.activation(size[:], pre[:], ACT.Abs, bias=bf1[:]).then_inc(sized, 1)
                    act.activation(above[:], pre[:], ACT.Relu, bias=bf1[:]).then_inc(aboved, 1)
                    act.wait_ge(sized, g + 1)
                    act.activation(size[:], size[:], ACT.Exp, scale=-1.0).then_inc(raised, 1)
                    act.wait_ge(raised, g + 1)
                    act.activation(size[:], size[:], ACT.Ln, bias=c.ones[:, 0:1]).then_inc(logged, 1)

                def scale(q, j):
                    k = j % 2
                    act.wait_ge(mixed, q + 1)
                    for i in range(3):
                        last = act.mul(mess[k][:, VA + i * P:VA + (i + 1) * P], mess[k][:, Q:Q + P],
                                       unit[:, bass.ds(q, 1), i:i + 1].rearrange("p a b -> p (a b)"))
                    last.then_inc(scaled, 1)

                def quad(g, u, more):
                    if more:
                        attributes(g + 1, 1 - u)
                    for j in range(QUAD):
                        if j == 1 and more:
                            hidden(g + 1)
                        scale(g * QUAD + j, j)

                attributes(0, 0)
                hidden(0)
                over_quads(act, quad)

            @block.tensor
            def _(pe):
                def hidden(g, u):
                    pe.wait_ge(attr_ok, g + 1)
                    if not isinstance(g, int) or g > 0:
                        pe.wait_ge(attr_t_ok, g)
                    for j in range(QUAD):
                        last = pe.transpose(turn[0:RBF, j * P:(j + 1) * P], attr[u][:, j, :], c.ident[:])
                    last.then_inc(turned, 1)
                    pe.wait_ge(attr_t_ok, g + 1)
                    pe.wait_ge(aboved, g + 1)
                    pe.matmul(pre[:], wf1[:], attr_t[:], start=True, stop=True).then_inc(pre_ok, 1)

                def sum_up(q, j):
                    k = j % 2
                    pe.wait_ge(marked, q + 1)
                    pe.wait_ge(added, q + 1)
                    pe.wait_ge(outer, q + 1)
                    pe.wait_ge(scaled, q + 1)
                    pe.matmul(part[k][:, 0:D], hot[k][:], mess[k][:, P:P + D], start=True, stop=True)
                    pe.matmul(part[k][:, D:2 * D], hot[k][:], mess[k][:, P + D:P + 2 * D], start=True, stop=True)\
                        .then_inc(summed, 1)

                def filter_at(g, u, j):
                    if j == 0:
                        pe.wait_ge(hid_ok, g + 2)
                    pe.wait_ge(biased, g * QUAD + j + 1)
                    pe.matmul(fps[j % 2][:], hid[u][:, j * P:(j + 1) * P], wf2[:], start=True, stop=True)\
                        .then_inc(filtered, 1)

                def quad(g, u, more):
                    for j in range(QUAD):
                        if j == 0 and more:
                            hidden(g + 1, 1 - u)
                        if j < QUAD - 1:
                            filter_at(g, u, j + 1)
                        elif more:
                            filter_at(g + 1, 1 - u, 0)
                        sum_up(g * QUAD + j, j)

                pe.wait_ge(w_in, 64)
                hidden(0, 0)
                filter_at(0, 0, 0)
                over_quads(pe, quad)

            @block.vector
            def _(dve):
                dve.memset(flat, 0.0).then_inc(added, 2)
                dve.sem_inc(summed, RING)
                dve.sem_inc(biased, 2)
                dve.sem_inc(turned, 2)
                dve.sem_inc(aboved, 1)
                dve.sem_inc(hid_ok, 1)

                def hidden(g, u):
                    dve.wait_ge(logged, g + 1)
                    dve.wait_ge(aboved, g + 2)
                    dve.scalar_tensor_tensor(out=hid[u][:], in0=above[:], scalar=-LOG2, in1=size[:],
                                             op0=ALU.add, op1=ALU.add).then_inc(hid_ok, 1)

                def message(q, turn, u, j):
                    k, slot = j % 2, u * QUAD + j
                    node, m = rows[slot], mess[k]
                    along_ = [unit[:, bass.ds(q, 1), i:i + 1].rearrange("p a b -> p (a b)") for i in range(3)]
                    dve.wait_ge(summed, RING - 2 + q + 1)
                    dve.tensor_scalar(hot[k][:], c.iota[:, 0:P],
                                      c.rec_s[:, bass.ds(q, 1), S_LO:S_LO + 1].rearrange("p a b -> p (a b)"),
                                      c.rec_s[:, bass.ds(q, 1), S_W:S_W + 1].rearrange("p a b -> p (a b)"),
                                      ALU.is_equal, ALU.mult).then_inc(marked, 1)
                    dve.wait_ge(filtered, q + 1)
                    dve.tensor_tensor(filt[k][:], fps[k][:], bf2[:], ALU.add).then_inc(biased, 1)
                    dve.wait_ge(landed[slot][0], landed[slot][1] + (turn + 1) * 16)
                    dve.tensor_scalar(along[k][:], node[:, P:2 * P], along_[0], None, ALU.mult).then_inc(dots, 1)
                    dve.wait_ge(biased, 2 + q + 1)
                    dve.tensor_tensor(m[:, Q:Q + 2 * P].rearrange("p (a f) -> p a f", a=2),
                                      filt[k][:, 0:2 * P].rearrange("p (a f) -> p a f", a=2),
                                      node[:, 0:P].unsqueeze(1).to_broadcast([P, 2, P]), ALU.mult).then_inc(mixed, 1)
                    for i in (1, 2):
                        dve.wait_ge(dots, q * 3 + i)
                        dve.scalar_tensor_tensor(out=along[k][:], in0=node[:, (i + 1) * P:(i + 2) * P],
                                                 scalar=along_[i], in1=along[k][:],
                                                 op0=ALU.mult, op1=ALU.add).then_inc(dots, 1)
                    dve.tensor_tensor(m[:, VB:VB + 3 * P].rearrange("p (a f) -> p a f", a=3),
                                      node[:, P:4 * P].rearrange("p (a f) -> p a f", a=3),
                                      filt[k][:, 3 * P:4 * P].unsqueeze(1).to_broadcast([P, 3, P]),
                                      ALU.mult)
                    dve.wait_ge(dots, q * 3 + 3)
                    dve.tensor_tensor(m[:, SB:SB + P], along[k][:], filt[k][:, 2 * P:3 * P], ALU.mult).then_inc(outer, 1)

                def add(q, j):
                    tile = dve.value_load(c.tile_row[0:1, 0, bass.ds(q, 1)], min_val=0, max_val=NT - 1)
                    dve.wait_ge(summed, RING + q + 1)
                    dve.wait_ge(added, 2 + q)
                    there = flat[:, bass.ds(tile * (2 * D), 2 * D)]
                    dve.tensor_tensor(there, there, part[j % 2][:], ALU.add).then_inc(added, 1)

                def quad(g, turn, u, more):
                    for j in range(QUAD):
                        if j == 3 and more:
                            hidden(g + 1, 1 - u)
                        message(g * QUAD + j, turn, u, j)
                        if j > 0:
                            add(g * QUAD + j - 1, j - 1)
                    add(g * QUAD + 3, 3)

                dve.wait_ge(w_in, 64)
                hidden(0, 0)
                with dve.Fori(0, QUADS // 2 - 1) as i:
                    for u in range(2):
                        quad(i * 2 + u, i, u, True)
                quad(QUADS - 2, QUADS // 2 - 1, 0, True)
                quad(QUADS - 1, QUADS // 2 - 1, 1, False)


def vector_update(nc, c, a, total):
    with Stage(nc, "t3") as s:
        w1 = s.sb("w1", [P, 2, 2, P])
        w2 = s.sb("w2", [P, 2, P])
        sums_t = s.sb("sums_t", [P, 8, N])
        size = s.sb("size", [P, N])
        mid = s.sb("mid", [P, 4, N])
        turn = [s.ps(f"turn{k}") for k in range(2)]
        first = [s.ps(f"first{k}") for k in range(2)]
        second = [s.ps(f"second{k}") for k in range(2)]
        w_in, w_ok, turned, taken, one, copied, sized, clipped, raised, logged, mid_ok, two, added, chain = (
            s.sem(n) for n in ("w_in", "w_ok", "turned", "taken", "one", "copied", "sized", "clipped", "raised",
                               "logged", "mid_ok", "two", "added", "chain"))
        kinds = [(0, 1)] + [(2 + i, 5 + i) for i in range(3)]
        scales = [(Y0 / 16, Y1 / math.sqrt(3.0) / 16), (Y1 / 16, Y0 / 16)]
        work = [(o, n) for o in range(4) for n in range(2)]
        with nc.Block() as block:
            @block.sync
            def _(sp):
                sp.dma_start(w1[:, 0], a["L2_gnn_W1_s_t"]).then_inc(w_in, 16)
                sp.dma_start(w1[:, 1], a["L2_gnn_W1_v_t"]).then_inc(w_in, 16)
                sp.dma_start(w2[:, 0], a["L2_gnn_W2_s"]).then_inc(w_in, 16)
                sp.dma_start(w2[:, 1], a["L2_gnn_W2_v"]).then_inc(w_in, 16)

            @block.tensor
            def _(pe):
                for i in range(NT * 2):
                    if i >= 2:
                        pe.wait_ge(taken, i - 1)
                    for k in range(4):
                        col = (i % 2 * 4 + k) * P
                        last = pe.transpose(turn[i % 2][:, k * P:(k + 1) * P], total[:, i // 2, col:col + P], c.ident[:])
                    last.then_inc(turned, 1)
                pe.wait_ge(w_ok, 6)
                pe.wait_ge(taken, NT * 2)
                for i, (o, n) in enumerate(work):
                    if i >= 2:
                        pe.wait_ge(copied, i - 1)
                    for k in range(2):
                        last = pe.matmul(first[i % 2][:], w1[:, min(o, 1), k, :],
                                         sums_t[:, kinds[o][k], n * D:(n + 1) * D], start=k == 0, stop=k == 1)
                    last.then_inc(one, 1)
                pe.wait_ge(copied, len(work))
                pe.wait_ge(mid_ok, 1)
                for t in range(NT):
                    if t >= 2:
                        pe.wait_ge(added, 2 * (t - 1))
                    for o in range(4):
                        last = pe.matmul(second[t % 2][:, o * P:(o + 1) * P], mid[:, o, t * P:(t + 1) * P],
                                         w2[:, min(o, 1), :], start=True, stop=True)
                    last.then_inc(two, 1)

            @block.scalar
            def _(act):
                act.wait_ge(w_in, 64)
                for o in range(2):
                    for k in range(2):
                        act.mul(w1[:, o, k, :], w1[:, o, k, :], scales[o][k]).then_inc(w_ok, 1)
                    act.mul(w2[:, o, :], w2[:, o, :], 1.0 / math.sqrt(P)).then_inc(w_ok, 1)
                for i in range(NT * 2):
                    act.wait_ge(turned, i + 1)
                    act.copy(sums_t[:, i % 2 * 4:i % 2 * 4 + 4, i // 2 * P:(i // 2 + 1) * P],
                             turn[i % 2][:].rearrange("p (k n) -> p k n", k=4)).then_inc(taken, 1)
                for i, (o, n) in enumerate(work):
                    act.wait_ge(one, i + 1)
                    act.copy(mid[:, o, n * D:(n + 1) * D], first[i % 2][:]).then_inc(copied, 1)
                    if i == 1:
                        act.wait_ge(copied, 2)
                        act.activation(size[:], mid[:, 0, :], ACT.Abs).then_inc(sized, 1)
                act.wait_ge(sized, 1)
                act.activation(size[:], size[:], ACT.Exp, scale=-1.0).then_inc(raised, 1)
                act.wait_ge(raised, 1)
                act.activation(size[:], size[:], ACT.Ln, bias=c.ones[:, 0:1]).then_inc(logged, 1)

            @block.vector
            def _(dve):
                dve.wait_ge(sized, 1)
                dve.tensor_scalar(mid[:, 0, :], mid[:, 0, :], 0.0, -LOG2, ALU.max, ALU.add).then_inc(clipped, 1)
                dve.wait_ge(clipped, 1)
                dve.wait_ge(logged, 1)
                dve.tensor_tensor(mid[:, 0, :], mid[:, 0, :], size[:], ALU.add).then_inc(mid_ok, 1)
                for t in range(NT):
                    dve.wait_ge(two, t + 1)
                    dve.tensor_tensor(c.X[:, t, 0:P], c.X[:, t, 0:P], second[t % 2][:, 0:P], ALU.add).then_inc(added, 1)
                    there = c.X[:, t, P:D].rearrange("p (d i) -> p d i", i=3)
                    dve.tensor_tensor(there, there, second[t % 2][:, P:D].rearrange("p (i d) -> p d i", i=3),
                                      ALU.add).then_inc(added, 1)



def layer0_messages(nc, c, a):
    with Stage(nc, "l0g") as s:
        c.XLT = s.sb("xlt", [P, DC, N])
        norm(nc, c, "l0n", c.X, c.XL, turned=c.XLT)
        node_tables(nc, c, "l0t", a["L0_gnn_weight_t"], None, c.rows)
    aggregate(nc, c, "l0a", 0, c.rec_s, S_OTHER, S_LO, S_W, c.rows[0:N, :], c.X)


def layer0_memory(nc, c, a):
    with Stage(nc, "m0g") as s:
        q = s.sb("q", [P, HEADS, N])
        with Stage(nc, "m0h") as t:
            c.XLT = t.sb("xlt", [P, DC, N])
            norm(nc, c, "m0n", c.X, c.XL, turned=c.XLT)
            memory_queries(nc, c, a, q)
        memory_lookup(nc, c, a, q)


def layer1_messages(nc, c, a):
    with Stage(nc, "l1g") as s:
        c.XLT = s.sb("xlt", [P, DC, N])
        agg = s.sb("agg", [P, NT, D])
        degree = s.sb("degree", [P, NT])
        norm(nc, c, "l1n", c.X, c.XL, turned=c.XLT)
        node_tables(nc, c, "l1t", a["L1_gnn_W_rel"], a["L1_gnn_b_rel"], c.rows)
        aggregate(nc, c, "l1a", 1, c.rec_d, D_TYPED, D_LO, D_W, c.rows, agg, degree, clear=True)
        with Stage(nc, "l1h") as h:
            mixed = h.sb("mixed", [P, NT, D])
            relation_update(nc, c, a, agg, degree, mixed)
            norm(nc, c, "l1p", mixed, c.XL, affine=(a["L1_gnn_ln1_g"], a["L1_gnn_ln1_b"]), turned=c.XLT)
            relation_mlp(nc, c, a, c.XL, c.XLT, mixed)
            norm(nc, c, "l1q", mixed, c.XL, affine=(a["L1_gnn_ln2_g"], a["L1_gnn_ln2_b"]), residual=True)


def layer1_experts(nc, c, a):
    with Stage(nc, "l1f") as s:
        c.XLT = s.sb("xlt", [P, DC, N])
        gate_t = s.sb("gate_t", [8, N])
        norm(nc, c, "l1r", c.X, c.XL, turned=c.XLT)
        capacity_gates(nc, c, a, gate_t)
        expert_mix(nc, c, "l1x", gate_t, a["L1_ffn_w1_t"], a["L1_ffn_b1_t"], a["L1_ffn_w2_t"], a["L1_ffn_b2"])


def layer2_messages(nc, c, a):
    with Stage(nc, "tg") as s:
        unit = s.sb("unit", [P, CH, 3])
        total = s.sb("total", [P, NT, 2 * D])
        directions(nc, c, unit)
        with Stage(nc, "th") as t:
            c.XLT = t.sb("xlt", [P, DC, N])
            norm(nc, c, "tn", c.X, c.XL, turned=c.XLT,
                 columns=[slice(0, P)] + [slice(P + i, D, 3) for i in range(3)])
            vector_node_rows(nc, c, a)
        vector_messages(nc, c, a, unit, total)
        vector_update(nc, c, a, total)


def layer2_experts(nc, c, a):
    with Stage(nc, "l2f") as s:
        c.XLT = s.sb("xlt", [P, DC, N])
        gate_t = s.sb("gate_t", [8, N])
        norm(nc, c, "l2r", c.X, c.XL, turned=c.XLT)
        choice_gates(nc, c, a, gate_t)
        expert_mix(nc, c, "l2x", gate_t, a["L2_ffn_W1_t"], a["L2_ffn_b1_t"], a["L2_ffn_W2_t"], a["L2_ffn_b2"])


def layer3_messages(nc, c, a):
    with Stage(nc, "l3g") as s:
        c.XLT = s.sb("xlt", [P, DC, N])
        agg = s.sb("agg", [P, NT, D])
        degree = s.sb("degree", [P, NT])
        norm(nc, c, "l3n", c.X, c.XL, turned=c.XLT, rows=c.rows)
        aggregate(nc, c, "l3a", 1, c.rec_d, D_OTHER, D_LO, None, c.rows[0:N, :], agg, degree, clear=True)
        sage_update(nc, c, a, agg, degree)


def layer3_expert(nc, c, a):
    with Stage(nc, "l3f") as s:
        c.XLT = s.sb("xlt", [P, DC, N])
        norm(nc, c, "l3r", c.X, c.XL, turned=c.XLT)
        one_expert(nc, c, a)


LAYERS = [layer0_messages, layer0_memory, layer1_messages, layer1_experts, layer2_messages, layer2_experts,
          layer3_messages, layer3_expert]


MESSAGES = [layer0_messages, layer1_messages, layer2_messages, layer3_messages]


def program(nc, a, out, layers=None):
    with ExitStack() as ctx:
        c = Shared(nc, ctx)
        load_nodes(nc, c, a["x"])
        if layers is None or layers[0] in MESSAGES or layers[-1] in MESSAGES:
            bin_edges(nc, c, a)
        for layer in layers or LAYERS:
            layer(nc, c, a)
        with nc.semaphore("out_stored") as stored, nc.Block() as block:
            @block.sync
            def _(sp):
                sp.dma_start(out.rearrange("(t p) d -> p t d", p=P), c.X[:, :, :]).then_inc(stored, 16)
                sp.wait_ge(stored, 16)


def layouts(i, np):
    o = {k: i[k] for k in ("x", "src", "dst", "edge_attr_20", "edge_attr_3", "edge_type_4", "edge_weight")}
    o["L0_gnn_weight_t"] = i["L0_gnn_weight"].T[None]
    o["L0_ffn_Wq"] = i["L0_ffn_Wq"]
    o["L0_ffn_bq_t"] = i["L0_ffn_bq"].reshape(HEADS, P).T
    o["L0_ffn_keys_t"] = i["L0_ffn_keys"].transpose(1, 3, 0, 2).reshape(P, HEADS, NKEYS)
    o["L0_ffn_w_rows"] = np.concatenate([i["L0_ffn_w_down"], i["L0_ffn_w_up"]], axis=1)
    for k in ("W_self", "b_self", "W_rel", "b_rel", "ln1_g", "ln1_b", "ln2_g", "ln2_b", "W_ffn1", "W_ffn2", "b_ffn2"):
        o[f"L1_gnn_{k}"] = i[f"L1_gnn_{k}"]
    o["L1_gnn_b_ffn1_t"] = i["L1_gnn_b_ffn1"].reshape(-1, P).T
    o["L1_ffn_gate_w_t"] = i["L1_ffn_gate_w"].T
    for name, w1, b1, w2 in (("L1_ffn", "w1", "b1", "w2"), ("L2_ffn", "W1", "b1", "W2")):
        o[f"{name}_{w1}_t"] = i[f"{name}_{w1}"].transpose(1, 0, 2).reshape(D, 256)
        o[f"{name}_{b1}_t"] = i[f"{name}_{b1}"].reshape(2, P).T
        o[f"{name}_{w2}_t"] = i[f"{name}_{w2}"].reshape(256, D)
        o[f"{name}_b2"] = i[f"{name}_b2"]
    def by_kind(w):
        w = w[..., :4 * P].reshape(*w.shape[:-1], 2, P, 2)
        return np.concatenate([w[..., 1, :, 0], w[..., 0, :, 0], w[..., 0, :, 1], w[..., 1, :, 1]], axis=-1)

    o["L2_gnn_Wf1"] = i["L2_gnn_Wf1"]
    o["L2_gnn_bf1_t"] = i["L2_gnn_bf1"][:, None]
    o["L2_gnn_Wf2_t"] = by_kind(i["L2_gnn_Wf2"])
    o["L2_gnn_bf2_t"] = by_kind(i["L2_gnn_bf2"])
    for k in ("W1_s", "W1_v"):
        o[f"L2_gnn_{k}_t"] = i[f"L2_gnn_{k}"].reshape(P, 2, P)
    for k in ("W_in2f_s", "W_in2f_v", "W2_s", "W2_v"):
        o[f"L2_gnn_{k}"] = i[f"L2_gnn_{k}"]
    for k in ("L2_ffn_Wr", "L3_gnn_W", "L3_gnn_b", "L3_ffn_Wg", "L3_ffn_bg", "L3_ffn_be"):
        o[k] = i[k]
    o["L3_ffn_We_rows"] = i["L3_ffn_We"].reshape(-1, D)
    return {k: np.ascontiguousarray(v) for k, v in o.items()}


def kernel(**inputs):
    import numpy as np
    import concourse.bacc as bacc
    from concourse.bass_utils import run_bass_kernel_spmd

    nc = bacc.Bacc("TRN2", target_bir_lowering=False, num_devices=1)
    arrays = layouts({k: np.asarray(v) for k, v in inputs.items()}, np)
    a = {k: nc.dram_tensor(f"in_{k}", v.shape, mybir.dt.from_np(v.dtype), kind="ExternalInput").ap()
         for k, v in arrays.items()}
    out = nc.dram_tensor("out_x", (N, D), F32, kind="ExternalOutput").ap()
    program(nc, a, out)
    r = run_bass_kernel_spmd(nc, [{f"in_{k}": v for k, v in arrays.items()}], core_ids=[0])
    return r.results[0]["out_x"]
```

```python
from contextlib import ExitStack
import math

import concourse.bass as bass
from concourse import mybir

F32 = mybir.dt.float32
BF16 = mybir.dt.bfloat16
I32 = mybir.dt.int32
U32 = mybir.dt.uint32
ALU = mybir.AluOpType
ACT = mybir.ActivationFunctionType
AX_X = mybir.AxisListType.X

P = 128
N = 1024
D = 512
NT = N // P
DC = D // P
E = 17408
EP = E // P
CH = EP + NT
SLOTS = CH * P
RS = 32
RD = 4
S_RBF, S_U, S_W, S_LO, S_OTHER = 0, 20, 23, 24, 25
D_W, D_LO, D_OTHER, D_TYPED = 0, 1, 2, 3
RBF = 20
EPS = 1e-5
ROWS = 16
PART = 4
FREED = 2
DEEP = 16
RING = 8
GROUP = EP // NT
KNOWN = 8
LEAD = 4


class Stage:

    def __init__(self, nc, tag):
        self.nc, self.tag, self.ctx, self.sems = nc, tag, ExitStack(), []

    def __enter__(self):
        return self

    def __exit__(self, *e):
        self.ctx.close()
        if self.sems:
            self.nc.clear_and_free_semaphores(self.sems)
            self.nc.all_engine_barrier(sem_only=True)
        return False

    def sb(self, name, shape, dt=F32):
        return self.ctx.enter_context(self.nc.sbuf_tensor(f"{self.tag}_{name}", shape, dt))

    def ps(self, name, shape=(P, D)):
        return self.ctx.enter_context(self.nc.psum_tensor(f"{self.tag}_{name}", list(shape), F32))

    def sem(self, name):
        self.sems.append(self.nc.alloc_semaphore(f"{self.tag}_{name}"))
        return self.sems[-1]


class Landings:

    def __init__(self, ctx, nc):
        self.sems = [ctx.enter_context(nc.semaphore(f"landed{k}")) for k in range(ROWS)]
        self.counts = [0] * ROWS
        self.scattered = [ctx.enter_context(nc.semaphore(f"scattered{u}")) for u in range(2)]

    def take(self, transfers):
        pairs = [(self.sems[k], self.counts[k]) for k in range(len(transfers))]
        for k, n in enumerate(transfers):
            self.counts[k] += 16 * n
        return pairs


class Shared:

    def __init__(self, nc, ctx):
        def sb(name, shape, dt=F32):
            return ctx.enter_context(nc.sbuf_tensor(name, shape, dt))

        def dram(name, shape):
            return nc.dram_tensor(name, shape, F32, kind="Internal").ap()

        self.X = sb("X", [P, NT, D])
        self.XL = sb("XL", [P, NT, D])
        self.XLT = None
        self.ident = sb("ident", [P, P])
        self.ones = sb("ones", [P, P])
        self.before = sb("before", [P, P])
        self.spread = sb("spread", [8, 256])
        self.iota = sb("iota", [P, 144])
        self.eps = sb("eps", [P, 1])
        self.rec_s = sb("rec_s", [P, CH, RS])
        self.rec_d = sb("rec_d", [P, CH, RD])
        self.tile_of = sb("tile_of", [P, 2, CH])
        self.tile_row = sb("tile_row", [1, 2, CH], I32)
        self.by_src = dram("by_src", [SLOTS, RS])
        self.by_dst = dram("by_dst", [SLOTS, RD])
        self.rows = dram("rows", [4 * N, D])
        self.slot = sb("slot", [P, 2, EP], I32)
        self.loose_d = sb("loose_d", [P, EP, RD])
        self.landings = Landings(ctx, nc)



def make_constants(nc, c):
    with Stage(nc, "setup") as s:
        filled, made, bounded = s.sem("filled"), s.sem("made"), s.sem("bounded")
        with nc.Block() as block:
            @block.vector
            def _(dve):
                dve.memset(c.eps[:], EPS)
                dve.memset(c.ones[:], 1.0).then_inc(filled, 1)
                dve.memset(c.ident[:], 0.0).then_inc(filled, 1)
                dve.memset(c.spread[:], 1.0).then_inc(filled, 1)

            @block.gpsimd
            def _(pool):
                pool.iota(c.iota[:], [[1, 144]], base=0, channel_multiplier=0,
                          allow_small_or_imprecise_dtypes=True).then_inc(made, 1)
                pool.wait_ge(filled, 3)
                pool.affine_select(out=c.ident[:], in_=c.ident[:], compare_op=ALU.not_equal, fill=1.0,
                                   base=0, pattern=[[-1, P]], channel_multiplier=1).then_inc(made, 1)
                pool.affine_select(out=c.before[:], in_=c.ones[:], compare_op=ALU.is_gt, fill=0.0,
                                   base=0, pattern=[[1, P]], channel_multiplier=-1).then_inc(made, 1)
                pool.affine_select(out=c.spread[:], in_=c.spread[:], compare_op=ALU.is_ge, fill=0.0,
                                   base=0, pattern=[[1, 256]], channel_multiplier=-32).then_inc(bounded, 1)
                pool.wait_ge(bounded, 1)
                pool.affine_select(out=c.spread[:], in_=c.spread[:], compare_op=ALU.is_ge, fill=0.0,
                                   base=31, pattern=[[-1, 256]], channel_multiplier=32).then_inc(made, 1)



def bin_edges(nc, c, a, loose_s):
    with Stage(nc, "bin") as s:
        keys = s.sb("keys", [P, 2, EP], I32)
        typ = s.sb("typ", [P, EP], I32)
        tile_i = s.sb("tile_i", [P, 2, EP], I32)
        low_i = s.sb("low_i", [P, 2, EP], I32)
        tile_f = s.sb("tile_f", [P, 2, EP])
        zeros = s.sb("zeros", [P, EP])
        member = s.sb("member", [P, 2, NT, EP])
        rank = s.sb("rank", [P, 2, NT, EP])
        slot_f = s.sb("slot_f", [P, 2, EP])
        slot_i = s.sb("slot_i", [P, 2, EP], I32)
        chunk_i = s.sb("chunk_i", [P, 2, EP], I32)
        total = s.sb("total", [P, 2 * NT])
        count_f = s.sb("count_f", [P, 2 * NT])
        count_i = s.sb("count_i", [P, 2 * NT], I32)
        chunks = s.sb("chunks", [P, 2, NT])
        ends = s.sb("ends", [P, 2, NT])
        shift = s.sb("shift", [P, 2, NT])
        tmap = s.sb("tmap", [P, 2, CH])
        square = s.sb("square", [P, EP, 3])
        length = s.sb("length", [P, EP])
        rec_s, rec_d = loose_s, c.loose_d
        pad_s = s.sb("pad_s", [P, CH, RS])
        pad_d = s.sb("pad_d", [P, CH, RD])
        earlier, all_of = s.ps("earlier", [P, 2 * NT]), s.ps("all_of", [P, 2 * NT])
        keys_in, fields_in, padded = s.sem("keys_in"), s.sem("fields_in"), s.sem("padded")
        chain, counted, summed = s.sem("chain"), s.sem("counted"), s.sem("summed")
        cleared, x_in, squared, rooted = s.sem("cleared"), s.sem("x_in"), s.sem("squared"), s.sem("rooted")
        with nc.Block() as block:
            @block.sync
            def _(sp):
                sp.dma_start(keys[:, 0, :], a["src"].rearrange("(p c) -> p c", p=P)).then_inc(keys_in, 16)
                sp.dma_start(keys[:, 1, :], a["dst"].rearrange("(p c) -> p c", p=P)).then_inc(keys_in, 16)
                sp.dma_start(typ[:], a["edge_type_4"].rearrange("(p c) -> p c", p=P)).then_inc(keys_in, 16)
                sp.dma_start(rec_s[:, :, S_RBF:S_RBF + RBF],
                             a["edge_attr_20"].rearrange("(p c) f -> p c f", p=P)).then_inc(fields_in, 16)
                sp.dma_start(rec_s[:, :, S_U:S_U + 3],
                             a["edge_attr_3"].rearrange("(p c) f -> p c f", p=P)).then_inc(fields_in, 16)
                sp.dma_start(tile_f[:, 0, :], a["edge_weight"].rearrange("(p c) -> p c", p=P)).then_inc(fields_in, 16)
                sp.dma_start(c.X[:, :, :], a["x"].rearrange("(t p) d -> p t d", p=P)).then_inc(x_in, 16)
                sp.wait_ge(cleared, 1)
                sp.dma_start(c.by_src.rearrange("(p c) f -> p c f", p=P), pad_s[:]).then_inc(padded, 16)
                sp.dma_start(c.by_dst.rearrange("(p c) f -> p c f", p=P), pad_d[:]).then_inc(padded, 16)
                sp.wait_ge(padded, 32)
                sp.wait_ge(x_in, 16)

            @block.scalar
            def _(act):
                act.wait_ge(squared, 1)
                act.sqrt(length[:], length[:]).then_inc(rooted, 1)

            @block.vector
            def _(dve):
                links = [0]

                def link(ins):
                    links[0] += 1
                    ins.then_inc(chain, 1)
                    dve.wait_ge(chain, links[0])

                dve.memset(zeros[:], 0.0)
                dve.memset(rec_s[:, :, S_OTHER + 1:RS], 0.0)
                dve.memset(pad_d[:], 0.0)
                link(dve.memset(pad_s[:], 0.0))
                dve.memset(pad_s[:, :, S_U:S_U + 3], 1.0)
                dve.memset(pad_s[:, :, S_LO:S_LO + 1], -1.0)
                link(dve.memset(pad_d[:, :, D_LO:D_LO + 1], -1.0))
                dve.sem_inc(cleared, 1)
                dve.wait_ge(fields_in, 48)
                dve.wait_ge(keys_in, 48)
                dve.tensor_copy(rec_s[:, :, S_W], tile_f[:, 0, :])
                dve.tensor_copy(rec_d[:, :, D_W], tile_f[:, 0, :])
                dve.tensor_copy(rec_s[:, :, S_OTHER].bitcast(I32), keys[:, 1, :])
                dve.tensor_copy(rec_d[:, :, D_OTHER].bitcast(I32), keys[:, 0, :])
                r = rec_s[:, :, S_U:S_U + 3]
                link(dve.tensor_tensor(square[:], r, r, ALU.mult))
                dve.tensor_reduce(length[:], square[:], AX_X, ALU.add).then_inc(squared, 1)
                dve.tensor_scalar(tile_i[:], keys[:], 7, None, ALU.logical_shift_right)
                link(dve.tensor_scalar(low_i[:], keys[:], P - 1, None, ALU.bitwise_and))
                dve.scalar_tensor_tensor(out=rec_d[:, :, D_TYPED].bitcast(I32), in0=typ[:], scalar=float(N),
                                         in1=keys[:, 0, :], op0=ALU.mult, op1=ALU.add)
                dve.tensor_copy(rec_s[:, :, S_LO], low_i[:, 0, :])
                dve.tensor_copy(rec_d[:, :, D_LO], low_i[:, 1, :])
                link(dve.tensor_copy(tile_f[:], tile_i[:]))
                for b in range(NT):
                    last = dve.tensor_scalar(member[:, :, b, :], tile_f[:], float(b), None, ALU.is_equal)
                link(last)
                for k in range(2):
                    for b in range(NT):
                        last = dve.tensor_tensor_scan(rank[:, k, b, :], zeros[:], member[:, k, b, :], 0.0,
                                                      ALU.add, ALU.add)
                link(last)
                dve.tensor_copy(total[:], rank[:, :, :, EP - 1].rearrange("p k b -> p (k b)")).then_inc(counted, 1)
                dve.wait_ge(rooted, 1)
                link(dve.reciprocal(length[:], length[:]))
                dve.tensor_tensor(r, r, length[:].unsqueeze(2).to_broadcast([P, EP, 3]), ALU.mult)
                dve.wait_ge(summed, 1)
                link(dve.tensor_scalar(count_f[:], all_of[:], float(P - 1), None, ALU.add))
                link(dve.tensor_copy(count_i[:], count_f[:]))
                link(dve.tensor_scalar(count_i[:], count_i[:], 7, None, ALU.logical_shift_right))
                link(dve.tensor_copy(chunks[:].rearrange("p k b -> p (k b)"), count_i[:]))
                for k in range(2):
                    last = dve.tensor_tensor_scan(ends[:, k, :], zeros[:, 0:NT], chunks[:, k, :], 0.0,
                                                  ALU.add, ALU.add)
                link(last)
                link(dve.tensor_tensor(shift[:], ends[:], chunks[:], ALU.subtract))
                link(dve.tensor_scalar(shift[:], shift[:], float(P), -1.0, ALU.mult, ALU.add))
                link(dve.tensor_tensor(shift[:].rearrange("p k b -> p (k b)"),
                                       shift[:].rearrange("p k b -> p (k b)"), earlier[:], ALU.add))
                for k in range(2):
                    for b in range(NT):
                        last = dve.scalar_tensor_tensor(out=rank[:, k, b, :], in0=rank[:, k, b, :],
                                                        scalar=shift[:, k, b:b + 1], in1=member[:, k, b, :],
                                                        op0=ALU.add, op1=ALU.mult)
                link(last)
                for k in range(2):
                    last = dve.tensor_reduce(slot_f[:, k, :], rank[:, k, :, :].rearrange("p b e -> p e b"),
                                             AX_X, ALU.add)
                link(last)
                link(dve.tensor_copy(slot_i[:], slot_f[:]))
                dve.tensor_scalar(chunk_i[:], slot_i[:], 7, None, ALU.logical_shift_right)
                link(dve.tensor_scalar(slot_i[:], slot_i[:], P - 1, None, ALU.bitwise_and))
                dve.scalar_tensor_tensor(out=c.slot[:], in0=slot_i[:], scalar=float(CH), in1=chunk_i[:],
                                         op0=ALU.mult, op1=ALU.add)
                for b in range(NT):
                    for k in range(2):
                        if b == 0:
                            last = dve.tensor_scalar(tmap[:, k, :], c.iota[:, 0:CH], ends[:, k, b:b + 1], None,
                                                     ALU.is_ge)
                        else:
                            last = dve.scalar_tensor_tensor(out=tmap[:, k, :], in0=c.iota[:, 0:CH],
                                                            scalar=ends[:, k, b:b + 1], in1=tmap[:, k, :],
                                                            op0=ALU.is_ge, op1=ALU.add)
                    link(last)
                link(dve.tensor_scalar(c.tile_of[:], tmap[:], float(NT - 1), None, ALU.min))
                dve.tensor_copy(c.tile_row[:], c.tile_of[0:1, :, :])

            @block.tensor
            def _(pe):
                pe.wait_ge(counted, 1)
                pe.matmul(earlier[:], c.before[:], total[:], start=True, stop=True)
                pe.matmul(all_of[:], c.ones[:], total[:], start=True, stop=True).then_inc(summed, 1)


class Scatter:

    def __init__(self, nc, c, s, order, loose, table, words):
        self.c, self.order, self.loose, self.table = c, order, loose, table
        self.at = [s.sb(f"slots{u}", [P, GROUP], I32) for u in range(2)]
        self.recs = [s.sb(f"recs{u}", [P, GROUP, words]) for u in range(2)]
        self.base = order * EP // 2 * 16
        self.copied, self.sent = s.sem("copied"), s.sem("sent")

    def copy(self, pool, g, u, first=False):
        if not first:
            pool.wait_ge(self.c.landings.scattered[u], self.base + (g - u) * (GROUP * 8))
        pool.tensor_copy(self.at[u][:], self.c.slot[:, self.order, bass.ds(g * GROUP, GROUP)])\
            .then_inc(self.copied, 1)
        pool.tensor_copy(self.recs[u][:], self.loose[:, bass.ds(g * GROUP, GROUP), :]).then_inc(self.copied, 1)

    def send(self, pool, g, u, columns):
        pool.wait_ge(self.copied, g * 2 + 2)
        pool.sem_inc(self.sent, 1)
        for k in columns:
            pool.indirect_dma_start(self.table, bass.IndirectOffsetOnAxis(ap=self.at[u][:, k:k + 1], axis=0),
                                    self.recs[u][:, k, :], None).then_inc(self.c.landings.scattered[u], 16)

    def finish(self, pool, done):
        for u in range(2):
            pool.wait_ge(self.c.landings.scattered[u], self.base + EP // 2 * 16)
        pool.sem_inc(done, 1)



def norm(nc, c, tag, src, dst, affine=None, turned=None, columns=None, rows=None, residual=False, scatter=None):
    columns = columns or [slice(k * P, (k + 1) * P) for k in range(DC)]
    with Stage(nc, tag) as s:
        stats = s.sb("stats", [P, NT, 6])
        mv = s.sb("mv", [P, NT, 2])
        dev = s.sb("dev", [P, NT])
        rdev = s.sb("rdev", [P, NT])
        gains = s.sb("gains", [P, 2, D]) if affine else None
        turn = [s.ps(f"turn{k}") for k in range(2)]
        stat, moment, rooted, inverted, centred, scaled, shifted, added = (s.sem(n) for n in (
            "stat", "moment", "rooted", "inverted", "centred", "scaled", "shifted", "added"))
        turned_ok, taken, stored, gains_in = s.sem("turned"), s.sem("taken"), s.sem("stored"), s.sem("gains_in")
        final = shifted if affine else centred
        with nc.Block() as block:
            if scatter:
                @block.gpsimd
                def _(pool):
                    scatter.copy(pool, 0, 0, first=True)
                    scatter.send(pool, 0, 0, range(GROUP))

            @block.sync
            def _(sp):
                if affine:
                    for k in range(2):
                        sp.dma_start(gains[:, k, :], affine[k].partition_broadcast(P)).then_inc(gains_in, 16)
                if rows is not None:
                    for t in range(NT):
                        sp.wait_ge(final, t + 1)
                        sp.dma_start(rows[t * P:(t + 1) * P, :], dst[:, t, :]).then_inc(stored, 16)
                    sp.wait_ge(stored, 16 * NT)

            @block.vector
            def _(dve):
                for t in range(NT):
                    dve.bn_stats(stats[:, t, :], src[:, t, :]).then_inc(stat, 1)
                for t in range(NT):
                    dve.wait_ge(stat, t + 1)
                    dve.bn_aggr(mv[:, t, :], stats[:, t, :]).then_inc(moment, 1)
                dve.wait_ge(rooted, 1)
                dve.reciprocal(rdev[:], dev[:]).then_inc(inverted, 1)
                dve.wait_ge(inverted, 1)
                for t in range(NT):
                    dve.tensor_scalar(dst[:, t, :], src[:, t, :], mv[:, t, 0:1], rdev[:, t:t + 1],
                                      ALU.subtract, ALU.mult).then_inc(centred, 1)
                if affine:
                    dve.wait_ge(gains_in, 32)
                    for t in range(NT):
                        dve.wait_ge(centred, t + 1)
                        dve.tensor_tensor(dst[:, t, :], dst[:, t, :], gains[:, 0, :], ALU.mult).then_inc(scaled, 1)
                    for t in range(NT):
                        dve.wait_ge(scaled, t + 1)
                        dve.tensor_tensor(dst[:, t, :], dst[:, t, :], gains[:, 1, :], ALU.add).then_inc(shifted, 1)
                if residual:
                    for t in range(NT):
                        dve.wait_ge(final, t + 1)
                        dve.tensor_tensor(c.X[:, t, :], c.X[:, t, :], dst[:, t, :], ALU.add).then_inc(added, 1)

            @block.scalar
            def _(act):
                act.wait_ge(moment, NT)
                act.activation(dev[:], mv[:, :, 1], ACT.Sqrt, bias=c.eps[:]).then_inc(rooted, 1)
                if turned is not None:
                    for t in range(NT):
                        act.wait_ge(turned_ok, t + 1)
                        act.copy(turned[:, :, t * P:(t + 1) * P],
                                 turn[t % 2][:, :].rearrange("p (k n) -> p k n", k=DC)).then_inc(taken, 1)

            @block.tensor
            def _(pe):
                if turned is not None:
                    for t in range(NT):
                        pe.wait_ge(final, t + 1)
                        if t >= 2:
                            pe.wait_ge(taken, t - 1)
                        for k, cols in enumerate(columns):
                            last = pe.transpose(turn[t % 2][:, k * P:(k + 1) * P], dst[:, t, cols], c.ident[:])
                        last.then_inc(turned_ok, 1)



def node_tables(nc, c, tag, weights, biases, table, scatter=None):
    R = weights.shape[0]
    with Stage(nc, tag) as s:
        w = s.sb("w", [P, R, DC, D])
        bias = s.sb("bias", [P, R, D]) if biases is not None else None
        row = [s.sb(f"row{k}", [P, D]) for k in range(4)]
        out = [s.ps(f"out{k}") for k in range(4)]
        w_in, product, biased = s.sem("w_in"), s.sem("product"), s.sem("biased")
        stored = [s.sem(f"stored{k}") for k in range(4)]
        scattered, reloaded = s.sem("scattered_ok"), s.sem("reloaded")
        work = [(r, t) for r in range(R) for t in range(NT)]
        with nc.Block() as block:
            if scatter:
                @block.gpsimd
                def _(pool):
                    scatter.copy(pool, 1, 1, first=True)
                    scatter.send(pool, 1, 1, range(GROUP))
                    with pool.Fori(1, NT // 2) as i:
                        for u in range(2):
                            scatter.copy(pool, i * 2 + u, u)
                            scatter.send(pool, i * 2 + u, u, range(GROUP))
                    scatter.finish(pool, scattered)

            @block.sync
            def _(sp):
                for r in range(R):
                    sp.dma_start(w[:, r], weights[r].rearrange("(k p) d -> p k d", p=P)).then_inc(w_in, 16)
                    if biases is not None:
                        sp.dma_start(bias[:, r, :], biases[r].partition_broadcast(P)).then_inc(w_in, 16)
                for i, (r, t) in enumerate(work):
                    sp.wait_ge(biased, i + 1)
                    sp.dma_start(table[(r * NT + t) * P:(r * NT + t + 1) * P, :], row[i % 4][:])\
                        .then_inc(stored[i % 4], 16)
                for k in range(4):
                    sp.wait_ge(stored[k], 16 * (len(work) // 4))
                if scatter:
                    sp.wait_ge(scattered, 1)
                    sp.dma_start(c.rec_s[:], c.by_src.rearrange("(p c) f -> p c f", p=P)).then_inc(reloaded, 16)
                    sp.wait_ge(reloaded, 16)

            @block.tensor
            def _(pe):
                pe.wait_ge(w_in, 16 * R * (2 if biases is not None else 1))
                for i, (r, t) in enumerate(work):
                    if i >= 4:
                        pe.wait_ge(biased, i - 3)
                    for k in range(DC):
                        last = pe.matmul(out[i % 4][:], c.XLT[:, k, t * P:(t + 1) * P], w[:, r, k, :],
                                         start=k == 0, stop=k == DC - 1)
                    last.then_inc(product, 1)

            @block.vector
            def _(dve):
                for i, (r, t) in enumerate(work):
                    dve.wait_ge(product, i + 1)
                    if i >= 4:
                        dve.wait_ge(stored[i % 4], 16 * (i // 4))
                    if biases is not None:
                        dve.tensor_tensor(row[i % 4][:], out[i % 4][:], bias[:, r, :], ALU.add).then_inc(biased, 1)
                    else:
                        dve.tensor_copy(row[i % 4][:], out[i % 4][:]).then_inc(biased, 1)



def tiles_of(nc, c, engine, order, first):
    _, tiles = nc.values_load_multi_w_load_instructions(
        c.tile_row[0:1, order, bass.ds(first, KNOWN)], engines=(engine.engine,), min_val=0, max_val=NT - 1,
        skip_runtime_bounds_check_because="bin_edges keeps the tiles within 0 and NT - 1")
    return tiles


def aggregate(nc, c, tag, order, rec, index, lo, weight, table, total, degree=None, clear=False):
    with Stage(nc, tag) as s:
        at = [s.sb(f"at{h}", [P, LEAD], I32) for h in range(DEEP // LEAD)]
        rows = [s.sb(f"rows{j}", [P, D]) for j in range(DEEP)]
        hot = [s.sb(f"hot{j}", [P, P]) for j in range(DEEP)]
        part = [s.ps(f"part{j}") for j in range(LEAD)]
        deg = s.ps("deg", [P, CH]) if degree is not None else None
        scratch = s.sb("scratch", [P, CH]) if degree is not None else None
        landed = c.landings.take([CH // DEEP] * DEEP)
        placed, marked, summed, added = s.sem("placed"), s.sem("marked"), s.sem("summed"), s.sem("added")
        issued, chain = s.sem("issued"), s.sem("chain")
        flat = total[:, :, :].rearrange("p t d -> p (t d)")
        LOOPS = CH // DEEP
        with nc.Block() as block:
            @block.gpsimd
            def _(pool):
                with pool.Fori(0, LOOPS) as i:
                    for h in range(DEEP // LEAD):
                        first = i * DEEP + h * LEAD
                        pool.wait_ge(summed, first + LEAD)
                        pool.tensor_copy(at[h][:], rec[:, bass.ds(first, LEAD), index].bitcast(I32))\
                            .then_inc(placed, 1)
                        pool.wait_ge(placed, i * (DEEP // LEAD) + h + 1)
                        pool.sem_inc(issued, 1)
                        for j in range(h * LEAD, (h + 1) * LEAD):
                            k = j - h * LEAD
                            pool.indirect_dma_start(rows[j][:], None, table,
                                                    bass.IndirectOffsetOnAxis(ap=at[h][:, k:k + 1], axis=0))\
                                .then_inc(landed[j][0], 16)

            @block.vector
            def _(dve):
                dve.sem_inc(summed, DEEP)
                if clear:
                    dve.memset(flat, 0.0).then_inc(added, LEAD)
                else:
                    dve.sem_inc(added, LEAD)

                def one_hot(chunk, j):
                    dve.wait_ge(summed, chunk + 1)
                    low = rec[:, bass.ds(chunk, 1), lo:lo + 1].rearrange("p a b -> p (a b)")
                    if weight is None:
                        dve.tensor_scalar(hot[j][:], c.iota[:, 0:P], low, None, ALU.is_equal).then_inc(marked, 1)
                    else:
                        w = rec[:, bass.ds(chunk, 1), weight:weight + 1].rearrange("p a b -> p (a b)")
                        dve.tensor_scalar(hot[j][:], c.iota[:, 0:P], low, w,
                                          ALU.is_equal, ALU.mult).then_inc(marked, 1)

                def add(chunk, j, tiles):
                    tile = tiles[j % KNOWN]
                    dve.wait_ge(summed, DEEP + chunk + 1)
                    dve.wait_ge(added, LEAD + chunk)
                    there = flat[:, bass.ds(tile * D, D)]
                    dve.tensor_tensor(there, there, part[j % LEAD][:], ALU.add).then_inc(added, 1)

                for j in range(LEAD):
                    one_hot(j, j)
                with dve.Fori(0, LOOPS - 1) as i:
                    for j in range(DEEP):
                        if j % KNOWN == 0:
                            tiles = tiles_of(nc, c, dve, order, i * DEEP + j)
                        one_hot(i * DEEP + j + LEAD, (j + LEAD) % DEEP)
                        add(i * DEEP + j, j, tiles)
                for j in range(DEEP):
                    chunk = (LOOPS - 1) * DEEP + j
                    if chunk + LEAD < CH:
                        one_hot(chunk + LEAD, (j + LEAD) % DEEP)
                    if j % KNOWN == 0:
                        tiles = tiles_of(nc, c, dve, order, chunk)
                    add(chunk, j, tiles)
                if degree is not None:
                    dve.wait_ge(summed, DEEP + CH)
                    for t in range(NT):
                        dve.scalar_tensor_tensor(out=scratch[:], in0=c.tile_of[:, order, :], scalar=float(t),
                                                 in1=deg[:], op0=ALU.is_equal, op1=ALU.mult).then_inc(chain, 1)
                        dve.wait_ge(chain, 2 * t + 1)
                        dve.tensor_reduce(degree[:, t:t + 1], scratch[:], AX_X, ALU.add).then_inc(chain, 1)
                        dve.wait_ge(chain, 2 * t + 2)

            @block.tensor
            def _(pe):
                with pe.Fori(0, LOOPS) as i:
                    for j in range(DEEP):
                        chunk = i * DEEP + j
                        pe.wait_ge(marked, chunk + 1)
                        pe.wait_ge(added, chunk + 1)
                        if degree is not None:
                            pe.matmul(deg[:, bass.ds(chunk, 1)], hot[j][:], c.ones[:, 0:1], start=True, stop=True)
                        pe.wait_ge(landed[j][0], landed[j][1] + (i + 1) * 16)
                        pe.matmul(part[j % LEAD][:], hot[j][:], rows[j][:], start=True, stop=True)\
                            .then_inc(summed, 1)



def relation_update(nc, c, a, agg, degree, mixed):
    with Stage(nc, "l1u") as s:
        w = s.sb("w", [P, DC, D])
        bias = s.sb("bias", [P, D])
        rdeg = s.sb("rdeg", [P, NT])
        out = [s.ps(f"out{k}") for k in range(4)]
        w_in, product, read, scaled, summed, chain = (s.sem(n) for n in (
            "w_in", "product", "read", "scaled", "summed", "chain"))
        with nc.Block() as block:
            @block.sync
            def _(sp):
                sp.dma_start(w[:], a["L1_gnn_W_self"].rearrange("(k p) d -> p k d", p=P)).then_inc(w_in, 16)
                sp.dma_start(bias[:], a["L1_gnn_b_self"].partition_broadcast(P)).then_inc(w_in, 16)

            @block.tensor
            def _(pe):
                pe.wait_ge(w_in, 32)
                for t in range(NT):
                    if t >= 4:
                        pe.wait_ge(read, t - 3)
                    for k in range(DC):
                        last = pe.matmul(out[t % 4][:], c.XLT[:, k, t * P:(t + 1) * P], w[:, k, :],
                                         start=k == 0, stop=k == DC - 1)
                    last.then_inc(product, 1)

            @block.vector
            def _(dve):
                dve.tensor_scalar(rdeg[:], degree[:], 1.0, None, ALU.max).then_inc(chain, 1)
                dve.wait_ge(chain, 1)
                dve.reciprocal(rdeg[:], rdeg[:]).then_inc(chain, 1)
                dve.wait_ge(chain, 2)
                dve.wait_ge(w_in, 32)
                for t in range(NT):
                    dve.wait_ge(product, t + 1)
                    dve.tensor_tensor(mixed[:, t, :], out[t % 4][:], bias[:], ALU.add).then_inc(read, 1)
                    dve.wait_ge(read, t + 1)
                    dve.scalar_tensor_tensor(out=mixed[:, t, :], in0=agg[:, t, :], scalar=rdeg[:, t:t + 1],
                                             in1=mixed[:, t, :], op0=ALU.mult, op1=ALU.add).then_inc(scaled, 1)
                    dve.wait_ge(scaled, t + 1)
                    dve.tensor_tensor(mixed[:, t, :], mixed[:, t, :], c.XL[:, t, :], ALU.add).then_inc(summed, 1)


def relation_mlp(nc, c, a, x1, x1t, out_sum):
    HC = 2 * D // P
    with Stage(nc, "l1m") as s:
        w1 = s.sb("w1", [P, DC, 2 * D])
        w2 = s.sb("w2", [P, HC, D])
        b1 = s.sb("b1", [P, HC])
        b2 = s.sb("b2", [P, D])
        hid = s.sb("hid", [P, HC, N])
        up = [s.ps(f"up{k}") for k in range(4)]
        down = [s.ps(f"down{k}") for k in range(4)]
        w1_in, w2_in, upped, active, downed, read, summed = (s.sem(n) for n in (
            "w1_in", "w2_in", "upped", "active", "downed", "read", "summed"))
        work = [(h, n) for h in range(HC) for n in range(2)]
        with nc.Block() as block:
            @block.sync
            def _(sp):
                sp.dma_start(w1[:], a["L1_gnn_W_ffn1"].rearrange("(k p) d -> p k d", p=P)).then_inc(w1_in, 16)
                sp.dma_start(b1[:], a["L1_gnn_b_ffn1_t"]).then_inc(w1_in, 16)
                sp.dma_start(w2[:], a["L1_gnn_W_ffn2"].rearrange("(k p) d -> p k d", p=P)).then_inc(w2_in, 16)
                sp.dma_start(b2[:], a["L1_gnn_b_ffn2"].partition_broadcast(P)).then_inc(w2_in, 16)

            @block.tensor
            def _(pe):
                pe.wait_ge(w1_in, 32)
                for i, (h, n) in enumerate(work):
                    if i >= 4:
                        pe.wait_ge(active, i - 3)
                    for k in range(DC):
                        last = pe.matmul(up[i % 4][:], w1[:, k, h * P:(h + 1) * P], x1t[:, k, n * D:(n + 1) * D],
                                         start=k == 0, stop=k == DC - 1)
                    last.then_inc(upped, 1)
                pe.wait_ge(w2_in, 32)
                pe.wait_ge(active, len(work))
                for t in range(NT):
                    if t >= 4:
                        pe.wait_ge(read, t - 3)
                    for h in range(HC):
                        last = pe.matmul(down[t % 4][:], hid[:, h, t * P:(t + 1) * P], w2[:, h, :],
                                         start=h == 0, stop=h == HC - 1)
                    last.then_inc(downed, 1)

            @block.scalar
            def _(act):
                act.wait_ge(w1_in, 32)
                for i, (h, n) in enumerate(work):
                    act.wait_ge(upped, i + 1)
                    act.activation(hid[:, h, n * D:(n + 1) * D], up[i % 4][:], ACT.Gelu,
                                   bias=b1[:, h:h + 1]).then_inc(active, 1)

            @block.vector
            def _(dve):
                dve.wait_ge(w2_in, 32)
                for t in range(NT):
                    dve.wait_ge(downed, t + 1)
                    dve.tensor_tensor(out_sum[:, t, :], down[t % 4][:], b2[:], ALU.add).then_inc(read, 1)
                    dve.wait_ge(read, t + 1)
                    dve.tensor_tensor(out_sum[:, t, :], out_sum[:, t, :], x1[:, t, :], ALU.add).then_inc(summed, 1)


def expert_mix(nc, c, tag, gate_t, w1_d, b1_d, w2_d, b2_d):
    with Stage(nc, tag) as s:
        w1 = s.sb("w1", [P, DC, 256])
        b1 = s.sb("b1", [P, 2])
        w2 = s.sb("w2", [P, 2, D])
        b2 = s.sb("b2", [8, D])
        hid = s.sb("hid", [P, 2, N])
        up = [s.ps(f"up{k}") for k in range(4)]
        wide = [s.ps(f"wide{k}") for k in range(4)]
        w_in, upped, active, gated, downed, added = (s.sem(n) for n in (
            "w_in", "upped", "active", "gated", "downed", "added"))
        work = [(h, n) for h in range(2) for n in range(2)]
        with nc.Block() as block:
            @block.sync
            def _(sp):
                sp.dma_start(w1[:], w1_d.rearrange("(k p) d -> p k d", p=P)).then_inc(w_in, 16)
                sp.dma_start(b1[:], b1_d).then_inc(w_in, 16)
                sp.dma_start(w2[:], w2_d.rearrange("(k p) d -> p k d", p=P)).then_inc(w_in, 16)
                sp.dma_start(b2[:], b2_d).then_inc(w_in, 16)

            @block.tensor
            def _(pe):
                pe.wait_ge(w_in, 64)
                for i, (h, n) in enumerate(work):
                    pe.matmul(wide[i][:], c.spread[:, h * P:(h + 1) * P], gate_t[:, n * D:(n + 1) * D],
                              start=True, stop=True)
                    for k in range(DC):
                        last = pe.matmul(up[i][:], w1[:, k, h * P:(h + 1) * P], c.XLT[:, k, n * D:(n + 1) * D],
                                         start=k == 0, stop=k == DC - 1)
                    last.then_inc(upped, 1)
                pe.wait_ge(gated, 4)
                for t in range(NT):
                    if t >= 4:
                        pe.wait_ge(added, t - 3)
                    for h in range(2):
                        pe.matmul(up[t % 4][:], hid[:, h, t * P:(t + 1) * P], w2[:, h, :], start=h == 0, stop=False)
                    pe.matmul(up[t % 4][:], gate_t[:, t * P:(t + 1) * P], b2[:], start=False, stop=True)\
                        .then_inc(downed, 1)

            @block.scalar
            def _(act):
                act.wait_ge(w_in, 64)
                for i, (h, n) in enumerate(work):
                    act.wait_ge(upped, i + 1)
                    act.activation(hid[:, h, n * D:(n + 1) * D], up[i][:], ACT.Gelu,
                                   bias=b1[:, h:h + 1]).then_inc(active, 1)

            @block.vector
            def _(dve):
                for i, (h, n) in enumerate(work):
                    dve.wait_ge(active, i + 1)
                    part = hid[:, h, n * D:(n + 1) * D]
                    dve.tensor_tensor(part, part, wide[i][:], ALU.mult).then_inc(gated, 1)
                for t in range(NT):
                    dve.wait_ge(downed, t + 1)
                    dve.tensor_tensor(c.X[:, t, :], c.X[:, t, :], up[t % 4][:], ALU.add).then_inc(added, 1)


def capacity_gates(nc, c, a, gate_t):
    NE, CAP = 8, math.ceil(1.25 * N / 8)
    with Stage(nc, "cg") as s:
        w = s.sb("w", [P, DC, NE])
        top = s.sb("top", [P, NT])
        probs = s.sb("probs", [P, NT, NE])
        sums = s.sb("sums", [P, NT])
        best = s.sb("best", [P, NT, NE])
        best_at = s.sb("best_at", [P, NT, NE], U32)
        at = s.sb("at", [P, NT, 2])
        pick = s.sb("pick", [P, 2, NT, NE])
        taken = s.sb("taken", [P, NT, NE])
        place = s.sb("place", [P, NT, NE])
        carry = s.sb("carry", [P, NT, NE])
        gate = s.sb("gate", [P, NT, NE])
        logits, earlier, all_of = (s.ps(n, [P, NT * NE]) for n in ("logits", "earlier", "all_of"))
        turn = [s.ps(f"turn{k}", [NE, D]) for k in range(2)]
        w_in, scored, cut, raised, chosen, counted, gates, turned, chain = (s.sem(n) for n in (
            "w_in", "scored", "cut", "raised", "chosen", "counted", "gates", "turned", "chain"))
        kept = s.sem("kept")

        def flat(t):
            return t[:].rearrange("p t e -> p (t e)")

        def over(t):
            return t.unsqueeze(2).to_broadcast([P, NT, NE])

        with nc.Block() as block:
            @block.sync
            def _(sp):
                sp.dma_start(w[:], a["L1_ffn_gate_w_t"].rearrange("(k p) d -> p k d", p=P)).then_inc(w_in, 16)

            @block.tensor
            def _(pe):
                pe.wait_ge(w_in, 16)
                for t in range(NT):
                    for k in range(DC):
                        last = pe.matmul(logits[:, t * NE:(t + 1) * NE], c.XLT[:, k, t * P:(t + 1) * P], w[:, k, :],
                                         start=k == 0, stop=k == DC - 1)
                last.then_inc(scored, 1)
                pe.wait_ge(chosen, 1)
                pe.matmul(earlier[:], c.before[:], flat(taken), start=True, stop=True)
                pe.matmul(all_of[:], c.ones[:], flat(taken), start=True, stop=True).then_inc(counted, 1)
                pe.wait_ge(gates, 1)
                for t in range(NT):
                    last = pe.transpose(turn[t // 4][:, (t % 4) * P:(t % 4 + 1) * P], gate[:, t, :], c.ident[:])
                last.then_inc(turned, 1)

            @block.scalar
            def _(act):
                act.wait_ge(cut, 1)
                act.activation(probs[:], probs[:], ACT.Exp).then_inc(raised, 1)

            @block.vector
            def _(dve):
                links = [0]

                def link(ins):
                    links[0] += 1
                    ins.then_inc(chain, 1)
                    dve.wait_ge(chain, links[0])

                scores = logits[:].rearrange("p (t e) -> p t e", e=NE)
                dve.wait_ge(scored, 1)
                link(dve.tensor_reduce(top[:], scores, AX_X, ALU.max))
                dve.tensor_tensor(probs[:], scores, over(top[:]), ALU.subtract).then_inc(cut, 1)
                dve.wait_ge(raised, 1)
                link(dve.tensor_reduce(sums[:], probs[:], AX_X, ALU.add))
                link(dve.reciprocal(sums[:], sums[:]))
                link(dve.tensor_tensor(probs[:], probs[:], over(sums[:]), ALU.mult))
                for t in range(NT):
                    last = dve.max(best[:, t, :], probs[:, t, :])
                link(last)
                for t in range(NT):
                    last = dve.max_index(best_at[:, t, :], best[:, t, :], probs[:, t, :])
                link(last)
                link(dve.tensor_copy(at[:], best_at[:, :, 0:2]))
                for k in range(2):
                    last = dve.tensor_tensor(pick[:, k], c.iota[:, 0:NE].unsqueeze(1).to_broadcast([P, NT, NE]),
                                             over(at[:, :, k]), ALU.is_equal)
                link(last)
                dve.tensor_tensor(taken[:], pick[:, 0], pick[:, 1], ALU.add).then_inc(chosen, 1)
                link(dve.tensor_tensor(sums[:], best[:, :, 0], best[:, :, 1], ALU.add))
                link(dve.reciprocal(sums[:], sums[:]))
                dve.wait_ge(chosen, 1)
                link(dve.tensor_tensor(gate[:], taken[:], probs[:], ALU.mult))
                link(dve.tensor_tensor(gate[:], gate[:], over(sums[:]), ALU.mult))
                link(dve.memset(carry[:, 0, :], 0.0))
                dve.wait_ge(counted, 1)
                totals = all_of[:].rearrange("p (t e) -> p t e", e=NE)
                for t in range(1, NT):
                    link(dve.tensor_tensor(carry[:, t, :], carry[:, t - 1, :], totals[:, t - 1, :], ALU.add))
                link(dve.tensor_tensor(flat(place), flat(carry), earlier[:], ALU.add))
                dve.scalar_tensor_tensor(out=flat(gate), in0=flat(place), scalar=float(CAP), in1=flat(gate),
                                         op0=ALU.is_lt, op1=ALU.mult).then_inc(gates, 1)
                dve.wait_ge(turned, 1)
                for k in range(2):
                    dve.tensor_copy(gate_t[:, k * D:(k + 1) * D], turn[k][:]).then_inc(kept, 1)


def choice_gates(nc, c, a, gate_t):
    NE, CAP = 8, 64
    with Stage(nc, "eg") as s:
        w = s.sb("w", [P, DC, NE])
        top = s.sb("top", [NE, 1])
        sums = s.sb("sums", [NE, 1])
        probs = s.sb("probs", [NE, N])
        left = s.sb("left", [NE, N])
        best = s.sb("best", [NE, CAP])
        logits = s.ps("logits", [NE, N])
        w_in, scored, cut, raised, chain = (s.sem(n) for n in ("w_in", "scored", "cut", "raised", "chain"))
        with nc.Block() as block:
            @block.sync
            def _(sp):
                sp.dma_start(w[:], a["L2_ffn_Wr"].rearrange("(k p) d -> p k d", p=P)).then_inc(w_in, 16)

            @block.tensor
            def _(pe):
                pe.wait_ge(w_in, 16)
                for n in range(2):
                    for k in range(DC):
                        last = pe.matmul(logits[:, n * D:(n + 1) * D], w[:, k, :], c.XLT[:, k, n * D:(n + 1) * D],
                                         start=k == 0, stop=k == DC - 1)
                last.then_inc(scored, 1)

            @block.scalar
            def _(act):
                act.wait_ge(cut, 1)
                act.activation(probs[:], logits[:], ACT.Exp, bias=top[:]).then_inc(raised, 1)

            @block.vector
            def _(dve):
                links = [0]

                def link(ins):
                    links[0] += 1
                    ins.then_inc(chain, 1)
                    dve.wait_ge(chain, links[0])

                dve.wait_ge(scored, 1)
                link(dve.tensor_reduce(top[:], logits[:], AX_X, ALU.max))
                dve.tensor_scalar(top[:], top[:], -1.0, None, ALU.mult).then_inc(cut, 1)
                dve.wait_ge(raised, 1)
                link(dve.tensor_reduce(sums[:], probs[:], AX_X, ALU.add))
                link(dve.reciprocal(sums[:], sums[:]))
                link(dve.tensor_scalar(probs[:], probs[:], sums[:], None, ALU.mult))
                for k in range(CAP // 8):
                    now = probs if k == 0 else left
                    link(dve.max(best[:, 8 * k:8 * k + 8], now[:]))
                    link(dve.match_replace(left[:], best[:, 8 * k:8 * k + 8], now[:], -1.0))
                link(dve.scalar_tensor_tensor(out=gate_t[:], in0=left[:], scalar=0.0, in1=probs[:],
                                              op0=ALU.is_lt, op1=ALU.mult))


def sage_update(nc, c, a, agg, degree):
    with Stage(nc, "l3u") as s:
        w = s.sb("w", [P, 2 * DC, D])
        bias = s.sb("bias", [P, D])
        rdeg = s.sb("rdeg", [P, NT])
        agg_t = s.sb("agg_t", [P, DC, N])
        turn = [s.ps(f"turn{k}") for k in range(2)]
        out = [s.ps(f"out{k}") for k in range(4)]
        w_in, mean, turned, taken, product, biased, clipped, chain = (s.sem(n) for n in (
            "w_in", "mean", "turned", "taken", "product", "biased", "clipped", "chain"))
        with nc.Block() as block:
            @block.sync
            def _(sp):
                sp.dma_start(w[:], a["L3_gnn_W"].rearrange("(k p) d -> p k d", p=P)).then_inc(w_in, 16)
                sp.dma_start(bias[:], a["L3_gnn_b"].partition_broadcast(P)).then_inc(w_in, 16)

            @block.tensor
            def _(pe):
                for t in range(NT):
                    pe.wait_ge(mean, t + 1)
                    if t >= 2:
                        pe.wait_ge(taken, t - 1)
                    for k in range(DC):
                        last = pe.transpose(turn[t % 2][:, k * P:(k + 1) * P], agg[:, t, k * P:(k + 1) * P], c.ident[:])
                    last.then_inc(turned, 1)
                pe.wait_ge(w_in, 32)
                for t in range(NT):
                    pe.wait_ge(taken, t + 1)
                    if t >= 4:
                        pe.wait_ge(biased, t - 3)
                    for k in range(2 * DC):
                        left = c.XLT if k < DC else agg_t
                        last = pe.matmul(out[t % 4][:], left[:, k % DC, t * P:(t + 1) * P], w[:, k, :],
                                         start=k == 0, stop=k == 2 * DC - 1)
                    last.then_inc(product, 1)

            @block.scalar
            def _(act):
                for t in range(NT):
                    act.wait_ge(turned, t + 1)
                    act.copy(agg_t[:, :, t * P:(t + 1) * P],
                             turn[t % 2][:, :].rearrange("p (k n) -> p k n", k=DC)).then_inc(taken, 1)

            @block.vector
            def _(dve):
                dve.tensor_scalar(rdeg[:], degree[:], 1.0, None, ALU.max).then_inc(chain, 1)
                dve.wait_ge(chain, 1)
                dve.reciprocal(rdeg[:], rdeg[:]).then_inc(chain, 1)
                dve.wait_ge(chain, 2)
                for t in range(NT):
                    dve.tensor_scalar(agg[:, t, :], agg[:, t, :], rdeg[:, t:t + 1], None, ALU.mult).then_inc(mean, 1)
                dve.wait_ge(w_in, 32)
                for t in range(NT):
                    dve.wait_ge(product, t + 1)
                    dve.wait_ge(turned, t + 1)
                    dve.tensor_tensor(agg[:, t, :], out[t % 4][:], bias[:], ALU.add).then_inc(biased, 1)
                    dve.wait_ge(biased, t + 1)
                    dve.scalar_tensor_tensor(out=c.X[:, t, :], in0=agg[:, t, :], scalar=0.0, in1=c.X[:, t, :],
                                             op0=ALU.max, op1=ALU.add).then_inc(clipped, 1)


def one_expert(nc, c, a):
    NE = 16
    with Stage(nc, "l3e") as s:
        wg = s.sb("wg", [P, DC, NE])
        bg = s.sb("bg", [P, NE])
        mean = s.sb("mean", [P, DC])
        mean_w = s.sb("mean_w", [P, DC, P])
        scores = s.sb("scores", [P, NE])
        top = s.sb("top", [P, 8])
        top_at = s.sb("top_at", [P, 8], U32)
        low = s.sb("low", [P, 1])
        raised_s = s.sb("raised_s", [P, NE])
        sums = s.sb("sums", [P, 1])
        gate = s.sb("gate", [P, 1])
        which = s.sb("which", [P, 1])
        line = s.sb("line", [P, DC])
        row_f = s.sb("row_f", [P, DC])
        row_i = s.sb("row_i", [P, DC], I32)
        which_i = s.sb("which_i", [P, 1], I32)
        w = s.sb("w", [P, DC, D])
        bias = s.sb("bias", [P, D])
        logits = s.ps("logits", [P, NE])
        out = [s.ps(f"out{k}") for k in range(4)]
        (w_in, base), = c.landings.take([DC + 1])
        g_in, spread, scored, cut, raised, picked, lined, product, biased, added, chain = (s.sem(n) for n in (
            "g_in", "spread", "scored", "cut", "raised", "picked", "lined", "product", "biased", "added",
            "chain"))
        with nc.Block() as block:
            @block.sync
            def _(sp):
                sp.dma_start(wg[:], a["L3_ffn_Wg"].rearrange("(k p) d -> p k d", p=P)).then_inc(g_in, 16)
                sp.dma_start(bg[:], a["L3_ffn_bg"].partition_broadcast(P)).then_inc(g_in, 16)

            @block.gpsimd
            def _(pool):
                pool.iota(line[:], [[P, DC]], base=0, channel_multiplier=1,
                          allow_small_or_imprecise_dtypes=True).then_inc(lined, 1)
                pool.wait_ge(picked, 1)
                for k in range(DC):
                    pool.indirect_dma_start(w[:, k, :], None, a["L3_ffn_We_rows"],
                                            bass.IndirectOffsetOnAxis(ap=row_i[:, k:k + 1], axis=0)).then_inc(w_in, 16)
                pool.indirect_dma_start(bias[:], None, a["L3_ffn_be"],
                                        bass.IndirectOffsetOnAxis(ap=which_i[:], axis=0)).then_inc(w_in, 16)

            @block.tensor
            def _(pe):
                pe.wait_ge(g_in, 32)
                pe.wait_ge(spread, 1)
                for k in range(DC):
                    last = pe.matmul(logits[:], mean_w[:, k, :], wg[:, k, :], start=k == 0, stop=k == DC - 1)
                last.then_inc(scored, 1)
                pe.wait_ge(w_in, base + 16 * (DC + 1))
                for t in range(NT):
                    if t >= 4:
                        pe.wait_ge(biased, t - 3)
                    for k in range(DC):
                        last = pe.matmul(out[t % 4][:], c.XLT[:, k, t * P:(t + 1) * P], w[:, k, :],
                                         start=k == 0, stop=k == DC - 1)
                    last.then_inc(product, 1)

            @block.scalar
            def _(act):
                act.wait_ge(cut, 1)
                act.activation(raised_s[:], scores[:], ACT.Exp, bias=low[:]).then_inc(raised, 1)

            @block.vector
            def _(dve):
                links = [0]

                def link(ins):
                    links[0] += 1
                    ins.then_inc(chain, 1)
                    dve.wait_ge(chain, links[0])

                link(dve.tensor_reduce(mean[:], c.XLT[:], AX_X, ALU.add))
                link(dve.tensor_scalar(mean[:], mean[:], 1.0 / N, None, ALU.mult))
                dve.tensor_copy(mean_w[:], mean[:].unsqueeze(2).to_broadcast([P, DC, P])).then_inc(spread, 1)
                dve.wait_ge(scored, 1)
                link(dve.tensor_tensor(scores[:], logits[:], bg[:], ALU.add))
                link(dve.max(top[:], scores[:]))
                dve.tensor_scalar(low[:], top[:, 0:1], -1.0, None, ALU.mult).then_inc(cut, 1)
                link(dve.max_index(top_at[:], top[:], scores[:]))
                link(dve.tensor_copy(which[:], top_at[:, 0:1]))
                dve.wait_ge(lined, 1)
                dve.tensor_copy(which_i[:], which[:])
                link(dve.tensor_scalar(which[:], which[:], float(D), None, ALU.mult))
                link(dve.tensor_scalar(row_f[:], line[:], which[:], None, ALU.add))
                dve.tensor_copy(row_i[:], row_f[:]).then_inc(picked, 1)
                dve.wait_ge(raised, 1)
                link(dve.tensor_reduce(sums[:], raised_s[:], AX_X, ALU.add))
                link(dve.reciprocal(gate[:], sums[:]))
                dve.wait_ge(w_in, base + 16 * (DC + 1))
                for t in range(NT):
                    dve.wait_ge(product, t + 1)
                    dve.tensor_tensor(c.XL[:, t, :], out[t % 4][:], bias[:], ALU.add).then_inc(biased, 1)
                    dve.wait_ge(biased, t + 1)
                    dve.scalar_tensor_tensor(out=c.X[:, t, :], in0=c.XL[:, t, :], scalar=gate[:], in1=c.X[:, t, :],
                                             op0=ALU.mult, op1=ALU.add).then_inc(added, 1)



HEADS, NKEYS, TOPK = 8, 256, 8
BANKS = 4


def memory_queries(nc, c, a, q):
    with Stage(nc, "m0q") as s:
        w = s.sb("w", [P, DC, HEADS * P])
        bias = s.sb("bias", [P, HEADS])
        out = [s.ps(f"out{k}") for k in range(4)]
        w_in, product, biased = s.sem("w_in"), s.sem("product"), s.sem("biased")
        work = [(h, n) for h in range(HEADS) for n in range(2)]
        with nc.Block() as block:
            @block.sync
            def _(sp):
                sp.dma_start(w[:], a["L0_ffn_Wq"].rearrange("(k p) d -> p k d", p=P)).then_inc(w_in, 16)
                sp.dma_start(bias[:], a["L0_ffn_bq_t"]).then_inc(w_in, 16)

            @block.tensor
            def _(pe):
                pe.wait_ge(w_in, 32)
                for i, (h, n) in enumerate(work):
                    if i >= 4:
                        pe.wait_ge(biased, i - 3)
                    for k in range(DC):
                        last = pe.matmul(out[i % 4][:], w[:, k, h * P:(h + 1) * P], c.XLT[:, k, n * D:(n + 1) * D],
                                         start=k == 0, stop=k == DC - 1)
                    last.then_inc(product, 1)

            @block.scalar
            def _(act):
                act.wait_ge(w_in, 32)
                for i, (h, n) in enumerate(work):
                    act.wait_ge(product, i + 1)
                    act.activation(q[:, h, n * D:(n + 1) * D], out[i % 4][:], ACT.Identity,
                                   bias=bias[:, h:h + 1]).then_inc(biased, 1)


def memory_lookup(nc, c, a, q):
    with Stage(nc, "m0") as s:
        keys = s.sb("keys", [P, HEADS, NKEYS])
        query = [s.sb(f"query{k}", [P, P]) for k in range(BANKS)]
        vals = s.sb("best", [P, HEADS, 2, TOPK])
        vals_at = s.sb("best_at", [P, HEADS, 2, TOPK], U32)
        key_no = s.sb("key_no", [P, HEADS, 2, TOPK])
        pairs = s.sb("pairs", [P, HEADS, TOPK, TOPK])
        score = s.sb("score", [P, HEADS, TOPK])
        pair_at = s.sb("pair_at", [P, HEADS, TOPK], U32)
        half_at = s.sb("half_at", [P, 2, HEADS * TOPK], U32)
        half_no = s.sb("half_no", [P, 2, HEADS * TOPK])
        same = s.sb("same", [P, 2, HEADS * TOPK, TOPK])
        chosen = s.sb("chosen", [P, 2, HEADS * TOPK])
        memory = [s.sb(f"memory{u}", [P, HEADS * TOPK], I32) for u in range(2)]
        share = [s.sb(f"share{u}", [P, HEADS, TOPK]) for u in range(2)]
        norms = s.sb("norms", [P, HEADS])
        rows = [s.sb(f"rows{k}", [P, 2 * D]) for k in range(ROWS)]
        inner = [s.sb(f"inner{k}", [P, PART]) for k in range(ROWS // PART)]
        value = [s.sb(f"value{k}", [P, PART]) for k in range(ROWS // PART)]
        diag = [s.sb(f"diag{k}", [P, P]) for k in range(ROWS)]
        scores = [s.ps(f"scores{k}") for k in range(BANKS)]
        out = [s.ps(f"out{u}") for u in range(2)]
        keys_in, queried, scored, maxed, ranked = (s.sem(n) for n in ("keys_in", "queried", "scored", "maxed", "ranked"))
        steps, indexed, issued, shifted, raised = (s.sem(n) for n in ("steps", "indexed", "issued", "shifted", "raised"))
        dotted, valued, spread, used, added = (s.sem(n) for n in ("dotted", "valued", "spread", "used", "added"))
        waited, scattered, reloaded = s.sem("waited"), s.sem("scattered_ok"), s.sem("reloaded")
        scatter = Scatter(nc, c, s, 1, c.loose_d, c.by_dst, RD)
        landed = c.landings.take([NT * HEADS * TOPK // ROWS] * ROWS)
        STEPS = 15
        PAIRS = HEADS // 2
        PARTS = TOPK // PART

        def bank(h, k):
            return scores[h % BANKS // 2 * 2 + k][:, h % 2 * NKEYS:(h % 2 + 1) * NKEYS]

        def over_tiles(engine, tile, before=None):
            with engine.Fori(0, NT // 2 - 1) as i:
                for u in range(2):
                    tile(i * 2 + u, u, True)
            tile(NT - 2, 0, True)
            tile(NT - 1, 1, False)

        with nc.Block() as block:
            @block.sync
            def _(sp):
                sp.dma_start(keys[:], a["L0_ffn_keys_t"]).then_inc(keys_in, 16)
                sp.wait_ge(scattered, 1)
                sp.dma_start(c.rec_d[:], c.by_dst.rearrange("(p c) f -> p c f", p=P)).then_inc(reloaded, 16)
                sp.wait_ge(reloaded, 16)

            @block.scalar
            def _(act):
                def place_queries(T, p):
                    act.wait_ge(scored, T * PAIRS + p + 1)
                    for h in (2 * p, 2 * p + 1):
                        act.copy(query[h % BANKS][:], q[:, h, bass.ds(T * P, P)]).then_inc(queried, 1)

                def raise_scores(T):
                    act.wait_ge(shifted, T + 1)
                    act.activation(score[:], score[:], ACT.Exp).then_inc(raised, 1)

                def spread_values(T, h):
                    for part in range(PARTS):
                        done = (T * HEADS + h) * PARTS + part
                        act.wait_ge(valued, done + 1)
                        act.wait_ge(used, done * PART + PART)
                        for k in range(PART):
                            slot = h % 2 * TOPK + part * PART + k
                            act.mul(diag[slot][:], c.ident[:], value[slot // PART][:, k:k + 1]).then_inc(spread, 1)

                def tile(T, u, more):
                    for h in range(HEADS):
                        if more and h < PAIRS:
                            place_queries(T + 1, h)
                        spread_values(T, h)
                        if more and h == PAIRS + 1:
                            raise_scores(T + 1)

                for p in range(PAIRS):
                    place_queries(0, p)
                raise_scores(0)
                over_tiles(act, tile)

            @block.tensor
            def _(pe):
                def score_pair(T, p):
                    pe.wait_ge(queried, (T * PAIRS + p + 1) * 2)
                    pe.wait_ge(ranked, T * PAIRS + p + 1)
                    for h in (2 * p, 2 * p + 1):
                        for k in range(2):
                            half = slice(k * 64, (k + 1) * 64)
                            last = pe.matmul(bank(h, k), query[h % BANKS][half, :],
                                             keys[half, h, :], start=True, stop=True)
                    last.then_inc(scored, 1)

                def sum_up(T, u, h):
                    if h == 0:
                        pe.wait_ge(added, T + 1)
                    for k in range(TOPK):
                        pe.wait_ge(spread, ROWS + (T * HEADS + h) * TOPK + k + 1)
                        slot = h % 2 * TOPK + k
                        pe.matmul(out[u][:], diag[slot][:], rows[slot][:, D:2 * D],
                                  start=h == 0 and k == 0, stop=h == HEADS - 1 and k == TOPK - 1).then_inc(used, 1)

                def tile(T, u, more):
                    for h in range(HEADS):
                        if more and h < PAIRS:
                            score_pair(T + 1, h)
                        sum_up(T, u, h)

                pe.wait_ge(keys_in, 16)
                for p in range(PAIRS):
                    score_pair(0, p)
                over_tiles(pe, tile)

            @block.gpsimd
            def _(pool):
                def tile(T, u, more):
                    pool.wait_ge(indexed, T + 1)
                    pool.sem_inc(issued, 1)
                    scatter.copy(pool, T, u)
                    for h in range(HEADS):
                        scatter.send(pool, T, u, range(GROUP)[3 * h:3 * h + 3])
                        for first in range(0, TOPK, FREED):
                            pool.wait_ge(used, (T * HEADS + h) * TOPK + first + FREED)
                            pool.sem_inc(issued, 1)
                            for k in range(first, first + FREED):
                                slot = h % 2 * TOPK + k
                                pool.indirect_dma_start(
                                    rows[slot][:], None, a["L0_ffn_w_rows"],
                                    bass.IndirectOffsetOnAxis(ap=memory[u][:, h * TOPK + k:h * TOPK + k + 1], axis=0))\
                                    .then_inc(landed[slot][0], 16)

                over_tiles(pool, tile)
                scatter.finish(pool, scattered)

            @block.vector
            def _(dve):
                dve.sem_inc(scored, 2)
                dve.sem_inc(ranked, 2)
                dve.sem_inc(spread, ROWS)
                dve.sem_inc(used, ROWS)
                dve.sem_inc(added, 2)

                def rank(T, p):
                    heads = [(h, k) for h in (2 * p, 2 * p + 1) for k in range(2)]
                    dve.wait_ge(scored, 2 + T * PAIRS + p + 1)
                    dve.sem_inc(waited, 1)
                    for h, k in heads:
                        last = dve.max(vals[:, h, k, :], bank(h, k))
                    last.then_inc(maxed, 1)
                    dve.wait_ge(maxed, T * PAIRS + p + 1)
                    dve.sem_inc(waited, 1)
                    for h, k in heads:
                        last = dve.max_index(vals_at[:, h, k, :], vals[:, h, k, :], bank(h, k))
                    last.then_inc(ranked, 1)

                def choose(T, u):
                    done = [0]

                    def link(ins):
                        done[0] += 1
                        ins.then_inc(steps, 1)
                        dve.wait_ge(steps, T * STEPS + done[0])

                    full = [P, HEADS, TOPK, TOPK]
                    dve.wait_ge(ranked, 2 + (T + 1) * PAIRS)
                    dve.tensor_copy(key_no[:], vals_at[:])
                    link(dve.tensor_tensor(pairs[:], vals[:, :, 0, :].unsqueeze(3).to_broadcast(full),
                                           vals[:, :, 1, :].unsqueeze(2).to_broadcast(full), ALU.add))
                    dve.sem_inc(waited, 1)
                    for h in range(HEADS):
                        last = dve.max(score[:, h, :], pairs[:, h].rearrange("p a b -> p (a b)"))
                    link(last)
                    dve.sem_inc(waited, 1)
                    for h in range(HEADS):
                        last = dve.max_index(pair_at[:, h, :], score[:, h, :], pairs[:, h].rearrange("p a b -> p (a b)"))
                    link(last)
                    at = pair_at[:].rearrange("p h k -> p (h k)")
                    dve.tensor_scalar(half_at[:, 0, :], at, 3, None, ALU.logical_shift_right)
                    link(dve.tensor_scalar(half_at[:, 1, :], at, TOPK - 1, None, ALU.bitwise_and))
                    link(dve.tensor_copy(norms[:], score[:, :, 0]))
                    dve.tensor_tensor(score[:], score[:], norms[:].unsqueeze(2).to_broadcast([P, HEADS, TOPK]),
                                      ALU.subtract).then_inc(shifted, 1)
                    link(dve.tensor_copy(half_no[:], half_at[:]))
                    wide = [P, 2 * HEADS * TOPK, TOPK]
                    link(dve.tensor_tensor(same[:].rearrange("p a n m -> p (a n) m"),
                                           c.iota[:, 0:TOPK].unsqueeze(1).to_broadcast(wide),
                                           half_no[:].rearrange("p a n -> p (a n)").unsqueeze(2).to_broadcast(wide),
                                           ALU.is_equal))
                    for k in range(2):
                        part = same[:, k].rearrange("p (h n) m -> p h n m", h=HEADS)
                        last = dve.tensor_tensor(part, part, key_no[:, :, k, :].unsqueeze(2).to_broadcast(full), ALU.mult)
                    link(last)
                    link(dve.tensor_reduce(chosen[:], same[:], AX_X, ALU.add))
                    dve.scalar_tensor_tensor(out=memory[u][:], in0=chosen[:, 0, :], scalar=float(NKEYS),
                                             in1=chosen[:, 1, :], op0=ALU.mult, op1=ALU.add).then_inc(indexed, 1)
                    for _ in range(STEPS - 4 - done[0]):
                        dve.sem_inc(steps, 1)
                        done[0] += 1

                def softmax(T, u):
                    def link(n, ins):
                        ins.then_inc(steps, 1)
                        dve.wait_ge(steps, T * STEPS + n)

                    dve.wait_ge(raised, T + 1)
                    link(STEPS - 3, dve.tensor_reduce(norms[:], score[:], AX_X, ALU.add))
                    link(STEPS - 2, dve.reciprocal(norms[:], norms[:]))
                    link(STEPS - 1, dve.tensor_tensor(share[u][:], score[:],
                                                      norms[:].unsqueeze(2).to_broadcast([P, HEADS, TOPK]), ALU.mult))
                    dve.sem_inc(steps, 1)

                def weigh(T, u, h):
                    for part in range(PARTS):
                        done = (T * HEADS + h) * PARTS + part
                        first = h % 2 * TOPK + part * PART
                        place = first // PART
                        for k in range(PART):
                            dve.wait_ge(landed[first + k][0], landed[first + k][1] + (T * (HEADS // 2) + h // 2 + 1) * 16)
                            last = dve.scalar_tensor_tensor(out=rows[first + k][:, 0:D], in0=c.XL[:, bass.ds(T, 1), :]
                                                            .rearrange("p a d -> p (a d)"), scalar=1.0,
                                                            in1=rows[first + k][:, 0:D], op0=ALU.mult, op1=ALU.mult,
                                                            accum_out=inner[place][:, k:k + 1])
                        last.then_inc(dotted, 1)
                        dve.wait_ge(dotted, done + 1)
                        dve.wait_ge(spread, done * PART + PART)
                        dve.scalar_tensor_tensor(out=value[place][:], in0=inner[place][:], scalar=0.0,
                                                 in1=share[u][:, h, part * PART:(part + 1) * PART],
                                                 op0=ALU.max, op1=ALU.mult).then_inc(valued, 1)

                def add(T, u):
                    dve.wait_ge(used, ROWS + (T + 1) * HEADS * TOPK)
                    there = c.X[:, bass.ds(T, 1), :].rearrange("p a d -> p (a d)")
                    dve.tensor_tensor(there, there, out[u][:], ALU.add).then_inc(added, 1)

                def tile(T, u, more):
                    for h in range(HEADS):
                        if more and 1 <= h <= PAIRS:
                            rank(T + 1, h - 1)
                        if more and h == PAIRS + 1:
                            choose(T + 1, 1 - u)
                        weigh(T, u, h)
                        if more and h == PAIRS + 1:
                            softmax(T + 1, 1 - u)
                    add(T, u)

                for p in range(PAIRS):
                    rank(0, p)
                choose(0, 0)
                softmax(0, 0)
                over_tiles(dve, tile)



LOG2 = math.log(2.0)
Y0 = 1.0 / math.sqrt(4.0 * math.pi)
Y1 = math.sqrt(3.0 / (4.0 * math.pi))
QUAD = 4
BODY = 16
MADE = 4
AHEAD = 3


def vector_node_rows(nc, c, a):
    with Stage(nc, "t0") as s:
        w = s.sb("w", [P, 2, P])
        row = [s.sb(f"row{k}", [P, D]) for k in range(4)]
        out = [s.ps(f"out{k}") for k in range(4)]
        w_in, product, scaled = s.sem("w_in"), s.sem("product"), s.sem("scaled")
        stored = [s.sem(f"stored{k}") for k in range(4)]
        with nc.Block() as block:
            @block.sync
            def _(sp):
                sp.dma_start(w[:, 0, :], a["L2_gnn_W_in2f_s"]).then_inc(w_in, 16)
                sp.dma_start(w[:, 1, :], a["L2_gnn_W_in2f_v"]).then_inc(w_in, 16)
                for t in range(NT):
                    sp.wait_ge(scaled, t + 1)
                    sp.dma_start(c.rows[t * P:(t + 1) * P, :], row[t % 4][:]).then_inc(stored[t % 4], 16)
                for k in range(4):
                    sp.wait_ge(stored[k], 16 * (NT // 4))

            @block.tensor
            def _(pe):
                pe.wait_ge(w_in, 32)
                for t in range(NT):
                    if t >= 4:
                        pe.wait_ge(scaled, t - 3)
                    for k in range(DC):
                        last = pe.matmul(out[t % 4][:, k * P:(k + 1) * P], c.XLT[:, k, t * P:(t + 1) * P],
                                         w[:, min(k, 1), :], start=True, stop=True)
                    last.then_inc(product, 1)

            @block.scalar
            def _(act):
                for t in range(NT):
                    act.wait_ge(product, t + 1)
                    if t >= 4:
                        act.wait_ge(stored[t % 4], 16 * (t // 4))
                    act.mul(row[t % 4][:], out[t % 4][:], 1.0 / math.sqrt(P)).then_inc(scaled, 1)


def vector_messages(nc, c, a, total):
    Q, SA, SB, VA, VB = (k * P for k in (0, 1, 2, 3, 6))
    QUADS = BODY // QUAD
    with Stage(nc, "t2") as s:
        wf1 = s.sb("wf1", [RBF, P])
        bf1 = s.sb("bf1", [P, 1])
        wf2 = s.sb("wf2", [P, D])
        bf2 = s.sb("bf2", [1, D])
        bf2_part = s.sb("bf2_part", [1, 3, D], BF16)
        bf2_rows = s.sb("bf2_rows", [3, D], BF16)
        ones = s.sb("ones", [3, P], BF16)
        attr = [s.sb(f"attr{k}", [P, QUAD, RBF]) for k in range(2)]
        attr_t = s.sb("attr_t", [RBF, D])
        size = [s.sb(f"size{b}", [P, D]) for b in range(QUADS)]
        above = [s.sb(f"above{b}", [P, D]) for b in range(QUADS)]
        hid = [s.sb(f"hid{b}", [P, D]) for b in range(QUADS)]
        at = [s.sb(f"at{h}", [P, QUAD], I32) for h in range(2)]
        rows = [s.sb(f"rows{j}", [P, D]) for j in range(RING)]
        hot = [s.sb(f"hot{j}", [P, P]) for j in range(MADE)]
        filt = [s.sb(f"filt{j}", [P, P]) for j in range(MADE)]
        along = [s.sb(f"along{j}", [P, P]) for j in range(MADE)]
        mess = [s.sb(f"mess{j}", [P, 9 * P]) for j in range(MADE)]
        turn, pre = s.ps("turn"), s.ps("pre")
        fps = [s.ps(f"fps{j}") for j in range(2)]
        part = [s.ps(f"part{j}", [P, 2 * D]) for j in range(2)]
        w_in, attr_ok, turned, attr_t_ok, pre_ok, sized, logged, aboved, hid_ok = (s.sem(n) for n in (
            "w_in", "attr_ok", "turned", "attr_t_ok", "pre_ok", "sized", "logged", "aboved", "hid_ok"))
        placed, issued, marked, filtered, copied = (s.sem(n) for n in (
            "placed", "issued", "marked", "filtered", "copied"))
        landed = c.landings.take([CH // RING] * RING)
        dots, mixed, scaled, outer, vectored, begun, summed, added, raised, waited = (s.sem(n) for n in (
            "dots", "mixed", "scaled", "outer", "vectored", "begun", "summed", "added", "raised", "waited"))
        split, parted = s.sem("split"), s.sem("parted")
        flat = total[:, :, :].rearrange("p t d -> p (t d)")

        def rows_in(i, j):
            return landed[j % RING][1] + (i * (BODY // RING) + j // RING + 1) * 16

        def over_bodies(engine, body):
            with engine.Fori(0, CH // BODY - 1) as i:
                body(i, True)
            body(CH // BODY - 1, False)

        with nc.Block() as block:
            @block.sync
            def _(sp):
                sp.dma_start(wf1[:], a["L2_gnn_Wf1"]).then_inc(w_in, 16)
                sp.dma_start(bf1[:], a["L2_gnn_bf1_t"]).then_inc(w_in, 16)
                sp.dma_start(wf2[:], a["L2_gnn_Wf2_t"]).then_inc(w_in, 16)
                sp.dma_start(bf2[:], a["L2_gnn_bf2_t"].partition_broadcast(1)).then_inc(w_in, 16)
                sp.wait_ge(split, 6)
                for k in range(3):
                    sp.dma_start(bf2_rows[k:k + 1, :], bf2_part[:, k, :]).then_inc(parted, 16)
                sp.wait_ge(parted, 48)

            @block.gpsimd
            def _(pool):
                def indices(g, h):
                    pool.wait_ge(summed, g * QUAD + 1)
                    pool.tensor_copy(at[h][:], c.rec_s[:, bass.ds(g * QUAD, QUAD), S_OTHER].bitcast(I32))\
                        .then_inc(placed, 1)

                def gather(g, h, k):
                    pool.wait_ge(placed, g + 1)
                    pool.wait_ge(summed, g * QUAD + k + 1)
                    pool.sem_inc(issued, 1)
                    pool.indirect_dma_start(rows[h * QUAD + k][:], None, c.rows[0:N, :],
                                            bass.IndirectOffsetOnAxis(ap=at[h][:, k:k + 1], axis=0))\
                        .then_inc(landed[h * QUAD + k][0], 16)

                def vectors(i, j):
                    k, slot = j % MADE, j % RING
                    pool.wait_ge(copied, i * BODY + j + 1)
                    pool.wait_ge(landed[slot][0], rows_in(i, j))
                    pool.tensor_tensor(mess[k][:, VB:VB + 3 * P].rearrange("p (a f) -> p a f", a=3),
                                       rows[slot][:, P:4 * P].rearrange("p (a f) -> p a f", a=3),
                                       filt[k][:].unsqueeze(1).to_broadcast([P, 3, P]),
                                       ALU.mult).then_inc(vectored, 1)

                def body(i, more):
                    for j in range(BODY):
                        b = j // QUAD + 1
                        if more or b < QUADS:
                            if j % QUAD == 0:
                                indices(i * QUADS + b, b % 2)
                            gather(i * QUADS + b, b % 2, j % QUAD)
                        vectors(i, j)

                indices(0, 0)
                for k in range(QUAD):
                    gather(0, 0, k)
                over_bodies(pool, body)

            @block.scalar
            def _(act):
                def attributes(g, b):
                    act.wait_ge(turned, g + 1)
                    act.sem_inc(waited, 1)
                    act.copy(attr[b % 2][:], c.rec_s[:, bass.ds(g * QUAD, QUAD), S_RBF:S_RBF + RBF]).then_inc(attr_ok, 1)

                def attributes_turned(g):
                    act.wait_ge(turned, 2 + g + 1)
                    act.copy(attr_t[:], turn[0:RBF, :]).then_inc(attr_t_ok, 1)

                def hidden(g, b):
                    act.wait_ge(pre_ok, g + 1)
                    act.wait_ge(hid_ok, g + 1)
                    act.activation(size[b][:], pre[:], ACT.Abs, bias=bf1[:]).then_inc(sized, 1)
                    act.activation(above[b][:], pre[:], ACT.Relu, bias=bf1[:]).then_inc(aboved, 1)
                    act.wait_ge(sized, g + 1)
                    act.activation(size[b][:], size[b][:], ACT.Exp, scale=-1.0).then_inc(raised, 1)

                def logarithm(g, b):
                    act.wait_ge(raised, g + 1)
                    act.activation(size[b][:], size[b][:], ACT.Ln, bias=c.ones[:, 0:1]).then_inc(logged, 1)

                def first_product(i, j):
                    slot = j % RING
                    act.wait_ge(outer, i * BODY + j + 1)
                    act.wait_ge(landed[slot][0], rows_in(i, j))
                    act.sem_inc(waited, 1)
                    act.mul(along[j % MADE][:], rows[slot][:, P:2 * P],
                            c.rec_s[:, bass.ds(i * BODY + j, 1), S_U:S_U + 1].rearrange("p a b -> p (a b)")).then_inc(begun, 1)

                def scale(q, j):
                    k = j % MADE
                    act.wait_ge(mixed, q + 1)
                    act.sem_inc(waited, 1)
                    for i in range(3):
                        last = act.mul(mess[k][:, VA + i * P:VA + (i + 1) * P], mess[k][:, Q:Q + P],
                                       c.rec_s[:, bass.ds(q, 1), S_U + i:S_U + i + 1].rearrange("p a b -> p (a b)"))
                    last.then_inc(scaled, 1)

                def body(i, more):
                    for j in range(BODY):
                        if j < BODY - 1:
                            first_product(i, j + 1)
                        elif more:
                            first_product(i + 1, 0)
                        scale(i * BODY + j, j)
                        if more and j < AHEAD * QUADS:
                            b = j // AHEAD
                            g = (i + 1) * QUADS + b
                            if j % AHEAD == 0:
                                attributes(g, b)
                            elif j % AHEAD == 1:
                                attributes_turned(g)
                            else:
                                hidden(g, b)
                        elif more:
                            b = j - AHEAD * QUADS
                            logarithm((i + 1) * QUADS + b, b)

                for b in range(QUADS):
                    attributes(b, b)
                    attributes_turned(b)
                    hidden(b, b)
                for b in range(QUADS):
                    logarithm(b, b)
                first_product(0, 0)
                over_bodies(act, body)

            @block.tensor
            def _(pe):
                def turn_attributes(g, b, first=False):
                    pe.wait_ge(attr_ok, g + 1)
                    if not first:
                        pe.wait_ge(attr_t_ok, g)
                    for j in range(QUAD):
                        last = pe.transpose(turn[0:RBF, j * P:(j + 1) * P], attr[b % 2][:, j, :], c.ident[:])
                    last.then_inc(turned, 1)

                def hidden(g):
                    pe.wait_ge(attr_t_ok, g + 1)
                    pe.wait_ge(aboved, g + 1)
                    pe.matmul(pre[:], wf1[:], attr_t[:], start=True, stop=True).then_inc(pre_ok, 1)

                def sum_up(q, j):
                    k = j % MADE
                    pe.wait_ge(marked, q + 1)
                    pe.wait_ge(added, q + 1)
                    pe.wait_ge(outer, MADE + q + 1)
                    pe.wait_ge(vectored, q + 1)
                    pe.wait_ge(scaled, q + 1)
                    pe.matmul(part[j % 2][:, 0:D], hot[k][:], mess[k][:, P:P + D], start=True, stop=True)
                    pe.matmul(part[j % 2][:, D:2 * D], hot[k][:], mess[k][:, P + D:P + 2 * D], start=True, stop=True)\
                        .then_inc(summed, 1)

                def filter_at(i, j):
                    if j % QUAD == 0:
                        pe.wait_ge(hid_ok, QUADS + i * QUADS + j // QUAD + 1)
                    pe.wait_ge(outer, MADE - 2 + i * BODY + j + 1)
                    pe.matmul(fps[j % 2][:], hid[j // QUAD][:, j % QUAD * P:(j % QUAD + 1) * P], wf2[:],
                              start=True, stop=False)
                    pe.matmul(fps[j % 2][:], ones[:], bf2_rows[:], start=False, stop=True).then_inc(filtered, 1)

                def body(i, more):
                    for j in range(BODY):
                        g, b = (i + 1) * QUADS + j // AHEAD, j // AHEAD
                        if more and b < QUADS and j % AHEAD == 1:
                            turn_attributes(g, b)
                        if more and b < QUADS and j % AHEAD == 2:
                            hidden(g)
                        if j < BODY - 1:
                            filter_at(i, j + 1)
                        elif more:
                            filter_at(i + 1, 0)
                        sum_up(i * BODY + j, j)

                pe.wait_ge(w_in, 64)
                pe.wait_ge(parted, 48)
                for b in range(QUADS):
                    turn_attributes(b, b, first=b == 0)
                    hidden(b)
                filter_at(0, 0)
                over_bodies(pe, body)

            @block.vector
            def _(dve):
                dve.memset(flat, 0.0).then_inc(added, 2)
                dve.sem_inc(summed, RING)
                dve.sem_inc(outer, MADE)
                dve.sem_inc(turned, 2)
                dve.sem_inc(aboved, 1)
                dve.sem_inc(hid_ok, QUADS)

                def hidden(g, b):
                    dve.wait_ge(logged, g + 1)
                    dve.wait_ge(aboved, g + 2)
                    dve.scalar_tensor_tensor(out=hid[b][:], in0=above[b][:], scalar=-LOG2, in1=size[b][:],
                                             op0=ALU.add, op1=ALU.add).then_inc(hid_ok, 1)

                def one_hot(i, j):
                    q, k = i * BODY + j, j % MADE
                    dve.wait_ge(summed, RING - MADE + q + 1)
                    dve.tensor_scalar(hot[k][:], c.iota[:, 0:P],
                                      c.rec_s[:, bass.ds(q, 1), S_LO:S_LO + 1].rearrange("p a b -> p (a b)"),
                                      c.rec_s[:, bass.ds(q, 1), S_W:S_W + 1].rearrange("p a b -> p (a b)"),
                                      ALU.is_equal, ALU.mult).then_inc(marked, 1)

                def message(i, j, more):
                    q, k, slot = i * BODY + j, j % MADE, j % RING
                    node, m = rows[slot], mess[k]

                    def dot(d):
                        dve.scalar_tensor_tensor(out=along[k][:], in0=node[:, (d + 1) * P:(d + 2) * P],
                                                 scalar=c.rec_s[:, bass.ds(q, 1), S_U + d:S_U + d + 1].rearrange("p a b -> p (a b)"),
                                                 in1=along[k][:], op0=ALU.mult, op1=ALU.add).then_inc(dots, 1)

                    dve.wait_ge(filtered, q + 1)
                    dve.tensor_copy(filt[k][:], fps[j % 2][:, 3 * P:4 * P]).then_inc(copied, 1)
                    dve.wait_ge(landed[slot][0], rows_in(i, j))
                    dve.wait_ge(begun, q + 1)
                    dot(1)
                    dve.tensor_tensor(m[:, Q:Q + 2 * P].rearrange("p (a f) -> p a f", a=2),
                                      fps[j % 2][:, 0:2 * P].rearrange("p (a f) -> p a f", a=2),
                                      node[:, 0:P].unsqueeze(1).to_broadcast([P, 2, P]), ALU.mult).then_inc(mixed, 1)
                    dve.wait_ge(dots, q * 2 + 1)
                    dot(2)
                    if more:
                        one_hot(i, j + 1)
                    dve.wait_ge(dots, q * 2 + 2)
                    dve.tensor_tensor(m[:, SB:SB + P], along[k][:], fps[j % 2][:, 2 * P:3 * P], ALU.mult).then_inc(outer, 1)

                def add(i, j, tiles):
                    q, tile = i * BODY + j, tiles[j % KNOWN]
                    dve.wait_ge(summed, RING + q + 1)
                    dve.wait_ge(added, 2 + q)
                    there = flat[:, bass.ds(tile * (2 * D), 2 * D)]
                    dve.tensor_tensor(there, there, part[j % 2][:], ALU.add).then_inc(added, 1)

                def body(i, more):
                    for j in range(BODY):
                        if j < BODY - 1:
                            message(i, j + 1, more or j < BODY - 2)
                        elif more:
                            message(i + 1, 0, True)
                        if j % KNOWN == 0:
                            tiles = tiles_of(nc, c, dve, 0, i * BODY + j)
                        add(i, j, tiles)
                        if more and j >= AHEAD * QUADS:
                            b = j - AHEAD * QUADS
                            hidden((i + 1) * QUADS + b, b)

                dve.memset(ones[:], 1.0).then_inc(split, 1)
                dve.wait_ge(w_in, 64)
                for k in range(3):
                    dve.tensor_copy(bf2_part[:, k, :], bf2[:]).then_inc(split, 1)
                    if k < 2:
                        dve.wait_ge(split, 1 + 2 * k + 1)
                        dve.tensor_tensor(bf2[:], bf2[:], bf2_part[:, k, :], ALU.subtract).then_inc(split, 1)
                        dve.wait_ge(split, 1 + 2 * k + 2)
                for b in range(QUADS):
                    hidden(b, b)
                one_hot(0, 0)
                message(0, 0, True)
                over_bodies(dve, body)


def vector_update(nc, c, a, total):
    with Stage(nc, "t3") as s:
        w1 = s.sb("w1", [P, 2, 2, P])
        w2 = s.sb("w2", [P, 2, P])
        sums_t = s.sb("sums_t", [P, 8, N])
        size = s.sb("size", [P, N])
        mid = s.sb("mid", [P, 4, N])
        turn = [s.ps(f"turn{k}") for k in range(2)]
        first = [s.ps(f"first{k}") for k in range(2)]
        second = [s.ps(f"second{k}") for k in range(2)]
        w_in, w_ok, turned, taken, one, copied, sized, clipped, raised, logged, mid_ok, two, added, chain = (
            s.sem(n) for n in ("w_in", "w_ok", "turned", "taken", "one", "copied", "sized", "clipped", "raised",
                               "logged", "mid_ok", "two", "added", "chain"))
        kinds = [(0, 1)] + [(2 + i, 5 + i) for i in range(3)]
        scales = [(Y0 / 16, Y1 / math.sqrt(3.0) / 16), (Y1 / 16, Y0 / 16)]
        work = [(o, n) for o in range(4) for n in range(2)]
        with nc.Block() as block:
            @block.sync
            def _(sp):
                sp.dma_start(w1[:, 0], a["L2_gnn_W1_s_t"]).then_inc(w_in, 16)
                sp.dma_start(w1[:, 1], a["L2_gnn_W1_v_t"]).then_inc(w_in, 16)
                sp.dma_start(w2[:, 0], a["L2_gnn_W2_s"]).then_inc(w_in, 16)
                sp.dma_start(w2[:, 1], a["L2_gnn_W2_v"]).then_inc(w_in, 16)

            @block.tensor
            def _(pe):
                for i in range(NT * 2):
                    if i >= 2:
                        pe.wait_ge(taken, i - 1)
                    for k in range(4):
                        col = (i % 2 * 4 + k) * P
                        last = pe.transpose(turn[i % 2][:, k * P:(k + 1) * P], total[:, i // 2, col:col + P], c.ident[:])
                    last.then_inc(turned, 1)
                pe.wait_ge(w_ok, 6)
                pe.wait_ge(taken, NT * 2)
                for i, (o, n) in enumerate(work):
                    if i >= 2:
                        pe.wait_ge(copied, i - 1)
                    for k in range(2):
                        last = pe.matmul(first[i % 2][:], w1[:, min(o, 1), k, :],
                                         sums_t[:, kinds[o][k], n * D:(n + 1) * D], start=k == 0, stop=k == 1)
                    last.then_inc(one, 1)
                pe.wait_ge(copied, len(work))
                pe.wait_ge(mid_ok, 1)
                for t in range(NT):
                    if t >= 2:
                        pe.wait_ge(added, 2 * (t - 1))
                    for o in range(4):
                        last = pe.matmul(second[t % 2][:, o * P:(o + 1) * P], mid[:, o, t * P:(t + 1) * P],
                                         w2[:, min(o, 1), :], start=True, stop=True)
                    last.then_inc(two, 1)

            @block.scalar
            def _(act):
                act.wait_ge(w_in, 64)
                for o in range(2):
                    for k in range(2):
                        act.mul(w1[:, o, k, :], w1[:, o, k, :], scales[o][k]).then_inc(w_ok, 1)
                    act.mul(w2[:, o, :], w2[:, o, :], 1.0 / math.sqrt(P)).then_inc(w_ok, 1)
                for i in range(NT * 2):
                    act.wait_ge(turned, i + 1)
                    act.copy(sums_t[:, i % 2 * 4:i % 2 * 4 + 4, i // 2 * P:(i // 2 + 1) * P],
                             turn[i % 2][:].rearrange("p (k n) -> p k n", k=4)).then_inc(taken, 1)
                for i, (o, n) in enumerate(work):
                    act.wait_ge(one, i + 1)
                    act.copy(mid[:, o, n * D:(n + 1) * D], first[i % 2][:]).then_inc(copied, 1)
                    if i == 1:
                        act.wait_ge(copied, 2)
                        act.activation(size[:], mid[:, 0, :], ACT.Abs).then_inc(sized, 1)
                act.wait_ge(sized, 1)
                act.activation(size[:], size[:], ACT.Exp, scale=-1.0).then_inc(raised, 1)
                act.wait_ge(raised, 1)
                act.activation(size[:], size[:], ACT.Ln, bias=c.ones[:, 0:1]).then_inc(logged, 1)

            @block.vector
            def _(dve):
                dve.wait_ge(sized, 1)
                dve.tensor_scalar(mid[:, 0, :], mid[:, 0, :], 0.0, -LOG2, ALU.max, ALU.add).then_inc(clipped, 1)
                dve.wait_ge(clipped, 1)
                dve.wait_ge(logged, 1)
                dve.tensor_tensor(mid[:, 0, :], mid[:, 0, :], size[:], ALU.add).then_inc(mid_ok, 1)
                for t in range(NT):
                    dve.wait_ge(two, t + 1)
                    dve.tensor_tensor(c.X[:, t, 0:P], c.X[:, t, 0:P], second[t % 2][:, 0:P], ALU.add).then_inc(added, 1)
                    there = c.X[:, t, P:D].rearrange("p (d i) -> p d i", i=3)
                    dve.tensor_tensor(there, there, second[t % 2][:, P:D].rearrange("p (i d) -> p d i", i=3),
                                      ALU.add).then_inc(added, 1)



def layer0_messages(nc, c, a):
    with Stage(nc, "l0g") as s:
        c.XLT = s.sb("xlt", [P, DC, N])
        loose_s = s.sb("loose_s", [P, EP, RS])
        bin_edges(nc, c, a, loose_s)
        scatter = Scatter(nc, c, s, 0, loose_s, c.by_src, RS)
        norm(nc, c, "l0n", c.X, c.XL, turned=c.XLT, scatter=scatter)
        node_tables(nc, c, "l0t", a["L0_gnn_weight_t"], None, c.rows, scatter=scatter)
    aggregate(nc, c, "l0a", 0, c.rec_s, S_OTHER, S_LO, S_W, c.rows[0:N, :], c.X)


def layer0_memory(nc, c, a):
    with Stage(nc, "m0g") as s:
        q = s.sb("q", [P, HEADS, N])
        with Stage(nc, "m0h") as t:
            c.XLT = t.sb("xlt", [P, DC, N])
            norm(nc, c, "m0n", c.X, c.XL, turned=c.XLT)
            memory_queries(nc, c, a, q)
        memory_lookup(nc, c, a, q)


def layer1_messages(nc, c, a):
    with Stage(nc, "l1g") as s:
        c.XLT = s.sb("xlt", [P, DC, N])
        agg = s.sb("agg", [P, NT, D])
        degree = s.sb("degree", [P, NT])
        norm(nc, c, "l1n", c.X, c.XL, turned=c.XLT)
        node_tables(nc, c, "l1t", a["L1_gnn_W_rel"], a["L1_gnn_b_rel"], c.rows)
        aggregate(nc, c, "l1a", 1, c.rec_d, D_TYPED, D_LO, D_W, c.rows, agg, degree, clear=True)
        with Stage(nc, "l1h") as h:
            mixed = h.sb("mixed", [P, NT, D])
            relation_update(nc, c, a, agg, degree, mixed)
            norm(nc, c, "l1p", mixed, c.XL, affine=(a["L1_gnn_ln1_g"], a["L1_gnn_ln1_b"]), turned=c.XLT)
            relation_mlp(nc, c, a, c.XL, c.XLT, mixed)
            norm(nc, c, "l1q", mixed, c.XL, affine=(a["L1_gnn_ln2_g"], a["L1_gnn_ln2_b"]), residual=True)


def layer1_experts(nc, c, a):
    with Stage(nc, "l1f") as s:
        c.XLT = s.sb("xlt", [P, DC, N])
        gate_t = s.sb("gate_t", [8, N])
        norm(nc, c, "l1r", c.X, c.XL, turned=c.XLT)
        capacity_gates(nc, c, a, gate_t)
        expert_mix(nc, c, "l1x", gate_t, a["L1_ffn_w1_t"], a["L1_ffn_b1_t"], a["L1_ffn_w2_t"], a["L1_ffn_b2"])


def layer2_messages(nc, c, a):
    with Stage(nc, "tg") as s:
        total = s.sb("total", [P, NT, 2 * D])
        with Stage(nc, "th") as t:
            c.XLT = t.sb("xlt", [P, DC, N])
            norm(nc, c, "tn", c.X, c.XL, turned=c.XLT,
                 columns=[slice(0, P)] + [slice(P + i, D, 3) for i in range(3)])
            vector_node_rows(nc, c, a)
        vector_messages(nc, c, a, total)
        vector_update(nc, c, a, total)


def layer2_experts(nc, c, a):
    with Stage(nc, "l2f") as s:
        c.XLT = s.sb("xlt", [P, DC, N])
        gate_t = s.sb("gate_t", [8, N])
        norm(nc, c, "l2r", c.X, c.XL, turned=c.XLT)
        choice_gates(nc, c, a, gate_t)
        expert_mix(nc, c, "l2x", gate_t, a["L2_ffn_W1_t"], a["L2_ffn_b1_t"], a["L2_ffn_W2_t"], a["L2_ffn_b2"])


def layer3_messages(nc, c, a):
    with Stage(nc, "l3g") as s:
        c.XLT = s.sb("xlt", [P, DC, N])
        agg = s.sb("agg", [P, NT, D])
        degree = s.sb("degree", [P, NT])
        norm(nc, c, "l3n", c.X, c.XL, turned=c.XLT, rows=c.rows)
        aggregate(nc, c, "l3a", 1, c.rec_d, D_OTHER, D_LO, None, c.rows[0:N, :], agg, degree, clear=True)
        sage_update(nc, c, a, agg, degree)


def layer3_expert(nc, c, a):
    with Stage(nc, "l3f") as s:
        c.XLT = s.sb("xlt", [P, DC, N])
        norm(nc, c, "l3r", c.X, c.XL, turned=c.XLT)
        one_expert(nc, c, a)


LAYERS = [layer0_messages, layer0_memory, layer1_messages, layer1_experts, layer2_messages, layer2_experts,
          layer3_messages, layer3_expert]


def program(nc, a, out, layers=None):
    with ExitStack() as ctx:
        c = Shared(nc, ctx)
        make_constants(nc, c)
        for layer in layers or LAYERS:
            layer(nc, c, a)
        with nc.semaphore("out_stored") as stored, nc.Block() as block:
            @block.sync
            def _(sp):
                sp.dma_start(out.rearrange("(t p) d -> p t d", p=P), c.X[:, :, :]).then_inc(stored, 16)
                sp.wait_ge(stored, 16)


def layouts(i, np):
    o = {k: i[k] for k in ("x", "src", "dst", "edge_attr_20", "edge_attr_3", "edge_type_4", "edge_weight")}
    o["L0_gnn_weight_t"] = i["L0_gnn_weight"].T[None]
    o["L0_ffn_Wq"] = i["L0_ffn_Wq"]
    o["L0_ffn_bq_t"] = i["L0_ffn_bq"].reshape(HEADS, P).T
    o["L0_ffn_keys_t"] = i["L0_ffn_keys"].transpose(1, 3, 0, 2).reshape(P, HEADS, NKEYS)
    o["L0_ffn_w_rows"] = np.concatenate([i["L0_ffn_w_down"], i["L0_ffn_w_up"]], axis=1)
    for k in ("W_self", "b_self", "W_rel", "b_rel", "ln1_g", "ln1_b", "ln2_g", "ln2_b", "W_ffn1", "W_ffn2", "b_ffn2"):
        o[f"L1_gnn_{k}"] = i[f"L1_gnn_{k}"]
    o["L1_gnn_b_ffn1_t"] = i["L1_gnn_b_ffn1"].reshape(-1, P).T
    o["L1_ffn_gate_w_t"] = i["L1_ffn_gate_w"].T
    for name, w1, b1, w2 in (("L1_ffn", "w1", "b1", "w2"), ("L2_ffn", "W1", "b1", "W2")):
        o[f"{name}_{w1}_t"] = i[f"{name}_{w1}"].transpose(1, 0, 2).reshape(D, 256)
        o[f"{name}_{b1}_t"] = i[f"{name}_{b1}"].reshape(2, P).T
        o[f"{name}_{w2}_t"] = i[f"{name}_{w2}"].reshape(256, D)
        o[f"{name}_b2"] = i[f"{name}_b2"]
    def by_kind(w):
        w = w[..., :4 * P].reshape(*w.shape[:-1], 2, P, 2)
        return np.concatenate([w[..., 1, :, 0], w[..., 0, :, 0], w[..., 0, :, 1], w[..., 1, :, 1]], axis=-1)

    o["L2_gnn_Wf1"] = i["L2_gnn_Wf1"]
    o["L2_gnn_bf1_t"] = i["L2_gnn_bf1"][:, None]
    o["L2_gnn_Wf2_t"] = by_kind(i["L2_gnn_Wf2"])
    o["L2_gnn_bf2_t"] = by_kind(i["L2_gnn_bf2"])
    for k in ("W1_s", "W1_v"):
        o[f"L2_gnn_{k}_t"] = i[f"L2_gnn_{k}"].reshape(P, 2, P)
    for k in ("W_in2f_s", "W_in2f_v", "W2_s", "W2_v"):
        o[f"L2_gnn_{k}"] = i[f"L2_gnn_{k}"]
    for k in ("L2_ffn_Wr", "L3_gnn_W", "L3_gnn_b", "L3_ffn_Wg", "L3_ffn_bg", "L3_ffn_be"):
        o[k] = i[k]
    o["L3_ffn_We_rows"] = i["L3_ffn_We"].reshape(-1, D)
    return {k: np.ascontiguousarray(v) for k, v in o.items()}


def kernel(**inputs):
    import numpy as np
    import concourse.bacc as bacc
    from concourse.bass_utils import run_bass_kernel_spmd

    nc = bacc.Bacc("TRN2", target_bir_lowering=False, num_devices=1)
    arrays = layouts({k: np.asarray(v) for k, v in inputs.items()}, np)
    a = {k: nc.dram_tensor(f"in_{k}", v.shape, mybir.dt.from_np(v.dtype), kind="ExternalInput").ap()
         for k, v in arrays.items()}
    out = nc.dram_tensor("out_x", (N, D), F32, kind="ExternalOutput").ap()
    program(nc, a, out)
    r = run_bass_kernel_spmd(nc, [{f"in_{k}": v for k, v in arrays.items()}], core_ids=[0])
    return r.results[0]["out_x"]
```

```python
from contextlib import ExitStack
import math

import concourse.bass as bass
from concourse import mybir

F32 = mybir.dt.float32
BF16 = mybir.dt.bfloat16
I32 = mybir.dt.int32
U32 = mybir.dt.uint32
ALU = mybir.AluOpType
ACT = mybir.ActivationFunctionType
AX_X = mybir.AxisListType.X

P = 128
N = 1024
D = 512
NT = N // P
DC = D // P
E = 17408
EP = E // P
CH = EP + NT
SLOTS = CH * P
RS = 32
RD = 4
S_RBF, S_U, S_W, S_LO, S_OTHER = 0, 20, 23, 24, 25
D_W, D_LO, D_OTHER, D_TYPED = 0, 1, 2, 3
RBF = 20
EPS = 1e-5
ROWS = 16
PART = 4
FREED = 2
DEEP = 16
RING = 8
GROUP = EP // NT
COLS = 8
KNOWN = 8
LEAD = 4


class Stage:

    def __init__(self, nc, tag):
        self.nc, self.tag, self.ctx, self.sems = nc, tag, ExitStack(), []

    def __enter__(self):
        return self

    def __exit__(self, *e):
        self.ctx.close()
        if self.sems:
            self.nc.clear_and_free_semaphores(self.sems)
            self.nc.all_engine_barrier(sem_only=True)
        return False

    def sb(self, name, shape, dt=F32):
        return self.ctx.enter_context(self.nc.sbuf_tensor(f"{self.tag}_{name}", shape, dt))

    def ps(self, name, shape=(P, D)):
        return self.ctx.enter_context(self.nc.psum_tensor(f"{self.tag}_{name}", list(shape), F32))

    def sem(self, name):
        self.sems.append(self.nc.alloc_semaphore(f"{self.tag}_{name}"))
        return self.sems[-1]


class Landings:

    def __init__(self, ctx, nc):
        self.sems = [ctx.enter_context(nc.semaphore(f"landed{k}")) for k in range(ROWS)]
        self.counts = [0] * ROWS
        self.scattered = [ctx.enter_context(nc.semaphore(f"scattered{u}")) for u in range(2)]

    def take(self, transfers):
        pairs = [(self.sems[k], self.counts[k]) for k in range(len(transfers))]
        for k, n in enumerate(transfers):
            self.counts[k] += 16 * n
        return pairs


class Weights:

    def __init__(self, s):
        self.s, self.loads = s, []

    def add(self, name, shape, src=None):
        tile = self.s.sb(name, shape)
        if src is not None:
            self.load(tile[:], src)
        return tile

    def load(self, dst, src):
        self.loads.append((dst, src))

    def start(self, sp, loaded):
        for dst, src in self.loads:
            sp.dma_start(dst, src).then_inc(loaded, 16)

    def finish(self, sp, loaded):
        sp.wait_ge(loaded, 16 * len(self.loads))


def by_rows(w):
    return w.rearrange("(k p) d -> p k d", p=P)


class Shared:

    def __init__(self, nc, ctx):
        def sb(name, shape, dt=F32):
            return ctx.enter_context(nc.sbuf_tensor(name, shape, dt))

        def dram(name, shape):
            return nc.dram_tensor(name, shape, F32, kind="Internal").ap()

        self.X = sb("X", [P, NT, D])
        self.XL = sb("XL", [P, NT, D])
        self.XLT = None
        self.ident = sb("ident", [P, P])
        self.ones = sb("ones", [P, P])
        self.before = sb("before", [P, P])
        self.spread = sb("spread", [8, 256])
        self.iota = sb("iota", [P, 144])
        self.eps = sb("eps", [P, 1])
        self.rec_s = sb("rec_s", [P, CH, RS])
        self.rec_d = sb("rec_d", [P, CH, RD])
        self.tile_of = sb("tile_of", [P, 2, CH])
        self.tile_row = sb("tile_row", [1, 2, CH], I32)
        self.by_src = dram("by_src", [SLOTS, RS])
        self.by_dst = dram("by_dst", [SLOTS, RD])
        self.rows = dram("rows", [4 * N, D])
        self.slot = sb("slot", [P, 2, EP], I32)
        self.loose_d = sb("loose_d", [P, EP, RD])
        self.degree = sb("degree", [P, 2, NT])
        self.landings = Landings(ctx, nc)



def make_constants(nc, c):
    with Stage(nc, "setup") as s:
        filled, made, bounded = s.sem("filled"), s.sem("made"), s.sem("bounded")
        with nc.Block() as block:
            @block.vector
            def _(dve):
                dve.memset(c.eps[:], EPS)
                dve.memset(c.ones[:], 1.0).then_inc(filled, 1)
                dve.memset(c.ident[:], 0.0).then_inc(filled, 1)
                dve.memset(c.spread[:], 1.0).then_inc(filled, 1)

            @block.gpsimd
            def _(pool):
                pool.iota(c.iota[:], [[1, 144]], base=0, channel_multiplier=0,
                          allow_small_or_imprecise_dtypes=True).then_inc(made, 1)
                pool.wait_ge(filled, 3)
                pool.affine_select(out=c.ident[:], in_=c.ident[:], compare_op=ALU.not_equal, fill=1.0,
                                   base=0, pattern=[[-1, P]], channel_multiplier=1).then_inc(made, 1)
                pool.affine_select(out=c.before[:], in_=c.ones[:], compare_op=ALU.is_gt, fill=0.0,
                                   base=0, pattern=[[1, P]], channel_multiplier=-1).then_inc(made, 1)
                pool.affine_select(out=c.spread[:], in_=c.spread[:], compare_op=ALU.is_ge, fill=0.0,
                                   base=0, pattern=[[1, 256]], channel_multiplier=-32).then_inc(bounded, 1)
                pool.wait_ge(bounded, 1)
                pool.affine_select(out=c.spread[:], in_=c.spread[:], compare_op=ALU.is_ge, fill=0.0,
                                   base=31, pattern=[[-1, 256]], channel_multiplier=32).then_inc(made, 1)



def bin_edges(nc, c, a, loose_s, of_tile):
    with Stage(nc, "bin") as s:
        keys = s.sb("keys", [P, 2, EP], I32)
        typ = s.sb("typ", [P, EP], I32)
        tile_i = s.sb("tile_i", [P, 2, EP], I32)
        low_i = s.sb("low_i", [P, 2, EP], I32)
        tile_f = s.sb("tile_f", [P, 2, EP])
        zeros = s.sb("zeros", [P, EP])
        member = s.sb("member", [P, 2, NT, EP])
        rank = s.sb("rank", [P, 2, NT, EP])
        slot_f = s.sb("slot_f", [P, 2, EP])
        slot_i = s.sb("slot_i", [P, 2, EP], I32)
        chunk_i = s.sb("chunk_i", [P, 2, EP], I32)
        total = s.sb("total", [P, 2 * NT])
        count_f = s.sb("count_f", [P, 2 * NT])
        count_i = s.sb("count_i", [P, 2 * NT], I32)
        chunks = s.sb("chunks", [P, 2, NT])
        ends = s.sb("ends", [P, 2, NT])
        shift = s.sb("shift", [P, 2, NT])
        tmap = s.sb("tmap", [P, 2, CH])
        square = s.sb("square", [P, EP, 3])
        length = s.sb("length", [P, EP])
        rec_s, rec_d = loose_s, c.loose_d
        pad_s = s.sb("pad_s", [P, CH, RS])
        pad_d = s.sb("pad_d", [P, CH, RD])
        earlier, all_of = s.ps("earlier", [P, 2 * NT]), s.ps("all_of", [P, 2 * NT])
        keys_in, fields_in, padded = s.sem("keys_in"), s.sem("fields_in"), s.sem("padded")
        chain, counted, summed = s.sem("chain"), s.sem("counted"), s.sem("summed")
        cleared, x_in, squared, rooted = s.sem("cleared"), s.sem("x_in"), s.sem("squared"), s.sem("rooted")
        with nc.Block() as block:
            @block.sync
            def _(sp):
                sp.dma_start(keys[:, 0, :], a["src"].rearrange("(p c) -> p c", p=P)).then_inc(keys_in, 16)
                sp.dma_start(keys[:, 1, :], a["dst"].rearrange("(p c) -> p c", p=P)).then_inc(keys_in, 16)
                sp.dma_start(typ[:], a["edge_type_4"].rearrange("(p c) -> p c", p=P)).then_inc(keys_in, 16)
                sp.dma_start(rec_s[:, :, S_RBF:S_RBF + RBF],
                             a["edge_attr_20"].rearrange("(p c) f -> p c f", p=P)).then_inc(fields_in, 16)
                sp.dma_start(rec_s[:, :, S_U:S_U + 3],
                             a["edge_attr_3"].rearrange("(p c) f -> p c f", p=P)).then_inc(fields_in, 16)
                sp.dma_start(tile_f[:, 0, :], a["edge_weight"].rearrange("(p c) -> p c", p=P)).then_inc(fields_in, 16)
                sp.dma_start(c.X[:, :, :], a["x"].rearrange("(t p) d -> p t d", p=P)).then_inc(x_in, 16)
                sp.wait_ge(cleared, 1)
                sp.dma_start(c.by_src.rearrange("(p c) f -> p c f", p=P), pad_s[:]).then_inc(padded, 16)
                sp.dma_start(c.by_dst.rearrange("(p c) f -> p c f", p=P), pad_d[:]).then_inc(padded, 16)
                sp.wait_ge(padded, 32)
                sp.wait_ge(x_in, 16)

            @block.scalar
            def _(act):
                act.wait_ge(squared, 1)
                act.sqrt(length[:], length[:]).then_inc(rooted, 1)

            @block.vector
            def _(dve):
                links = [0]

                def link(ins):
                    links[0] += 1
                    ins.then_inc(chain, 1)
                    dve.wait_ge(chain, links[0])

                dve.memset(zeros[:], 0.0)
                dve.memset(rec_s[:, :, S_OTHER + 1:RS], 0.0)
                dve.memset(pad_d[:], 0.0)
                link(dve.memset(pad_s[:], 0.0))
                dve.memset(pad_s[:, :, S_U:S_U + 3], 1.0)
                dve.memset(pad_s[:, :, S_LO:S_LO + 1], -1.0)
                link(dve.memset(pad_d[:, :, D_LO:D_LO + 1], -1.0))
                dve.sem_inc(cleared, 1)
                dve.wait_ge(fields_in, 48)
                dve.wait_ge(keys_in, 48)
                dve.tensor_copy(rec_s[:, :, S_W], tile_f[:, 0, :])
                dve.tensor_copy(rec_d[:, :, D_W], tile_f[:, 0, :])
                dve.tensor_copy(rec_s[:, :, S_OTHER], keys[:, 1, :])
                dve.tensor_copy(rec_d[:, :, D_OTHER], keys[:, 0, :])
                r = rec_s[:, :, S_U:S_U + 3]
                link(dve.tensor_tensor(square[:], r, r, ALU.mult))
                dve.tensor_reduce(length[:], square[:], AX_X, ALU.add).then_inc(squared, 1)
                dve.tensor_scalar(tile_i[:], keys[:], 7, None, ALU.logical_shift_right)
                link(dve.tensor_scalar(low_i[:], keys[:], P - 1, None, ALU.bitwise_and))
                dve.scalar_tensor_tensor(out=rec_d[:, :, D_TYPED], in0=typ[:], scalar=float(N),
                                         in1=keys[:, 0, :], op0=ALU.mult, op1=ALU.add)
                dve.tensor_copy(rec_s[:, :, S_LO], low_i[:, 0, :])
                dve.tensor_copy(rec_d[:, :, D_LO], low_i[:, 1, :])
                link(dve.tensor_copy(tile_f[:], tile_i[:]))
                for b in range(NT):
                    last = dve.tensor_scalar(member[:, :, b, :], tile_f[:], float(b), None, ALU.is_equal)
                link(last)
                for k in range(2):
                    for b in range(NT):
                        last = dve.tensor_tensor_scan(rank[:, k, b, :], zeros[:], member[:, k, b, :], 0.0,
                                                      ALU.add, ALU.add)
                link(last)
                dve.tensor_copy(total[:], rank[:, :, :, EP - 1].rearrange("p k b -> p (k b)")).then_inc(counted, 1)
                dve.wait_ge(rooted, 1)
                link(dve.reciprocal(length[:], length[:]))
                dve.tensor_tensor(r, r, length[:].unsqueeze(2).to_broadcast([P, EP, 3]), ALU.mult)
                dve.wait_ge(summed, 1)
                link(dve.tensor_scalar(count_f[:], all_of[:], float(P - 1), None, ALU.add))
                link(dve.tensor_copy(count_i[:], count_f[:]))
                link(dve.tensor_scalar(count_i[:], count_i[:], 7, None, ALU.logical_shift_right))
                link(dve.tensor_copy(chunks[:].rearrange("p k b -> p (k b)"), count_i[:]))
                for k in range(2):
                    last = dve.tensor_tensor_scan(ends[:, k, :], zeros[:, 0:NT], chunks[:, k, :], 0.0,
                                                  ALU.add, ALU.add)
                link(last)
                link(dve.tensor_tensor(shift[:], ends[:], chunks[:], ALU.subtract))
                link(dve.tensor_scalar(shift[:], shift[:], float(P), -1.0, ALU.mult, ALU.add))
                link(dve.tensor_tensor(shift[:].rearrange("p k b -> p (k b)"),
                                       shift[:].rearrange("p k b -> p (k b)"), earlier[:], ALU.add))
                for k in range(2):
                    for b in range(NT):
                        last = dve.scalar_tensor_tensor(out=rank[:, k, b, :], in0=rank[:, k, b, :],
                                                        scalar=shift[:, k, b:b + 1], in1=member[:, k, b, :],
                                                        op0=ALU.add, op1=ALU.mult)
                link(last)
                for k in range(2):
                    last = dve.tensor_reduce(slot_f[:, k, :], rank[:, k, :, :].rearrange("p b e -> p e b"),
                                             AX_X, ALU.add)
                link(last)
                link(dve.tensor_copy(slot_i[:], slot_f[:]))
                dve.tensor_scalar(chunk_i[:], slot_i[:], 7, None, ALU.logical_shift_right)
                link(dve.tensor_scalar(slot_i[:], slot_i[:], P - 1, None, ALU.bitwise_and))
                dve.scalar_tensor_tensor(out=c.slot[:], in0=slot_i[:], scalar=float(CH), in1=chunk_i[:],
                                         op0=ALU.mult, op1=ALU.add)
                dst_tile = member[:, 1].rearrange("p b e -> p e b")
                dve.tensor_tensor(of_tile[:, :, 0:NT], dst_tile,
                                  rec_d[:, :, D_W:D_W + 1].to_broadcast([P, EP, NT]), ALU.mult)
                dve.tensor_copy(of_tile[:, :, NT:2 * NT], dst_tile)
                for b in range(NT):
                    for k in range(2):
                        if b == 0:
                            last = dve.tensor_scalar(tmap[:, k, :], c.iota[:, 0:CH], ends[:, k, b:b + 1], None,
                                                     ALU.is_ge)
                        else:
                            last = dve.scalar_tensor_tensor(out=tmap[:, k, :], in0=c.iota[:, 0:CH],
                                                            scalar=ends[:, k, b:b + 1], in1=tmap[:, k, :],
                                                            op0=ALU.is_ge, op1=ALU.add)
                    link(last)
                link(dve.tensor_scalar(c.tile_of[:], tmap[:], float(NT - 1), None, ALU.min))
                dve.tensor_copy(c.tile_row[:], c.tile_of[0:1, :, :])

            @block.tensor
            def _(pe):
                pe.wait_ge(counted, 1)
                pe.matmul(earlier[:], c.before[:], total[:], start=True, stop=True)
                pe.matmul(all_of[:], c.ones[:], total[:], start=True, stop=True).then_inc(summed, 1)


class Scatter:

    def __init__(self, nc, c, s, order, loose, table, words):
        self.c, self.order, self.loose, self.table = c, order, loose, table
        self.at = [s.sb(f"slots{u}", [P, GROUP], I32) for u in range(2)]
        self.recs = [s.sb(f"recs{u}", [P, GROUP, words]) for u in range(2)]
        self.base = order * EP // 2 * 16
        self.slots_in, self.recs_in, self.sent = s.sem("slots_in"), s.sem("recs_in"), s.sem("sent")

    def free(self, engine, g, u, first):
        if not first:
            engine.wait_ge(self.c.landings.scattered[u], self.base + (g - u) * (GROUP * 8))
            engine.sem_inc(self.sent, 1)

    def copy_slots(self, pool, g, u, first=False):
        self.free(pool, g, u, first)
        pool.tensor_copy(self.at[u][:], self.c.slot[:, self.order, bass.ds(g * GROUP, GROUP)])\
            .then_inc(self.slots_in, 1)

    def copy_recs(self, engine, copy, g, u, first=False):
        self.free(engine, g, u, first)
        copy(self.recs[u][:], self.loose[:, bass.ds(g * GROUP, GROUP), :]).then_inc(self.recs_in, 1)

    def send(self, pool, g, u, columns):
        pool.wait_ge(self.slots_in, g + 1)
        pool.wait_ge(self.recs_in, g + 1)
        pool.sem_inc(self.sent, 1)
        for k in columns:
            pool.indirect_dma_start(self.table, bass.IndirectOffsetOnAxis(ap=self.at[u][:, k:k + 1], axis=0),
                                    self.recs[u][:, k, :], None).then_inc(self.c.landings.scattered[u], 16)

    def finish(self, pool, done):
        for u in range(2):
            pool.wait_ge(self.c.landings.scattered[u], self.base + EP // 2 * 16)
        pool.sem_inc(done, 1)



def norm(nc, c, tag, src, dst, affine=None, turned=None, columns=None, rows=None, residual=False, scatter=None,
         ahead=None):
    columns = columns or [slice(k * P, (k + 1) * P) for k in range(DC)]
    with Stage(nc, tag) as s:
        stats = s.sb("stats", [P, NT, 6])
        mv = s.sb("mv", [P, NT, 2])
        dev = s.sb("dev", [P, NT])
        rdev = s.sb("rdev", [P, NT])
        gains = s.sb("gains", [P, 2, D]) if affine else None
        turn = [s.ps(f"turn{k}") for k in range(2)]
        stat, moment, rooted, inverted, centred, shifted, added = (s.sem(n) for n in (
            "stat", "moment", "rooted", "inverted", "centred", "shifted", "added"))
        scaled = [s.sem("scaled_even"), s.sem("scaled_odd")]
        turned_ok, taken, stored, gains_in = s.sem("turned"), s.sem("taken"), s.sem("stored"), s.sem("gains_in")
        final = shifted if affine else centred
        loaded = s.sem("loaded")
        with nc.Block() as block:
            if scatter:
                @block.gpsimd
                def _(pool):
                    scatter.copy_slots(pool, 0, 0, first=True)
                    scatter.copy_recs(pool, pool.tensor_copy, 0, 0, first=True)
                    scatter.send(pool, 0, 0, range(GROUP))

            @block.sync
            def _(sp):
                if ahead:
                    ahead.start(sp, loaded)
                if affine:
                    for k in range(2):
                        sp.dma_start(gains[:, k, :], affine[k].partition_broadcast(P)).then_inc(gains_in, 16)
                if rows is not None:
                    for t in range(NT):
                        sp.wait_ge(final, t + 1)
                        sp.dma_start(rows[t * P:(t + 1) * P, :], dst[:, t, :]).then_inc(stored, 16)
                    sp.wait_ge(stored, 16 * NT)
                if ahead:
                    ahead.finish(sp, loaded)

            if affine:
                @block.gpsimd
                def _(pool):
                    pool.wait_ge(gains_in, 32)
                    for t in range(1, NT, 2):
                        pool.wait_ge(centred, t + 1)
                        pool.tensor_tensor(dst[:, t, :], dst[:, t, :], gains[:, 0, :], ALU.mult).then_inc(scaled[1], 1)

            @block.vector
            def _(dve):
                for t in range(NT):
                    dve.bn_stats(stats[:, t, :], src[:, t, :]).then_inc(stat, 1)
                for t in range(NT):
                    dve.wait_ge(stat, t + 1)
                    dve.bn_aggr(mv[:, t, :], stats[:, t, :]).then_inc(moment, 1)
                dve.wait_ge(rooted, 1)
                dve.reciprocal(rdev[:], dev[:]).then_inc(inverted, 1)
                dve.wait_ge(inverted, 1)
                for t in range(NT):
                    dve.tensor_scalar(dst[:, t, :], src[:, t, :], mv[:, t, 0:1], rdev[:, t:t + 1],
                                      ALU.subtract, ALU.mult).then_inc(centred, 1)
                if affine:
                    dve.wait_ge(gains_in, 32)
                    for t in range(0, NT, 2):
                        dve.wait_ge(centred, t + 1)
                        dve.tensor_tensor(dst[:, t, :], dst[:, t, :], gains[:, 0, :], ALU.mult).then_inc(scaled[0], 1)
                    for t in range(NT):
                        dve.wait_ge(scaled[t % 2], t // 2 + 1)
                        dve.tensor_tensor(dst[:, t, :], dst[:, t, :], gains[:, 1, :], ALU.add).then_inc(shifted, 1)
                if residual:
                    for t in range(NT):
                        dve.wait_ge(final, t + 1)
                        dve.tensor_tensor(c.X[:, t, :], c.X[:, t, :], dst[:, t, :], ALU.add).then_inc(added, 1)

            @block.scalar
            def _(act):
                act.wait_ge(moment, NT)
                act.activation(dev[:], mv[:, :, 1], ACT.Sqrt, bias=c.eps[:]).then_inc(rooted, 1)
                if turned is not None:
                    for t in range(NT):
                        act.wait_ge(turned_ok, t + 1)
                        act.copy(turned[:, :, t * P:(t + 1) * P],
                                 turn[t % 2][:, :].rearrange("p (k n) -> p k n", k=DC)).then_inc(taken, 1)

            @block.tensor
            def _(pe):
                if turned is not None:
                    for t in range(NT):
                        pe.wait_ge(final, t + 1)
                        if t >= 2:
                            pe.wait_ge(taken, t - 1)
                        for k, cols in enumerate(columns):
                            last = pe.transpose(turn[t % 2][:, k * P:(k + 1) * P], dst[:, t, cols], c.ident[:])
                        last.then_inc(turned_ok, 1)



def table_weights(s, weights, biases):
    R = weights.shape[0]
    ahead = Weights(s)
    w = ahead.add("w", [P, R, DC, D])
    bias = ahead.add("bias", [P, R, D]) if biases is not None else None
    for r in range(R):
        ahead.load(w[:, r], by_rows(weights[r]))
        if biases is not None:
            ahead.load(bias[:, r, :], biases[r].partition_broadcast(P))
    return ahead, w, bias


def node_tables(nc, c, tag, w, bias, table, scatter=None, of_tile=None):
    R = w.shape[1]
    with Stage(nc, tag) as s:
        row = [s.sb(f"row{k}", [P, D]) for k in range(4)]
        out = [s.ps(f"out{k}") for k in range(4)]
        product, biased = s.sem("product"), s.sem("biased")
        stored = [s.sem(f"stored{k}") for k in range(4)]
        scattered, reloaded = s.sem("scattered_ok"), s.sem("reloaded")
        work = [(r, t) for r in range(R) for t in range(NT)]
        if scatter:
            hot = [s.sb(f"hot{j}", [P, P]) for j in range(COLS)]
            degree = s.ps("degree", [P, 2 * NT])
            marked, counted, kept = s.sem("marked"), s.sem("counted"), s.sem("kept")
        with nc.Block() as block:
            if scatter:
                @block.gpsimd
                def _(pool):
                    scatter.copy_slots(pool, 1, 1, first=True)
                    scatter.send(pool, 1, 1, range(GROUP))
                    with pool.Fori(1, NT // 2) as i:
                        for u in range(2):
                            scatter.copy_slots(pool, i * 2 + u, u)
                            scatter.send(pool, i * 2 + u, u, range(GROUP))
                    scatter.finish(pool, scattered)

                @block.scalar
                def _(act):
                    scatter.copy_recs(act, act.copy, 1, 1, first=True)
                    with act.Fori(1, NT // 2) as i:
                        for u in range(2):
                            scatter.copy_recs(act, act.copy, i * 2 + u, u)

            @block.sync
            def _(sp):
                for i, (r, t) in enumerate(work):
                    sp.wait_ge(biased, i + 1)
                    sp.dma_start(table[(r * NT + t) * P:(r * NT + t + 1) * P, :], row[i % 4][:])\
                        .then_inc(stored[i % 4], 16)
                for k in range(4):
                    sp.wait_ge(stored[k], 16 * (len(work) // 4))
                if scatter:
                    sp.wait_ge(scattered, 1)
                    sp.dma_start(c.rec_s[:], c.by_src.rearrange("(p c) f -> p c f", p=P)).then_inc(reloaded, 16)
                    sp.wait_ge(reloaded, 16)

            @block.tensor
            def _(pe):
                for i, (r, t) in enumerate(work):
                    if i >= 4:
                        pe.wait_ge(biased, i - 3)
                    for k in range(DC):
                        last = pe.matmul(out[i % 4][:], c.XLT[:, k, t * P:(t + 1) * P], w[:, r, k, :],
                                         start=k == 0, stop=k == DC - 1)
                    last.then_inc(product, 1)
                if scatter:
                    def count(i, first, last):
                        for j in range(COLS):
                            e = i * COLS + j
                            pe.wait_ge(marked, e + 1)
                            pe.matmul(degree[:], hot[j][:], of_tile[:, bass.ds(e, 1), :].rearrange("p a b -> p (a b)"),
                                      start=first and j == 0, stop=last and j == COLS - 1).then_inc(counted, 1)

                    count(0, True, False)
                    with pe.Fori(1, EP // COLS - 1) as i:
                        count(i, False, False)
                    count(EP // COLS - 1, False, True)

            @block.vector
            def _(dve):
                for i, (r, t) in enumerate(work):
                    dve.wait_ge(product, i + 1)
                    if i >= 4:
                        dve.wait_ge(stored[i % 4], 16 * (i // 4))
                    if bias is not None:
                        dve.tensor_tensor(row[i % 4][:], out[i % 4][:], bias[:, r, :], ALU.add).then_inc(biased, 1)
                    else:
                        dve.tensor_copy(row[i % 4][:], out[i % 4][:]).then_inc(biased, 1)
                if scatter:
                    dve.sem_inc(counted, COLS)
                    with dve.Fori(0, EP // COLS) as i:
                        for j in range(COLS):
                            e = i * COLS + j
                            dve.wait_ge(counted, e + 1)
                            low = c.loose_d[:, bass.ds(e, 1), D_LO:D_LO + 1].rearrange("p a b -> p (a b)")
                            dve.tensor_scalar(hot[j][:], c.iota[:, 0:P], low, None, ALU.is_equal)\
                                .then_inc(marked, 1)
                    dve.wait_ge(counted, COLS + EP)
                    dve.tensor_copy(c.degree[:].rearrange("p k t -> p (k t)"), degree[:]).then_inc(kept, 1)



def tiles_of(nc, c, engine, order, first):
    _, tiles = nc.values_load_multi_w_load_instructions(
        c.tile_row[0:1, order, bass.ds(first, KNOWN)], engines=(engine.engine,), min_val=0, max_val=NT - 1,
        skip_runtime_bounds_check_because="bin_edges keeps the tiles within 0 and NT - 1")
    return tiles


def aggregate(nc, c, tag, order, rec, index, lo, weight, table, total, clear=False, ahead=None, dense=None):
    with Stage(nc, tag) as s:
        at = [s.sb(f"at{h}", [P, LEAD], I32) for h in range(DEEP // LEAD)]
        rows = [s.sb(f"rows{j}", [P, D]) for j in range(DEEP)]
        hot = [s.sb(f"hot{j}", [P, P]) for j in range(DEEP)]
        part = [s.ps(f"part{j}") for j in range(LEAD)]
        landed = c.landings.take([CH // DEEP] * DEEP)
        placed, marked, summed, added = s.sem("placed"), s.sem("marked"), s.sem("summed"), s.sem("added")
        issued, loaded = s.sem("issued"), s.sem("loaded")
        flat = total[:, :, :].rearrange("p t d -> p (t d)")
        LOOPS = CH // DEEP
        dense_out = [s.ps(f"dense{k}") for k in range(2)] if dense else None
        dense_made, dense_kept = s.sem("dense_made"), s.sem("dense_kept")
        with nc.Block() as block:
            if dense:
                @block.scalar
                def _(act):
                    for t in range(NT):
                        act.wait_ge(dense_made, t + 1)
                        act.copy(dense[1][:, t, :], dense_out[t % 2][:]).then_inc(dense_kept, 1)

            if ahead:
                @block.sync
                def _(sp):
                    ahead.start(sp, loaded)
                    ahead.finish(sp, loaded)

            @block.gpsimd
            def _(pool):
                with pool.Fori(0, LOOPS) as i:
                    for h in range(DEEP // LEAD):
                        first = i * DEEP + h * LEAD
                        pool.wait_ge(summed, first + LEAD)
                        pool.tensor_copy(at[h][:], rec[:, bass.ds(first, LEAD), index])\
                            .then_inc(placed, 1)
                        pool.wait_ge(placed, i * (DEEP // LEAD) + h + 1)
                        pool.sem_inc(issued, 1)
                        for j in range(h * LEAD, (h + 1) * LEAD):
                            k = j - h * LEAD
                            pool.indirect_dma_start(rows[j][:], None, table,
                                                    bass.IndirectOffsetOnAxis(ap=at[h][:, k:k + 1], axis=0))\
                                .then_inc(landed[j][0], 16)

            @block.vector
            def _(dve):
                dve.sem_inc(summed, DEEP)
                if clear:
                    dve.memset(flat, 0.0).then_inc(added, LEAD)
                else:
                    dve.sem_inc(added, LEAD)

                def one_hot(chunk, j):
                    dve.wait_ge(summed, chunk + 1)
                    low = rec[:, bass.ds(chunk, 1), lo:lo + 1].rearrange("p a b -> p (a b)")
                    if weight is None:
                        dve.tensor_scalar(hot[j][:], c.iota[:, 0:P], low, None, ALU.is_equal).then_inc(marked, 1)
                    else:
                        w = rec[:, bass.ds(chunk, 1), weight:weight + 1].rearrange("p a b -> p (a b)")
                        dve.tensor_scalar(hot[j][:], c.iota[:, 0:P], low, w,
                                          ALU.is_equal, ALU.mult).then_inc(marked, 1)

                def add(chunk, j, tiles):
                    tile = tiles[j % KNOWN]
                    dve.wait_ge(summed, DEEP + chunk + 1)
                    dve.wait_ge(added, LEAD + chunk)
                    there = flat[:, bass.ds(tile * D, D)]
                    dve.tensor_tensor(there, there, part[j % LEAD][:], ALU.add).then_inc(added, 1)

                for j in range(LEAD):
                    one_hot(j, j)
                with dve.Fori(0, LOOPS - 1) as i:
                    for j in range(DEEP):
                        if j % KNOWN == 0:
                            tiles = tiles_of(nc, c, dve, order, i * DEEP + j)
                        one_hot(i * DEEP + j + LEAD, (j + LEAD) % DEEP)
                        add(i * DEEP + j, j, tiles)
                for j in range(DEEP):
                    chunk = (LOOPS - 1) * DEEP + j
                    if chunk + LEAD < CH:
                        one_hot(chunk + LEAD, (j + LEAD) % DEEP)
                    if j % KNOWN == 0:
                        tiles = tiles_of(nc, c, dve, order, chunk)
                    add(chunk, j, tiles)

            @block.tensor
            def _(pe):
                def products(tiles):
                    for t in tiles:
                        if t >= 2:
                            pe.wait_ge(dense_kept, t - 1)
                        for k in range(DC):
                            last = pe.matmul(dense_out[t % 2][:], c.XLT[:, k, t * P:(t + 1) * P], dense[0][:, k, :],
                                             start=k == 0, stop=k == DC - 1)
                        last.then_inc(dense_made, 1)

                def sums(i):
                    for j in range(DEEP):
                        chunk = i * DEEP + j
                        pe.wait_ge(marked, chunk + 1)
                        pe.wait_ge(added, chunk + 1)
                        pe.wait_ge(landed[j][0], landed[j][1] + (i + 1) * 16)
                        pe.matmul(part[j % LEAD][:], hot[j][:], rows[j][:], start=True, stop=True)\
                            .then_inc(summed, 1)

                for part_of in range(2):
                    if dense:
                        products(range(part_of * NT // 2, (part_of + 1) * NT // 2))
                    with pe.Fori(*((0, LOOPS // 2), (LOOPS // 2, LOOPS))[part_of]) as i:
                        sums(i)



def relation_update(nc, c, bias, agg, mixed, ahead):
    with Stage(nc, "l1u") as s:
        rdeg = s.sb("rdeg", [P, NT])
        loaded, biased, scaled, summed, chain = (s.sem(n) for n in ("loaded", "biased", "scaled", "summed", "chain"))
        with nc.Block() as block:
            @block.sync
            def _(sp):
                ahead.start(sp, loaded)
                ahead.finish(sp, loaded)

            @block.gpsimd
            def _(pool):
                for t in range(NT):
                    pool.tensor_tensor(c.XL[:, t, :], c.XL[:, t, :], bias[:], ALU.add).then_inc(biased, 1)

            @block.vector
            def _(dve):
                dve.tensor_scalar(rdeg[:], c.degree[:, 0, :], 1.0, None, ALU.max).then_inc(chain, 1)
                dve.wait_ge(chain, 1)
                dve.reciprocal(rdeg[:], rdeg[:]).then_inc(chain, 1)
                dve.wait_ge(chain, 2)
                for t in range(NT):
                    dve.scalar_tensor_tensor(out=mixed[:, t, :], in0=agg[:, t, :], scalar=rdeg[:, t:t + 1],
                                             in1=mixed[:, t, :], op0=ALU.mult, op1=ALU.add).then_inc(scaled, 1)
                for t in range(NT):
                    dve.wait_ge(scaled, t + 1)
                    dve.wait_ge(biased, t + 1)
                    dve.tensor_tensor(mixed[:, t, :], mixed[:, t, :], c.XL[:, t, :], ALU.add).then_inc(summed, 1)


def relation_mlp(nc, c, w1, b1, w2, b2, x1, x1t, out_sum):
    HC = 2 * D // P
    with Stage(nc, "l1m") as s:
        hid = s.sb("hid", [P, HC, N])
        up = [s.ps(f"up{k}") for k in range(4)]
        down = [s.ps(f"down{k}") for k in range(4)]
        upped, active, downed, read, summed = (s.sem(n) for n in (
            "upped", "active", "downed", "read", "summed"))
        work = [(h, n) for h in range(HC) for n in range(2)]
        with nc.Block() as block:
            @block.tensor
            def _(pe):
                for i, (h, n) in enumerate(work):
                    if i >= 4:
                        pe.wait_ge(active, i - 3)
                    for k in range(DC):
                        last = pe.matmul(up[i % 4][:], w1[:, k, h * P:(h + 1) * P], x1t[:, k, n * D:(n + 1) * D],
                                         start=k == 0, stop=k == DC - 1)
                    last.then_inc(upped, 1)
                pe.wait_ge(active, len(work))
                for t in range(NT):
                    if t >= 4:
                        pe.wait_ge(read, t - 3)
                    for h in range(HC):
                        last = pe.matmul(down[t % 4][:], hid[:, h, t * P:(t + 1) * P], w2[:, h, :],
                                         start=h == 0, stop=h == HC - 1)
                    last.then_inc(downed, 1)

            @block.scalar
            def _(act):
                for i, (h, n) in enumerate(work):
                    act.wait_ge(upped, i + 1)
                    act.activation(hid[:, h, n * D:(n + 1) * D], up[i % 4][:], ACT.Gelu,
                                   bias=b1[:, h:h + 1]).then_inc(active, 1)

            @block.vector
            def _(dve):
                for t in range(NT):
                    dve.wait_ge(downed, t + 1)
                    dve.tensor_tensor(out_sum[:, t, :], down[t % 4][:], b2[:], ALU.add).then_inc(read, 1)
                    dve.wait_ge(read, t + 1)
                    dve.tensor_tensor(out_sum[:, t, :], out_sum[:, t, :], x1[:, t, :], ALU.add).then_inc(summed, 1)


def expert_weights(s, w1_d, b1_d, w2_d, b2_d):
    ahead = Weights(s)
    return (ahead, ahead.add("w1", [P, DC, 256], by_rows(w1_d)), ahead.add("b1", [P, 2], b1_d),
            ahead.add("w2", [P, 2, D], by_rows(w2_d)), ahead.add("b2", [8, D], b2_d))


def expert_mix(nc, c, tag, gate_t, w1, b1, w2, b2):
    with Stage(nc, tag) as s:
        hid = s.sb("hid", [P, 2, N])
        up = [s.ps(f"up{k}") for k in range(4)]
        wide = [s.ps(f"wide{k}") for k in range(4)]
        upped, active, gated, downed, added = (s.sem(n) for n in (
            "upped", "active", "gated", "downed", "added"))
        work = [(h, n) for h in range(2) for n in range(2)]
        with nc.Block() as block:
            @block.tensor
            def _(pe):
                for i, (h, n) in enumerate(work):
                    pe.matmul(wide[i][:], c.spread[:, h * P:(h + 1) * P], gate_t[:, n * D:(n + 1) * D],
                              start=True, stop=True)
                    for k in range(DC):
                        last = pe.matmul(up[i][:], w1[:, k, h * P:(h + 1) * P], c.XLT[:, k, n * D:(n + 1) * D],
                                         start=k == 0, stop=k == DC - 1)
                    last.then_inc(upped, 1)
                pe.wait_ge(gated, 4)
                for t in range(NT):
                    if t >= 4:
                        pe.wait_ge(added, t - 3)
                    for h in range(2):
                        pe.matmul(up[t % 4][:], hid[:, h, t * P:(t + 1) * P], w2[:, h, :], start=h == 0, stop=False)
                    pe.matmul(up[t % 4][:], gate_t[:, t * P:(t + 1) * P], b2[:], start=False, stop=True)\
                        .then_inc(downed, 1)

            @block.scalar
            def _(act):
                for i, (h, n) in enumerate(work):
                    act.wait_ge(upped, i + 1)
                    act.activation(hid[:, h, n * D:(n + 1) * D], up[i][:], ACT.Gelu,
                                   bias=b1[:, h:h + 1]).then_inc(active, 1)

            @block.vector
            def _(dve):
                for i, (h, n) in enumerate(work):
                    dve.wait_ge(active, i + 1)
                    part = hid[:, h, n * D:(n + 1) * D]
                    dve.tensor_tensor(part, part, wide[i][:], ALU.mult).then_inc(gated, 1)
                for t in range(NT):
                    dve.wait_ge(downed, t + 1)
                    dve.tensor_tensor(c.X[:, t, :], c.X[:, t, :], up[t % 4][:], ALU.add).then_inc(added, 1)


def capacity_gates(nc, c, w, gate_t, ahead):
    NE, CAP = 8, math.ceil(1.25 * N / 8)
    with Stage(nc, "cg") as s:
        top = s.sb("top", [P, NT])
        probs = s.sb("probs", [P, NT, NE])
        sums = s.sb("sums", [P, NT])
        best = s.sb("best", [P, NT, NE])
        best_at = s.sb("best_at", [P, NT, NE], U32)
        at = s.sb("at", [P, NT, 2])
        pick = s.sb("pick", [P, 2, NT, NE])
        taken = s.sb("taken", [P, NT, NE])
        place = s.sb("place", [P, NT, NE])
        carry = s.sb("carry", [P, NT, NE])
        gate = s.sb("gate", [P, NT, NE])
        logits, earlier, all_of = (s.ps(n, [P, NT * NE]) for n in ("logits", "earlier", "all_of"))
        turn = [s.ps(f"turn{k}", [NE, D]) for k in range(2)]
        loaded, scored, cut, raised, chosen, counted, gates, turned, chain = (s.sem(n) for n in (
            "loaded", "scored", "cut", "raised", "chosen", "counted", "gates", "turned", "chain"))
        kept = s.sem("kept")

        def flat(t):
            return t[:].rearrange("p t e -> p (t e)")

        def over(t):
            return t.unsqueeze(2).to_broadcast([P, NT, NE])

        with nc.Block() as block:
            @block.sync
            def _(sp):
                ahead.start(sp, loaded)
                ahead.finish(sp, loaded)

            @block.tensor
            def _(pe):
                for t in range(NT):
                    for k in range(DC):
                        last = pe.matmul(logits[:, t * NE:(t + 1) * NE], c.XLT[:, k, t * P:(t + 1) * P], w[:, k, :],
                                         start=k == 0, stop=k == DC - 1)
                last.then_inc(scored, 1)
                pe.wait_ge(chosen, 1)
                pe.matmul(earlier[:], c.before[:], flat(taken), start=True, stop=True)
                pe.matmul(all_of[:], c.ones[:], flat(taken), start=True, stop=True).then_inc(counted, 1)
                pe.wait_ge(gates, 1)
                for t in range(NT):
                    last = pe.transpose(turn[t // 4][:, (t % 4) * P:(t % 4 + 1) * P], gate[:, t, :], c.ident[:])
                last.then_inc(turned, 1)

            @block.scalar
            def _(act):
                act.wait_ge(cut, 1)
                act.activation(probs[:], probs[:], ACT.Exp).then_inc(raised, 1)

            @block.vector
            def _(dve):
                links = [0]

                def link(ins):
                    links[0] += 1
                    ins.then_inc(chain, 1)
                    dve.wait_ge(chain, links[0])

                scores = logits[:].rearrange("p (t e) -> p t e", e=NE)
                dve.wait_ge(scored, 1)
                link(dve.tensor_reduce(top[:], scores, AX_X, ALU.max))
                dve.tensor_tensor(probs[:], scores, over(top[:]), ALU.subtract).then_inc(cut, 1)
                dve.wait_ge(raised, 1)
                link(dve.tensor_reduce(sums[:], probs[:], AX_X, ALU.add))
                link(dve.reciprocal(sums[:], sums[:]))
                link(dve.tensor_tensor(probs[:], probs[:], over(sums[:]), ALU.mult))
                for t in range(NT):
                    last = dve.max(best[:, t, :], probs[:, t, :])
                link(last)
                for t in range(NT):
                    last = dve.max_index(best_at[:, t, :], best[:, t, :], probs[:, t, :])
                link(last)
                link(dve.tensor_copy(at[:], best_at[:, :, 0:2]))
                for k in range(2):
                    last = dve.tensor_tensor(pick[:, k], c.iota[:, 0:NE].unsqueeze(1).to_broadcast([P, NT, NE]),
                                             over(at[:, :, k]), ALU.is_equal)
                link(last)
                dve.tensor_tensor(taken[:], pick[:, 0], pick[:, 1], ALU.add).then_inc(chosen, 1)
                link(dve.tensor_tensor(sums[:], best[:, :, 0], best[:, :, 1], ALU.add))
                link(dve.reciprocal(sums[:], sums[:]))
                dve.wait_ge(chosen, 1)
                link(dve.tensor_tensor(gate[:], taken[:], probs[:], ALU.mult))
                link(dve.tensor_tensor(gate[:], gate[:], over(sums[:]), ALU.mult))
                link(dve.memset(carry[:, 0, :], 0.0))
                dve.wait_ge(counted, 1)
                totals = all_of[:].rearrange("p (t e) -> p t e", e=NE)
                for t in range(1, NT):
                    link(dve.tensor_tensor(carry[:, t, :], carry[:, t - 1, :], totals[:, t - 1, :], ALU.add))
                link(dve.tensor_tensor(flat(place), flat(carry), earlier[:], ALU.add))
                dve.scalar_tensor_tensor(out=flat(gate), in0=flat(place), scalar=float(CAP), in1=flat(gate),
                                         op0=ALU.is_lt, op1=ALU.mult).then_inc(gates, 1)
                dve.wait_ge(turned, 1)
                for k in range(2):
                    dve.tensor_copy(gate_t[:, k * D:(k + 1) * D], turn[k][:]).then_inc(kept, 1)


def choice_gates(nc, c, w, gate_t, ahead):
    NE, CAP = 8, 64
    with Stage(nc, "eg") as s:
        top = s.sb("top", [NE, 1])
        sums = s.sb("sums", [NE, 1])
        probs = s.sb("probs", [NE, N])
        left = s.sb("left", [NE, N])
        best = s.sb("best", [NE, CAP])
        logits = s.ps("logits", [NE, N])
        loaded, scored, cut, raised, chain = (s.sem(n) for n in ("loaded", "scored", "cut", "raised", "chain"))
        with nc.Block() as block:
            @block.sync
            def _(sp):
                ahead.start(sp, loaded)
                ahead.finish(sp, loaded)

            @block.tensor
            def _(pe):
                for n in range(2):
                    for k in range(DC):
                        last = pe.matmul(logits[:, n * D:(n + 1) * D], w[:, k, :], c.XLT[:, k, n * D:(n + 1) * D],
                                         start=k == 0, stop=k == DC - 1)
                last.then_inc(scored, 1)

            @block.scalar
            def _(act):
                act.wait_ge(cut, 1)
                act.activation(probs[:], logits[:], ACT.Exp, bias=top[:]).then_inc(raised, 1)

            @block.vector
            def _(dve):
                links = [0]

                def link(ins):
                    links[0] += 1
                    ins.then_inc(chain, 1)
                    dve.wait_ge(chain, links[0])

                dve.wait_ge(scored, 1)
                link(dve.tensor_reduce(top[:], logits[:], AX_X, ALU.max))
                dve.tensor_scalar(top[:], top[:], -1.0, None, ALU.mult).then_inc(cut, 1)
                dve.wait_ge(raised, 1)
                link(dve.tensor_reduce(sums[:], probs[:], AX_X, ALU.add))
                link(dve.reciprocal(sums[:], sums[:]))
                link(dve.tensor_scalar(probs[:], probs[:], sums[:], None, ALU.mult))
                for k in range(CAP // 8):
                    now = probs if k == 0 else left
                    link(dve.max(best[:, 8 * k:8 * k + 8], now[:]))
                    link(dve.match_replace(left[:], best[:, 8 * k:8 * k + 8], now[:], -1.0))
                link(dve.scalar_tensor_tensor(out=gate_t[:], in0=left[:], scalar=0.0, in1=probs[:],
                                              op0=ALU.is_lt, op1=ALU.mult))


def sage_update(nc, c, w, bias, agg, own):
    with Stage(nc, "l3u") as s:
        rdeg = s.sb("rdeg", [P, NT])
        agg_t = s.sb("agg_t", [P, DC, N])
        turn = [s.ps(f"turn{k}") for k in range(2)]
        out = [s.ps(f"out{k}") for k in range(4)]
        shifted, mean, turned, taken, product, biased, clipped, chain = (s.sem(n) for n in (
            "shifted", "mean", "turned", "taken", "product", "biased", "clipped", "chain"))
        with nc.Block() as block:
            @block.gpsimd
            def _(pool):
                for t in range(NT):
                    pool.tensor_tensor(own[:, t, :], own[:, t, :], bias[:], ALU.add).then_inc(shifted, 1)

            @block.tensor
            def _(pe):
                for t in range(NT):
                    pe.wait_ge(mean, t + 1)
                    if t >= 2:
                        pe.wait_ge(taken, t - 1)
                    for k in range(DC):
                        last = pe.transpose(turn[t % 2][:, k * P:(k + 1) * P], agg[:, t, k * P:(k + 1) * P], c.ident[:])
                    last.then_inc(turned, 1)
                for t in range(NT):
                    pe.wait_ge(taken, t + 1)
                    if t >= 4:
                        pe.wait_ge(biased, t - 3)
                    for k in range(DC):
                        last = pe.matmul(out[t % 4][:], agg_t[:, k, t * P:(t + 1) * P], w[:, DC + k, :],
                                         start=k == 0, stop=k == DC - 1)
                    last.then_inc(product, 1)

            @block.scalar
            def _(act):
                for t in range(NT):
                    act.wait_ge(turned, t + 1)
                    act.copy(agg_t[:, :, t * P:(t + 1) * P],
                             turn[t % 2][:, :].rearrange("p (k n) -> p k n", k=DC)).then_inc(taken, 1)

            @block.vector
            def _(dve):
                dve.tensor_scalar(rdeg[:], c.degree[:, 1, :], 1.0, None, ALU.max).then_inc(chain, 1)
                dve.wait_ge(chain, 1)
                dve.reciprocal(rdeg[:], rdeg[:]).then_inc(chain, 1)
                dve.wait_ge(chain, 2)
                for t in range(NT):
                    dve.tensor_scalar(agg[:, t, :], agg[:, t, :], rdeg[:, t:t + 1], None, ALU.mult).then_inc(mean, 1)
                for t in range(NT):
                    dve.wait_ge(product, t + 1)
                    dve.wait_ge(turned, t + 1)
                    dve.wait_ge(shifted, t + 1)
                    dve.tensor_tensor(agg[:, t, :], out[t % 4][:], own[:, t, :], ALU.add).then_inc(biased, 1)
                    dve.wait_ge(biased, t + 1)
                    dve.scalar_tensor_tensor(out=c.X[:, t, :], in0=agg[:, t, :], scalar=0.0, in1=c.X[:, t, :],
                                             op0=ALU.max, op1=ALU.add).then_inc(clipped, 1)


def one_expert(nc, c, a, wg, bg):
    NE = 16
    with Stage(nc, "l3e") as s:
        mean = s.sb("mean", [P, DC])
        mean_w = s.sb("mean_w", [P, DC, P])
        scores = s.sb("scores", [P, NE])
        top = s.sb("top", [P, 8])
        top_at = s.sb("top_at", [P, 8], U32)
        low = s.sb("low", [P, 1])
        raised_s = s.sb("raised_s", [P, NE])
        sums = s.sb("sums", [P, 1])
        gate = s.sb("gate", [P, 1])
        which = s.sb("which", [P, 1])
        line = s.sb("line", [P, DC])
        row_f = s.sb("row_f", [P, DC])
        row_i = s.sb("row_i", [P, DC], I32)
        which_i = s.sb("which_i", [P, 1], I32)
        w = s.sb("w", [P, DC, D])
        bias = s.sb("bias", [P, D])
        logits = s.ps("logits", [P, NE])
        out = [s.ps(f"out{k}") for k in range(4)]
        (w_in, base), = c.landings.take([DC + 1])
        spread, scored, cut, raised, picked, lined, product, biased, added, chain = (s.sem(n) for n in (
            "spread", "scored", "cut", "raised", "picked", "lined", "product", "biased", "added",
            "chain"))
        with nc.Block() as block:
            @block.gpsimd
            def _(pool):
                pool.iota(line[:], [[P, DC]], base=0, channel_multiplier=1,
                          allow_small_or_imprecise_dtypes=True).then_inc(lined, 1)
                pool.wait_ge(picked, 1)
                for k in range(DC):
                    pool.indirect_dma_start(w[:, k, :], None, a["L3_ffn_We_rows"],
                                            bass.IndirectOffsetOnAxis(ap=row_i[:, k:k + 1], axis=0)).then_inc(w_in, 16)
                pool.indirect_dma_start(bias[:], None, a["L3_ffn_be"],
                                        bass.IndirectOffsetOnAxis(ap=which_i[:], axis=0)).then_inc(w_in, 16)

            @block.tensor
            def _(pe):
                pe.wait_ge(spread, 1)
                for k in range(DC):
                    last = pe.matmul(logits[:], mean_w[:, k, :], wg[:, k, :], start=k == 0, stop=k == DC - 1)
                last.then_inc(scored, 1)
                pe.wait_ge(w_in, base + 16 * (DC + 1))
                for t in range(NT):
                    if t >= 4:
                        pe.wait_ge(biased, t - 3)
                    for k in range(DC):
                        last = pe.matmul(out[t % 4][:], c.XLT[:, k, t * P:(t + 1) * P], w[:, k, :],
                                         start=k == 0, stop=k == DC - 1)
                    last.then_inc(product, 1)

            @block.scalar
            def _(act):
                act.wait_ge(cut, 1)
                act.activation(raised_s[:], scores[:], ACT.Exp, bias=low[:]).then_inc(raised, 1)

            @block.vector
            def _(dve):
                links = [0]

                def link(ins):
                    links[0] += 1
                    ins.then_inc(chain, 1)
                    dve.wait_ge(chain, links[0])

                link(dve.tensor_reduce(mean[:], c.XLT[:], AX_X, ALU.add))
                link(dve.tensor_scalar(mean[:], mean[:], 1.0 / N, None, ALU.mult))
                dve.tensor_copy(mean_w[:], mean[:].unsqueeze(2).to_broadcast([P, DC, P])).then_inc(spread, 1)
                dve.wait_ge(scored, 1)
                link(dve.tensor_tensor(scores[:], logits[:], bg[:], ALU.add))
                link(dve.max(top[:], scores[:]))
                dve.tensor_scalar(low[:], top[:, 0:1], -1.0, None, ALU.mult).then_inc(cut, 1)
                link(dve.max_index(top_at[:], top[:], scores[:]))
                link(dve.tensor_copy(which[:], top_at[:, 0:1]))
                dve.wait_ge(lined, 1)
                dve.tensor_copy(which_i[:], which[:])
                link(dve.tensor_scalar(which[:], which[:], float(D), None, ALU.mult))
                link(dve.tensor_scalar(row_f[:], line[:], which[:], None, ALU.add))
                dve.tensor_copy(row_i[:], row_f[:]).then_inc(picked, 1)
                dve.wait_ge(raised, 1)
                link(dve.tensor_reduce(sums[:], raised_s[:], AX_X, ALU.add))
                link(dve.reciprocal(gate[:], sums[:]))
                dve.wait_ge(w_in, base + 16 * (DC + 1))
                for t in range(NT):
                    dve.wait_ge(product, t + 1)
                    dve.tensor_tensor(c.XL[:, t, :], out[t % 4][:], bias[:], ALU.add).then_inc(biased, 1)
                    dve.wait_ge(biased, t + 1)
                    dve.scalar_tensor_tensor(out=c.X[:, t, :], in0=c.XL[:, t, :], scalar=gate[:], in1=c.X[:, t, :],
                                             op0=ALU.mult, op1=ALU.add).then_inc(added, 1)



HEADS, NKEYS, TOPK = 8, 256, 8
BANKS = 4


def memory_queries(nc, c, w, bias, q, ahead):
    with Stage(nc, "m0q") as s:
        out = [s.ps(f"out{k}") for k in range(4)]
        loaded, product, biased = s.sem("loaded"), s.sem("product"), s.sem("biased")
        work = [(h, n) for h in range(HEADS) for n in range(2)]
        with nc.Block() as block:
            @block.sync
            def _(sp):
                ahead.start(sp, loaded)
                ahead.finish(sp, loaded)

            @block.tensor
            def _(pe):
                for i, (h, n) in enumerate(work):
                    if i >= 4:
                        pe.wait_ge(biased, i - 3)
                    for k in range(DC):
                        last = pe.matmul(out[i % 4][:], w[:, k, h * P:(h + 1) * P], c.XLT[:, k, n * D:(n + 1) * D],
                                         start=k == 0, stop=k == DC - 1)
                    last.then_inc(product, 1)

            @block.scalar
            def _(act):
                for i, (h, n) in enumerate(work):
                    act.wait_ge(product, i + 1)
                    act.activation(q[:, h, n * D:(n + 1) * D], out[i % 4][:], ACT.Identity,
                                   bias=bias[:, h:h + 1]).then_inc(biased, 1)


def memory_lookup(nc, c, a, q, keys):
    with Stage(nc, "m0") as s:
        query = [s.sb(f"query{k}", [P, P]) for k in range(BANKS)]
        vals = s.sb("best", [P, HEADS, 2, TOPK])
        vals_at = s.sb("best_at", [P, HEADS, 2, TOPK], U32)
        key_no = s.sb("key_no", [P, HEADS, 2, TOPK])
        pairs = s.sb("pairs", [P, HEADS, TOPK, TOPK])
        score = s.sb("score", [P, HEADS, TOPK])
        pair_at = s.sb("pair_at", [P, HEADS, TOPK], U32)
        half_at = s.sb("half_at", [P, 2, HEADS * TOPK], U32)
        half_no = s.sb("half_no", [P, 2, HEADS * TOPK])
        same = s.sb("same", [P, 2, HEADS * TOPK, TOPK])
        chosen = s.sb("chosen", [P, 2, HEADS * TOPK])
        memory = [s.sb(f"memory{u}", [P, HEADS * TOPK], I32) for u in range(2)]
        share = [s.sb(f"share{u}", [P, HEADS, TOPK]) for u in range(2)]
        norms = s.sb("norms", [P, HEADS])
        rows = [s.sb(f"rows{k}", [P, 2 * D]) for k in range(ROWS)]
        inner = [s.sb(f"inner{k}", [P, PART]) for k in range(ROWS // PART)]
        value = [s.sb(f"value{k}", [P, PART]) for k in range(ROWS // PART)]
        diag = [s.sb(f"diag{k}", [P, P]) for k in range(ROWS)]
        scores = [s.ps(f"scores{k}") for k in range(BANKS)]
        out = [s.ps(f"out{u}") for u in range(2)]
        queried, scored, maxed, ranked = (s.sem(n) for n in ("queried", "scored", "maxed", "ranked"))
        steps, indexed, issued, shifted, raised = (s.sem(n) for n in (
            "steps", "indexed", "issued", "shifted", "raised"))
        dotted, valued, spread, used, added = (s.sem(n) for n in ("dotted", "valued", "spread", "used", "added"))
        waited, scattered, reloaded = s.sem("waited"), s.sem("scattered_ok"), s.sem("reloaded")
        scatter = Scatter(nc, c, s, 1, c.loose_d, c.by_dst, RD)
        landed = c.landings.take([NT * HEADS * TOPK // ROWS] * ROWS)
        STEPS = 15
        PAIRS = HEADS // 2
        PARTS = TOPK // PART

        def bank(h, k):
            return scores[h % BANKS // 2 * 2 + k][:, h % 2 * NKEYS:(h % 2 + 1) * NKEYS]

        def over_tiles(engine, tile, before=None):
            with engine.Fori(0, NT // 2 - 1) as i:
                for u in range(2):
                    tile(i * 2 + u, u, True)
            tile(NT - 2, 0, True)
            tile(NT - 1, 1, False)

        with nc.Block() as block:
            @block.sync
            def _(sp):
                sp.wait_ge(scattered, 1)
                sp.dma_start(c.rec_d[:], c.by_dst.rearrange("(p c) f -> p c f", p=P)).then_inc(reloaded, 16)
                sp.wait_ge(reloaded, 16)

            @block.scalar
            def _(act):
                def place_queries(T, p):
                    act.wait_ge(scored, T * PAIRS + p + 1)
                    for h in (2 * p, 2 * p + 1):
                        act.copy(query[h % BANKS][:], q[:, h, bass.ds(T * P, P)]).then_inc(queried, 1)

                def raise_scores(T):
                    act.wait_ge(shifted, T + 1)
                    act.activation(score[:], score[:], ACT.Exp).then_inc(raised, 1)

                def spread_values(T, h):
                    for part in range(PARTS):
                        done = (T * HEADS + h) * PARTS + part
                        act.wait_ge(valued, done + 1)
                        act.wait_ge(used, done * PART + PART)
                        for k in range(PART):
                            slot = h % 2 * TOPK + part * PART + k
                            act.mul(diag[slot][:], c.ident[:], value[slot // PART][:, k:k + 1]).then_inc(spread, 1)

                def tile(T, u, more):
                    for h in range(HEADS):
                        if more and h < PAIRS:
                            place_queries(T + 1, h)
                        spread_values(T, h)
                        if more and h == PAIRS + 1:
                            raise_scores(T + 1)

                for p in range(PAIRS):
                    place_queries(0, p)
                raise_scores(0)
                over_tiles(act, tile)

            @block.tensor
            def _(pe):
                def score_pair(T, p):
                    pe.wait_ge(queried, (T * PAIRS + p + 1) * 2)
                    pe.wait_ge(ranked, T * PAIRS + p + 1)
                    for h in (2 * p, 2 * p + 1):
                        for k in range(2):
                            half = slice(k * 64, (k + 1) * 64)
                            last = pe.matmul(bank(h, k), query[h % BANKS][half, :],
                                             keys[half, h, :], start=True, stop=True)
                    last.then_inc(scored, 1)

                def sum_up(T, u, h):
                    if h == 0:
                        pe.wait_ge(added, T + 1)
                    for k in range(TOPK):
                        pe.wait_ge(spread, ROWS + (T * HEADS + h) * TOPK + k + 1)
                        slot = h % 2 * TOPK + k
                        pe.matmul(out[u][:], diag[slot][:], rows[slot][:, D:2 * D],
                                  start=h == 0 and k == 0, stop=h == HEADS - 1 and k == TOPK - 1).then_inc(used, 1)

                def tile(T, u, more):
                    for h in range(HEADS):
                        if more and h < PAIRS:
                            score_pair(T + 1, h)
                        sum_up(T, u, h)

                for p in range(PAIRS):
                    score_pair(0, p)
                over_tiles(pe, tile)

            @block.gpsimd
            def _(pool):
                def tile(T, u, more):
                    pool.wait_ge(indexed, T + 1)
                    pool.sem_inc(issued, 1)
                    for h in range(HEADS):
                        for first in range(0, TOPK, FREED):
                            pool.wait_ge(used, (T * HEADS + h) * TOPK + first + FREED)
                            pool.sem_inc(issued, 1)
                            for k in range(first, first + FREED):
                                slot = h % 2 * TOPK + k
                                pool.indirect_dma_start(
                                    rows[slot][:], None, a["L0_ffn_w_rows"],
                                    bass.IndirectOffsetOnAxis(ap=memory[u][:, h * TOPK + k:h * TOPK + k + 1], axis=0))\
                                    .then_inc(landed[slot][0], 16)
                        if h == 0:
                            scatter.copy_slots(pool, T, u)
                            scatter.copy_recs(pool, pool.tensor_copy, T, u)
                        scatter.send(pool, T, u, range(GROUP)[3 * h:3 * h + 3])

                over_tiles(pool, tile)
                scatter.finish(pool, scattered)

            @block.vector
            def _(dve):
                dve.sem_inc(scored, 2)
                dve.sem_inc(ranked, 2)
                dve.sem_inc(spread, ROWS)
                dve.sem_inc(used, ROWS)
                dve.sem_inc(added, 2)

                def rank(T, p):
                    heads = [(h, k) for h in (2 * p, 2 * p + 1) for k in range(2)]
                    dve.wait_ge(scored, 2 + T * PAIRS + p + 1)
                    dve.sem_inc(waited, 1)
                    for h, k in heads:
                        last = dve.max(vals[:, h, k, :], bank(h, k))
                    last.then_inc(maxed, 1)
                    dve.wait_ge(maxed, T * PAIRS + p + 1)
                    dve.sem_inc(waited, 1)
                    for h, k in heads:
                        last = dve.max_index(vals_at[:, h, k, :], vals[:, h, k, :], bank(h, k))
                    last.then_inc(ranked, 1)

                def choose(T, u):
                    done = [0]

                    def link(ins):
                        done[0] += 1
                        ins.then_inc(steps, 1)
                        dve.wait_ge(steps, T * STEPS + done[0])

                    full = [P, HEADS, TOPK, TOPK]
                    dve.wait_ge(ranked, 2 + (T + 1) * PAIRS)
                    dve.tensor_copy(key_no[:], vals_at[:])
                    link(dve.tensor_tensor(pairs[:], vals[:, :, 0, :].unsqueeze(3).to_broadcast(full),
                                           vals[:, :, 1, :].unsqueeze(2).to_broadcast(full), ALU.add))
                    dve.sem_inc(waited, 1)
                    for h in range(HEADS):
                        last = dve.max(score[:, h, :], pairs[:, h].rearrange("p a b -> p (a b)"))
                    link(last)
                    dve.sem_inc(waited, 1)
                    for h in range(HEADS):
                        last = dve.max_index(pair_at[:, h, :], score[:, h, :], pairs[:, h].rearrange("p a b -> p (a b)"))
                    link(last)
                    at = pair_at[:].rearrange("p h k -> p (h k)")
                    dve.tensor_scalar(half_at[:, 0, :], at, 3, None, ALU.logical_shift_right)
                    link(dve.tensor_scalar(half_at[:, 1, :], at, TOPK - 1, None, ALU.bitwise_and))
                    link(dve.tensor_copy(norms[:], score[:, :, 0]))
                    dve.tensor_tensor(score[:], score[:], norms[:].unsqueeze(2).to_broadcast([P, HEADS, TOPK]),
                                      ALU.subtract).then_inc(shifted, 1)
                    link(dve.tensor_copy(half_no[:], half_at[:]))
                    wide = [P, 2 * HEADS * TOPK, TOPK]
                    link(dve.tensor_tensor(same[:].rearrange("p a n m -> p (a n) m"),
                                           c.iota[:, 0:TOPK].unsqueeze(1).to_broadcast(wide),
                                           half_no[:].rearrange("p a n -> p (a n)").unsqueeze(2).to_broadcast(wide),
                                           ALU.is_equal))
                    for k in range(2):
                        part = same[:, k].rearrange("p (h n) m -> p h n m", h=HEADS)
                        last = dve.tensor_tensor(part, part, key_no[:, :, k, :].unsqueeze(2).to_broadcast(full), ALU.mult)
                    link(last)
                    link(dve.tensor_reduce(chosen[:], same[:], AX_X, ALU.add))
                    dve.scalar_tensor_tensor(out=memory[u][:], in0=chosen[:, 0, :], scalar=float(NKEYS),
                                             in1=chosen[:, 1, :], op0=ALU.mult, op1=ALU.add).then_inc(indexed, 1)
                    for _ in range(STEPS - 4 - done[0]):
                        dve.sem_inc(steps, 1)
                        done[0] += 1

                def softmax(T, u):
                    def link(n, ins):
                        ins.then_inc(steps, 1)
                        dve.wait_ge(steps, T * STEPS + n)

                    dve.wait_ge(raised, T + 1)
                    link(STEPS - 3, dve.tensor_reduce(norms[:], score[:], AX_X, ALU.add))
                    link(STEPS - 2, dve.reciprocal(norms[:], norms[:]))
                    link(STEPS - 1, dve.tensor_tensor(share[u][:], score[:],
                                                      norms[:].unsqueeze(2).to_broadcast([P, HEADS, TOPK]), ALU.mult))
                    dve.sem_inc(steps, 1)

                def weigh(T, u, h):
                    for part in range(PARTS):
                        done = (T * HEADS + h) * PARTS + part
                        first = h % 2 * TOPK + part * PART
                        place = first // PART
                        for k in range(PART):
                            dve.wait_ge(landed[first + k][0],
                                        landed[first + k][1] + (T * (HEADS // 2) + h // 2 + 1) * 16)
                            last = dve.scalar_tensor_tensor(out=rows[first + k][:, 0:D], in0=c.XL[:, bass.ds(T, 1), :]
                                                            .rearrange("p a d -> p (a d)"), scalar=1.0,
                                                            in1=rows[first + k][:, 0:D], op0=ALU.mult, op1=ALU.mult,
                                                            accum_out=inner[place][:, k:k + 1])
                        last.then_inc(dotted, 1)
                        dve.wait_ge(dotted, done + 1)
                        dve.wait_ge(spread, done * PART + PART)
                        dve.scalar_tensor_tensor(out=value[place][:], in0=inner[place][:], scalar=0.0,
                                                 in1=share[u][:, h, part * PART:(part + 1) * PART],
                                                 op0=ALU.max, op1=ALU.mult).then_inc(valued, 1)

                def add(T, u):
                    dve.wait_ge(used, ROWS + (T + 1) * HEADS * TOPK)
                    there = c.X[:, bass.ds(T, 1), :].rearrange("p a d -> p (a d)")
                    dve.tensor_tensor(there, there, out[u][:], ALU.add).then_inc(added, 1)

                def tile(T, u, more):
                    for h in range(HEADS):
                        if more and 1 <= h <= PAIRS:
                            rank(T + 1, h - 1)
                        if more and h == PAIRS + 1:
                            choose(T + 1, 1 - u)
                        weigh(T, u, h)
                        if more and h == PAIRS + 1:
                            softmax(T + 1, 1 - u)
                    add(T, u)

                for p in range(PAIRS):
                    rank(0, p)
                choose(0, 0)
                softmax(0, 0)
                over_tiles(dve, tile)



LOG2 = math.log(2.0)
Y0 = 1.0 / math.sqrt(4.0 * math.pi)
Y1 = math.sqrt(3.0 / (4.0 * math.pi))
QUAD = 4
BODY = 16
MADE = 4
AHEAD = 3


def vector_node_rows(nc, c, w):
    with Stage(nc, "t0") as s:
        row = [s.sb(f"row{k}", [P, D]) for k in range(4)]
        out = [s.ps(f"out{k}") for k in range(4)]
        product, scaled = s.sem("product"), s.sem("scaled")
        stored = [s.sem(f"stored{k}") for k in range(4)]
        with nc.Block() as block:
            @block.sync
            def _(sp):
                for t in range(NT):
                    sp.wait_ge(scaled, t + 1)
                    sp.dma_start(c.rows[t * P:(t + 1) * P, :], row[t % 4][:]).then_inc(stored[t % 4], 16)
                for k in range(4):
                    sp.wait_ge(stored[k], 16 * (NT // 4))

            @block.tensor
            def _(pe):
                for t in range(NT):
                    if t >= 4:
                        pe.wait_ge(scaled, t - 3)
                    for k in range(DC):
                        last = pe.matmul(out[t % 4][:, k * P:(k + 1) * P], c.XLT[:, k, t * P:(t + 1) * P],
                                         w[:, min(k, 1), :], start=True, stop=True)
                    last.then_inc(product, 1)

            @block.scalar
            def _(act):
                for t in range(NT):
                    act.wait_ge(product, t + 1)
                    if t >= 4:
                        act.wait_ge(stored[t % 4], 16 * (t // 4))
                    act.mul(row[t % 4][:], out[t % 4][:], 1.0 / math.sqrt(P)).then_inc(scaled, 1)


def vector_messages(nc, c, a, total, ahead):
    Q, SA, SB, VA, VB = (k * P for k in (0, 1, 2, 3, 6))
    QUADS = BODY // QUAD
    with Stage(nc, "t2") as s:
        wf1 = s.sb("wf1", [RBF, P])
        bf1 = s.sb("bf1", [P, 1])
        wf2 = s.sb("wf2", [P, D])
        bf2 = s.sb("bf2", [1, D])
        bf2_part = s.sb("bf2_part", [1, 3, D], BF16)
        bf2_rows = s.sb("bf2_rows", [3, D], BF16)
        ones = s.sb("ones", [3, P], BF16)
        attr = [s.sb(f"attr{k}", [P, QUAD, RBF]) for k in range(2)]
        attr_t = s.sb("attr_t", [RBF, D])
        size = [s.sb(f"size{b}", [P, D]) for b in range(QUADS)]
        above = [s.sb(f"above{b}", [P, D]) for b in range(QUADS)]
        hid = [s.sb(f"hid{b}", [P, D]) for b in range(QUADS)]
        at = [s.sb(f"at{h}", [P, QUAD], I32) for h in range(2)]
        rows = [s.sb(f"rows{j}", [P, D]) for j in range(RING)]
        hot = [s.sb(f"hot{j}", [P, P]) for j in range(MADE)]
        filt = [s.sb(f"filt{j}", [P, P]) for j in range(MADE)]
        along = [s.sb(f"along{j}", [P, P]) for j in range(MADE)]
        mess = [s.sb(f"mess{j}", [P, 9 * P]) for j in range(MADE)]
        turn, pre = s.ps("turn"), s.ps("pre")
        fps = [s.ps(f"fps{j}") for j in range(2)]
        part = [s.ps(f"part{j}", [P, 2 * D]) for j in range(2)]
        w_in, attr_ok, turned, attr_t_ok, pre_ok, sized, logged, aboved, hid_ok = (s.sem(n) for n in (
            "w_in", "attr_ok", "turned", "attr_t_ok", "pre_ok", "sized", "logged", "aboved", "hid_ok"))
        placed, issued, marked, filtered, copied = (s.sem(n) for n in (
            "placed", "issued", "marked", "filtered", "copied"))
        landed = c.landings.take([CH // RING] * RING)
        dots, mixed, scaled, outer, vectored, begun, summed, added, raised, waited = (s.sem(n) for n in (
            "dots", "mixed", "scaled", "outer", "vectored", "begun", "summed", "added", "raised", "waited"))
        split, parted, loaded = s.sem("split"), s.sem("parted"), s.sem("loaded")
        flat = total[:, :, :].rearrange("p t d -> p (t d)")

        def rows_in(i, j):
            return landed[j % RING][1] + (i * (BODY // RING) + j // RING + 1) * 16

        def over_bodies(engine, body):
            with engine.Fori(0, CH // BODY - 1) as i:
                body(i, True)
            body(CH // BODY - 1, False)

        with nc.Block() as block:
            @block.sync
            def _(sp):
                sp.dma_start(wf1[:], a["L2_gnn_Wf1"]).then_inc(w_in, 16)
                sp.dma_start(bf1[:], a["L2_gnn_bf1_t"]).then_inc(w_in, 16)
                sp.dma_start(wf2[:], a["L2_gnn_Wf2_t"]).then_inc(w_in, 16)
                sp.dma_start(bf2[:], a["L2_gnn_bf2_t"].partition_broadcast(1)).then_inc(w_in, 16)
                sp.wait_ge(split, 6)
                for k in range(3):
                    sp.dma_start(bf2_rows[k:k + 1, :], bf2_part[:, k, :]).then_inc(parted, 16)
                sp.wait_ge(parted, 48)
                ahead.start(sp, loaded)
                ahead.finish(sp, loaded)

            @block.gpsimd
            def _(pool):
                def indices(g, h):
                    pool.wait_ge(summed, g * QUAD + 1)
                    pool.tensor_copy(at[h][:], c.rec_s[:, bass.ds(g * QUAD, QUAD), S_OTHER])\
                        .then_inc(placed, 1)

                def gather(g, h, k):
                    pool.wait_ge(placed, g + 1)
                    pool.wait_ge(summed, g * QUAD + k + 1)
                    pool.sem_inc(issued, 1)
                    pool.indirect_dma_start(rows[h * QUAD + k][:], None, c.rows[0:N, :],
                                            bass.IndirectOffsetOnAxis(ap=at[h][:, k:k + 1], axis=0))\
                        .then_inc(landed[h * QUAD + k][0], 16)

                def vectors(i, j):
                    k, slot = j % MADE, j % RING
                    pool.wait_ge(copied, i * BODY + j + 1)
                    pool.wait_ge(landed[slot][0], rows_in(i, j))
                    pool.tensor_tensor(mess[k][:, VB:VB + 3 * P].rearrange("p (a f) -> p a f", a=3),
                                       rows[slot][:, P:4 * P].rearrange("p (a f) -> p a f", a=3),
                                       filt[k][:].unsqueeze(1).to_broadcast([P, 3, P]),
                                       ALU.mult).then_inc(vectored, 1)

                def body(i, more):
                    for j in range(BODY):
                        b = j // QUAD + 1
                        if more or b < QUADS:
                            if j % QUAD == 0:
                                indices(i * QUADS + b, b % 2)
                            gather(i * QUADS + b, b % 2, j % QUAD)
                        vectors(i, j)

                indices(0, 0)
                for k in range(QUAD):
                    gather(0, 0, k)
                over_bodies(pool, body)

            @block.scalar
            def _(act):
                def attributes(g, b):
                    act.wait_ge(turned, g + 1)
                    act.sem_inc(waited, 1)
                    act.copy(attr[b % 2][:], c.rec_s[:, bass.ds(g * QUAD, QUAD), S_RBF:S_RBF + RBF])\
                        .then_inc(attr_ok, 1)

                def attributes_turned(g):
                    act.wait_ge(turned, 2 + g + 1)
                    act.copy(attr_t[:], turn[0:RBF, :]).then_inc(attr_t_ok, 1)

                def hidden(g, b):
                    act.wait_ge(pre_ok, g + 1)
                    act.wait_ge(hid_ok, g + 1)
                    act.activation(size[b][:], pre[:], ACT.Abs, bias=bf1[:]).then_inc(sized, 1)
                    act.activation(above[b][:], pre[:], ACT.Relu, bias=bf1[:]).then_inc(aboved, 1)
                    act.wait_ge(sized, g + 1)
                    act.activation(size[b][:], size[b][:], ACT.Exp, scale=-1.0).then_inc(raised, 1)

                def logarithm(g, b):
                    act.wait_ge(raised, g + 1)
                    act.activation(size[b][:], size[b][:], ACT.Ln, bias=c.ones[:, 0:1]).then_inc(logged, 1)

                def first_product(i, j):
                    slot = j % RING
                    act.wait_ge(outer, i * BODY + j + 1)
                    act.wait_ge(landed[slot][0], rows_in(i, j))
                    act.sem_inc(waited, 1)
                    act.mul(along[j % MADE][:], rows[slot][:, P:2 * P],
                            c.rec_s[:, bass.ds(i * BODY + j, 1), S_U:S_U + 1].rearrange("p a b -> p (a b)"))\
                        .then_inc(begun, 1)

                def scale(q, j):
                    k = j % MADE
                    act.wait_ge(mixed, q + 1)
                    act.sem_inc(waited, 1)
                    for i in range(3):
                        last = act.mul(mess[k][:, VA + i * P:VA + (i + 1) * P], mess[k][:, Q:Q + P],
                                       c.rec_s[:, bass.ds(q, 1), S_U + i:S_U + i + 1].rearrange("p a b -> p (a b)"))
                    last.then_inc(scaled, 1)

                def body(i, more):
                    for j in range(BODY):
                        if j < BODY - 1:
                            first_product(i, j + 1)
                        elif more:
                            first_product(i + 1, 0)
                        scale(i * BODY + j, j)
                        if more and j < AHEAD * QUADS:
                            b = j // AHEAD
                            g = (i + 1) * QUADS + b
                            if j % AHEAD == 0:
                                attributes(g, b)
                            elif j % AHEAD == 1:
                                attributes_turned(g)
                            else:
                                hidden(g, b)
                        elif more:
                            b = j - AHEAD * QUADS
                            logarithm((i + 1) * QUADS + b, b)

                attributes(0, 0)
                for b in range(QUADS):
                    if b < QUADS - 1:
                        attributes(b + 1, b + 1)
                    attributes_turned(b)
                    hidden(b, b)
                for b in range(QUADS):
                    logarithm(b, b)
                first_product(0, 0)
                over_bodies(act, body)

            @block.tensor
            def _(pe):
                def turn_attributes(g, b, first=False):
                    pe.wait_ge(attr_ok, g + 1)
                    if not first:
                        pe.wait_ge(attr_t_ok, g)
                    for j in range(QUAD):
                        last = pe.transpose(turn[0:RBF, j * P:(j + 1) * P], attr[b % 2][:, j, :], c.ident[:])
                    last.then_inc(turned, 1)

                def hidden(g):
                    pe.wait_ge(attr_t_ok, g + 1)
                    pe.wait_ge(aboved, g + 1)
                    pe.matmul(pre[:], wf1[:], attr_t[:], start=True, stop=True).then_inc(pre_ok, 1)

                def sum_up(q, j):
                    k = j % MADE
                    pe.wait_ge(marked, q + 1)
                    pe.wait_ge(added, q + 1)
                    pe.wait_ge(outer, MADE + q + 1)
                    pe.wait_ge(vectored, q + 1)
                    pe.wait_ge(scaled, q + 1)
                    pe.matmul(part[j % 2][:, 0:D], hot[k][:], mess[k][:, P:P + D], start=True, stop=True)
                    pe.matmul(part[j % 2][:, D:2 * D], hot[k][:], mess[k][:, P + D:P + 2 * D], start=True, stop=True)\
                        .then_inc(summed, 1)

                def filter_at(i, j):
                    if j % QUAD == 0:
                        pe.wait_ge(hid_ok, QUADS + i * QUADS + j // QUAD + 1)
                    pe.wait_ge(outer, MADE - 2 + i * BODY + j + 1)
                    pe.matmul(fps[j % 2][:], hid[j // QUAD][:, j % QUAD * P:(j % QUAD + 1) * P], wf2[:],
                              start=True, stop=False)
                    pe.matmul(fps[j % 2][:], ones[:], bf2_rows[:], start=False, stop=True).then_inc(filtered, 1)

                def body(i, more):
                    for j in range(BODY):
                        g, b = (i + 1) * QUADS + j // AHEAD, j // AHEAD
                        if more and b < QUADS and j % AHEAD == 1:
                            turn_attributes(g, b)
                        if more and b < QUADS and j % AHEAD == 2:
                            hidden(g)
                        if j < BODY - 1:
                            filter_at(i, j + 1)
                        elif more:
                            filter_at(i + 1, 0)
                        sum_up(i * BODY + j, j)

                pe.wait_ge(w_in, 64)
                for b in range(QUADS):
                    turn_attributes(b, b, first=b == 0)
                    hidden(b)
                pe.wait_ge(parted, 48)
                filter_at(0, 0)
                over_bodies(pe, body)

            @block.vector
            def _(dve):
                dve.memset(flat, 0.0).then_inc(added, 2)
                dve.sem_inc(summed, RING)
                dve.sem_inc(outer, MADE)
                dve.sem_inc(turned, 2)
                dve.sem_inc(aboved, 1)
                dve.sem_inc(hid_ok, QUADS)

                def hidden(g, b):
                    dve.wait_ge(logged, g + 1)
                    dve.wait_ge(aboved, g + 2)
                    dve.scalar_tensor_tensor(out=hid[b][:], in0=above[b][:], scalar=-LOG2, in1=size[b][:],
                                             op0=ALU.add, op1=ALU.add).then_inc(hid_ok, 1)

                def one_hot(i, j):
                    q, k = i * BODY + j, j % MADE
                    dve.wait_ge(summed, RING - MADE + q + 1)
                    dve.tensor_scalar(hot[k][:], c.iota[:, 0:P],
                                      c.rec_s[:, bass.ds(q, 1), S_LO:S_LO + 1].rearrange("p a b -> p (a b)"),
                                      c.rec_s[:, bass.ds(q, 1), S_W:S_W + 1].rearrange("p a b -> p (a b)"),
                                      ALU.is_equal, ALU.mult).then_inc(marked, 1)

                def message(i, j, more):
                    q, k, slot = i * BODY + j, j % MADE, j % RING
                    node, m = rows[slot], mess[k]

                    def dot(d):
                        dve.scalar_tensor_tensor(out=along[k][:], in0=node[:, (d + 1) * P:(d + 2) * P],
                                                 scalar=c.rec_s[:, bass.ds(q, 1), S_U + d:S_U + d + 1]
                                                 .rearrange("p a b -> p (a b)"),
                                                 in1=along[k][:], op0=ALU.mult, op1=ALU.add).then_inc(dots, 1)

                    dve.wait_ge(filtered, q + 1)
                    dve.tensor_copy(filt[k][:], fps[j % 2][:, 3 * P:4 * P]).then_inc(copied, 1)
                    dve.wait_ge(landed[slot][0], rows_in(i, j))
                    dve.wait_ge(begun, q + 1)
                    dot(1)
                    dve.tensor_tensor(m[:, Q:Q + 2 * P].rearrange("p (a f) -> p a f", a=2),
                                      fps[j % 2][:, 0:2 * P].rearrange("p (a f) -> p a f", a=2),
                                      node[:, 0:P].unsqueeze(1).to_broadcast([P, 2, P]), ALU.mult).then_inc(mixed, 1)
                    dve.wait_ge(dots, q * 2 + 1)
                    dot(2)
                    if more:
                        one_hot(i, j + 1)
                    dve.wait_ge(dots, q * 2 + 2)
                    dve.tensor_tensor(m[:, SB:SB + P], along[k][:], fps[j % 2][:, 2 * P:3 * P], ALU.mult)\
                        .then_inc(outer, 1)

                def add(i, j, tiles):
                    q, tile = i * BODY + j, tiles[j % KNOWN]
                    dve.wait_ge(summed, RING + q + 1)
                    dve.wait_ge(added, 2 + q)
                    there = flat[:, bass.ds(tile * (2 * D), 2 * D)]
                    dve.tensor_tensor(there, there, part[j % 2][:], ALU.add).then_inc(added, 1)

                def body(i, more):
                    for j in range(BODY):
                        if j < BODY - 1:
                            message(i, j + 1, more or j < BODY - 2)
                        elif more:
                            message(i + 1, 0, True)
                        if j % KNOWN == 0:
                            tiles = tiles_of(nc, c, dve, 0, i * BODY + j)
                        add(i, j, tiles)
                        if more and j >= AHEAD * QUADS:
                            b = j - AHEAD * QUADS
                            hidden((i + 1) * QUADS + b, b)

                dve.memset(ones[:], 1.0).then_inc(split, 1)
                dve.wait_ge(w_in, 64)
                for k in range(3):
                    dve.tensor_copy(bf2_part[:, k, :], bf2[:]).then_inc(split, 1)
                    if k < 2:
                        dve.wait_ge(split, 1 + 2 * k + 1)
                        dve.tensor_tensor(bf2[:], bf2[:], bf2_part[:, k, :], ALU.subtract).then_inc(split, 1)
                        dve.wait_ge(split, 1 + 2 * k + 2)
                for b in range(QUADS):
                    hidden(b, b)
                one_hot(0, 0)
                message(0, 0, True)
                over_bodies(dve, body)


def vector_update(nc, c, w1, w2, total):
    with Stage(nc, "t3") as s:
        sums_t = s.sb("sums_t", [P, 8, N])
        size = s.sb("size", [P, N])
        mid = s.sb("mid", [P, 4, N])
        turn = [s.ps(f"turn{k}") for k in range(2)]
        first = [s.ps(f"first{k}") for k in range(2)]
        second = [s.ps(f"second{k}") for k in range(2)]
        w_ok, turned, taken, one, copied, sized, clipped, raised, logged, mid_ok, two, added, chain = (
            s.sem(n) for n in ("w_ok", "turned", "taken", "one", "copied", "sized", "clipped", "raised",
                               "logged", "mid_ok", "two", "added", "chain"))
        kinds = [(0, 1)] + [(2 + i, 5 + i) for i in range(3)]
        scales = [(Y0 / 16, Y1 / math.sqrt(3.0) / 16), (Y1 / 16, Y0 / 16)]
        work = [(o, n) for o in range(4) for n in range(2)]
        with nc.Block() as block:
            @block.tensor
            def _(pe):
                for i in range(NT * 2):
                    if i >= 2:
                        pe.wait_ge(taken, i - 1)
                    for k in range(4):
                        col = (i % 2 * 4 + k) * P
                        last = pe.transpose(turn[i % 2][:, k * P:(k + 1) * P], total[:, i // 2, col:col + P], c.ident[:])
                    last.then_inc(turned, 1)
                pe.wait_ge(w_ok, 6)
                pe.wait_ge(taken, NT * 2)
                for i, (o, n) in enumerate(work):
                    if i >= 2:
                        pe.wait_ge(copied, i - 1)
                    for k in range(2):
                        last = pe.matmul(first[i % 2][:], w1[:, min(o, 1), k, :],
                                         sums_t[:, kinds[o][k], n * D:(n + 1) * D], start=k == 0, stop=k == 1)
                    last.then_inc(one, 1)
                pe.wait_ge(copied, len(work))
                pe.wait_ge(mid_ok, 1)
                for t in range(NT):
                    if t >= 2:
                        pe.wait_ge(added, 2 * (t - 1))
                    for o in range(4):
                        last = pe.matmul(second[t % 2][:, o * P:(o + 1) * P], mid[:, o, t * P:(t + 1) * P],
                                         w2[:, min(o, 1), :], start=True, stop=True)
                    last.then_inc(two, 1)

            @block.scalar
            def _(act):
                for o in range(2):
                    for k in range(2):
                        act.mul(w1[:, o, k, :], w1[:, o, k, :], scales[o][k]).then_inc(w_ok, 1)
                    act.mul(w2[:, o, :], w2[:, o, :], 1.0 / math.sqrt(P)).then_inc(w_ok, 1)
                for i in range(NT * 2):
                    act.wait_ge(turned, i + 1)
                    act.copy(sums_t[:, i % 2 * 4:i % 2 * 4 + 4, i // 2 * P:(i // 2 + 1) * P],
                             turn[i % 2][:].rearrange("p (k n) -> p k n", k=4)).then_inc(taken, 1)
                for i, (o, n) in enumerate(work):
                    act.wait_ge(one, i + 1)
                    act.copy(mid[:, o, n * D:(n + 1) * D], first[i % 2][:]).then_inc(copied, 1)
                    if i == 1:
                        act.wait_ge(copied, 2)
                        act.activation(size[:], mid[:, 0, :], ACT.Abs).then_inc(sized, 1)
                act.wait_ge(sized, 1)
                act.activation(size[:], size[:], ACT.Exp, scale=-1.0).then_inc(raised, 1)
                act.wait_ge(raised, 1)
                act.activation(size[:], size[:], ACT.Ln, bias=c.ones[:, 0:1]).then_inc(logged, 1)

            @block.vector
            def _(dve):
                dve.wait_ge(sized, 1)
                dve.tensor_scalar(mid[:, 0, :], mid[:, 0, :], 0.0, -LOG2, ALU.max, ALU.add).then_inc(clipped, 1)
                dve.wait_ge(clipped, 1)
                dve.wait_ge(logged, 1)
                dve.tensor_tensor(mid[:, 0, :], mid[:, 0, :], size[:], ALU.add).then_inc(mid_ok, 1)
                for t in range(NT):
                    dve.wait_ge(two, t + 1)
                    dve.tensor_tensor(c.X[:, t, 0:P], c.X[:, t, 0:P], second[t % 2][:, 0:P], ALU.add).then_inc(added, 1)
                    there = c.X[:, t, P:D].rearrange("p (d i) -> p d i", i=3)
                    dve.tensor_tensor(there, there, second[t % 2][:, P:D].rearrange("p (i d) -> p d i", i=3),
                                      ALU.add).then_inc(added, 1)



def layer0_messages(nc, c, a):
    with Stage(nc, "l0g") as s:
        c.XLT = s.sb("xlt", [P, DC, N])
        loose_s = s.sb("loose_s", [P, EP, RS])
        of_tile = s.sb("of_tile", [P, EP, 2 * NT])
        bin_edges(nc, c, a, loose_s, of_tile)
        scatter = Scatter(nc, c, s, 0, loose_s, c.by_src, RS)
        ahead, w, bias = table_weights(s, a["L0_gnn_weight_t"], None)
        norm(nc, c, "l0n", c.X, c.XL, turned=c.XLT, scatter=scatter, ahead=ahead)
        node_tables(nc, c, "l0t", w, bias, c.rows, scatter=scatter, of_tile=of_tile)
    aggregate(nc, c, "l0a", 0, c.rec_s, S_OTHER, S_LO, S_W, c.rows[0:N, :], c.X)


def layer0_memory(nc, c, a):
    with Stage(nc, "m0g") as s:
        q = s.sb("q", [P, HEADS, N])
        keys_ahead = Weights(s)
        keys = keys_ahead.add("keys", [P, HEADS, NKEYS], a["L0_ffn_keys_t"])
        with Stage(nc, "m0h") as t:
            c.XLT = t.sb("xlt", [P, DC, N])
            ahead = Weights(t)
            w = ahead.add("w", [P, DC, HEADS * P], by_rows(a["L0_ffn_Wq"]))
            bias = ahead.add("bias", [P, HEADS], a["L0_ffn_bq_t"])
            norm(nc, c, "m0n", c.X, c.XL, turned=c.XLT, ahead=ahead)
            memory_queries(nc, c, w, bias, q, keys_ahead)
        memory_lookup(nc, c, a, q, keys)


def layer1_messages(nc, c, a):
    with Stage(nc, "l1g") as s:
        c.XLT = s.sb("xlt", [P, DC, N])
        agg = s.sb("agg", [P, NT, D])
        w_self = s.sb("w_self", [P, DC, D])
        b_self = s.sb("b_self", [P, D])
        mixed = s.sb("mixed", [P, NT, D])
        with Stage(nc, "l1w") as t:
            ahead, w, bias = table_weights(t, a["L1_gnn_W_rel"], a["L1_gnn_b_rel"])
            ahead.load(w_self[:], by_rows(a["L1_gnn_W_self"]))
            ahead.load(b_self[:], a["L1_gnn_b_self"].partition_broadcast(P))
            norm(nc, c, "l1n", c.X, c.XL, turned=c.XLT, ahead=ahead)
            node_tables(nc, c, "l1t", w, bias, c.rows)
        with Stage(nc, "l1h") as h:
            up, down = Weights(h), Weights(h)
            w1 = up.add("w1", [P, DC, 2 * D], by_rows(a["L1_gnn_W_ffn1"]))
            b1 = up.add("b1", [P, 2 * DC], a["L1_gnn_b_ffn1_t"])
            aggregate(nc, c, "l1a", 1, c.rec_d, D_TYPED, D_LO, D_W, c.rows, agg, clear=True, ahead=up,
                      dense=(w_self, mixed))
            w2 = down.add("w2", [P, 2 * DC, D], by_rows(a["L1_gnn_W_ffn2"]))
            b2 = down.add("b2", [P, D], a["L1_gnn_b_ffn2"].partition_broadcast(P))
            relation_update(nc, c, b_self, agg, mixed, down)
            norm(nc, c, "l1p", mixed, c.XL, affine=(a["L1_gnn_ln1_g"], a["L1_gnn_ln1_b"]), turned=c.XLT)
            relation_mlp(nc, c, w1, b1, w2, b2, c.XL, c.XLT, mixed)
            norm(nc, c, "l1q", mixed, c.XL, affine=(a["L1_gnn_ln2_g"], a["L1_gnn_ln2_b"]), residual=True)


def layer1_experts(nc, c, a):
    with Stage(nc, "l1f") as s:
        c.XLT = s.sb("xlt", [P, DC, N])
        gate_t = s.sb("gate_t", [8, N])
        gate_ahead = Weights(s)
        w = gate_ahead.add("w", [P, DC, 8], by_rows(a["L1_ffn_gate_w_t"]))
        norm(nc, c, "l1r", c.X, c.XL, turned=c.XLT, ahead=gate_ahead)
        ahead, *weights = expert_weights(s, a["L1_ffn_w1_t"], a["L1_ffn_b1_t"], a["L1_ffn_w2_t"], a["L1_ffn_b2"])
        capacity_gates(nc, c, w, gate_t, ahead)
        expert_mix(nc, c, "l1x", gate_t, *weights)


def layer2_messages(nc, c, a):
    with Stage(nc, "tg") as s:
        total = s.sb("total", [P, NT, 2 * D])
        with Stage(nc, "th") as t:
            c.XLT = t.sb("xlt", [P, DC, N])
            ahead = Weights(t)
            w = ahead.add("w", [P, 2, P])
            ahead.load(w[:, 0, :], a["L2_gnn_W_in2f_s"])
            ahead.load(w[:, 1, :], a["L2_gnn_W_in2f_v"])
            norm(nc, c, "tn", c.X, c.XL, turned=c.XLT, ahead=ahead,
                 columns=[slice(0, P)] + [slice(P + i, D, 3) for i in range(3)])
            vector_node_rows(nc, c, w)
        ahead = Weights(s)
        w1 = ahead.add("w1", [P, 2, 2, P])
        w2 = ahead.add("w2", [P, 2, P])
        for k, kind in enumerate(("s", "v")):
            ahead.load(w1[:, k], a[f"L2_gnn_W1_{kind}_t"])
            ahead.load(w2[:, k], a[f"L2_gnn_W2_{kind}"])
        vector_messages(nc, c, a, total, ahead)
        vector_update(nc, c, w1, w2, total)


def layer2_experts(nc, c, a):
    with Stage(nc, "l2f") as s:
        c.XLT = s.sb("xlt", [P, DC, N])
        gate_t = s.sb("gate_t", [8, N])
        gate_ahead = Weights(s)
        w = gate_ahead.add("w", [P, DC, 8], by_rows(a["L2_ffn_Wr"]))
        norm(nc, c, "l2r", c.X, c.XL, turned=c.XLT, ahead=gate_ahead)
        ahead, *weights = expert_weights(s, a["L2_ffn_W1_t"], a["L2_ffn_b1_t"], a["L2_ffn_W2_t"], a["L2_ffn_b2"])
        choice_gates(nc, c, w, gate_t, ahead)
        expert_mix(nc, c, "l2x", gate_t, *weights)


def layer3_messages(nc, c, a):
    with Stage(nc, "l3g") as s:
        c.XLT = s.sb("xlt", [P, DC, N])
        agg = s.sb("agg", [P, NT, D])
        ahead = Weights(s)
        w = ahead.add("w", [P, 2 * DC, D], by_rows(a["L3_gnn_W"]))
        bias = ahead.add("bias", [P, D], a["L3_gnn_b"].partition_broadcast(P))
        own = s.sb("own", [P, NT, D])
        norm(nc, c, "l3n", c.X, c.XL, turned=c.XLT, rows=c.rows, ahead=ahead)
        aggregate(nc, c, "l3a", 1, c.rec_d, D_OTHER, D_LO, None, c.rows[0:N, :], agg, clear=True,
                  dense=(w, own))
        sage_update(nc, c, w, bias, agg, own)


def layer3_expert(nc, c, a):
    with Stage(nc, "l3f") as s:
        c.XLT = s.sb("xlt", [P, DC, N])
        ahead = Weights(s)
        wg = ahead.add("wg", [P, DC, 16], by_rows(a["L3_ffn_Wg"]))
        bg = ahead.add("bg", [P, 16], a["L3_ffn_bg"].partition_broadcast(P))
        norm(nc, c, "l3r", c.X, c.XL, turned=c.XLT, ahead=ahead)
        one_expert(nc, c, a, wg, bg)


LAYERS = [layer0_messages, layer0_memory, layer1_messages, layer1_experts, layer2_messages, layer2_experts,
          layer3_messages, layer3_expert]


def program(nc, a, out, layers=LAYERS):
    with ExitStack() as ctx:
        c = Shared(nc, ctx)
        make_constants(nc, c)
        for layer in layers:
            layer(nc, c, a)
        with nc.semaphore("out_stored") as stored, nc.Block() as block:
            @block.sync
            def _(sp):
                sp.dma_start(out.rearrange("(t p) d -> p t d", p=P), c.X[:, :, :]).then_inc(stored, 16)
                sp.wait_ge(stored, 16)


def layouts(i, np):
    o = {k: i[k] for k in ("x", "src", "dst", "edge_attr_20", "edge_attr_3", "edge_type_4", "edge_weight")}
    o["L0_gnn_weight_t"] = i["L0_gnn_weight"].T[None]
    o["L0_ffn_Wq"] = i["L0_ffn_Wq"]
    o["L0_ffn_bq_t"] = i["L0_ffn_bq"].reshape(HEADS, P).T
    o["L0_ffn_keys_t"] = i["L0_ffn_keys"].transpose(1, 3, 0, 2).reshape(P, HEADS, NKEYS)
    o["L0_ffn_w_rows"] = np.concatenate([i["L0_ffn_w_down"], i["L0_ffn_w_up"]], axis=1)
    for k in ("W_self", "b_self", "W_rel", "b_rel", "ln1_g", "ln1_b", "ln2_g", "ln2_b", "W_ffn1", "W_ffn2", "b_ffn2"):
        o[f"L1_gnn_{k}"] = i[f"L1_gnn_{k}"]
    o["L1_gnn_b_ffn1_t"] = i["L1_gnn_b_ffn1"].reshape(-1, P).T
    o["L1_ffn_gate_w_t"] = i["L1_ffn_gate_w"].T
    for name, w1, b1, w2 in (("L1_ffn", "w1", "b1", "w2"), ("L2_ffn", "W1", "b1", "W2")):
        o[f"{name}_{w1}_t"] = i[f"{name}_{w1}"].transpose(1, 0, 2).reshape(D, 256)
        o[f"{name}_{b1}_t"] = i[f"{name}_{b1}"].reshape(2, P).T
        o[f"{name}_{w2}_t"] = i[f"{name}_{w2}"].reshape(256, D)
        o[f"{name}_b2"] = i[f"{name}_b2"]
    def by_kind(w):
        w = w[..., :4 * P].reshape(*w.shape[:-1], 2, P, 2)
        return np.concatenate([w[..., 1, :, 0], w[..., 0, :, 0], w[..., 0, :, 1], w[..., 1, :, 1]], axis=-1)

    o["L2_gnn_Wf1"] = i["L2_gnn_Wf1"]
    o["L2_gnn_bf1_t"] = i["L2_gnn_bf1"][:, None]
    o["L2_gnn_Wf2_t"] = by_kind(i["L2_gnn_Wf2"])
    o["L2_gnn_bf2_t"] = by_kind(i["L2_gnn_bf2"])
    for k in ("W1_s", "W1_v"):
        o[f"L2_gnn_{k}_t"] = i[f"L2_gnn_{k}"].reshape(P, 2, P)
    for k in ("W_in2f_s", "W_in2f_v", "W2_s", "W2_v"):
        o[f"L2_gnn_{k}"] = i[f"L2_gnn_{k}"]
    for k in ("L2_ffn_Wr", "L3_gnn_W", "L3_gnn_b", "L3_ffn_Wg", "L3_ffn_bg", "L3_ffn_be"):
        o[k] = i[k]
    o["L3_ffn_We_rows"] = i["L3_ffn_We"].reshape(-1, D)
    return {k: np.ascontiguousarray(v) for k, v in o.items()}


def kernel(**inputs):
    import numpy as np
    import concourse.bacc as bacc
    from concourse.bass_utils import run_bass_kernel_spmd

    nc = bacc.Bacc("TRN2", target_bir_lowering=False, num_devices=1)
    arrays = layouts({k: np.asarray(v) for k, v in inputs.items()}, np)
    a = {k: nc.dram_tensor(f"in_{k}", v.shape, mybir.dt.from_np(v.dtype), kind="ExternalInput").ap()
         for k, v in arrays.items()}
    out = nc.dram_tensor("out_x", (N, D), F32, kind="ExternalOutput").ap()
    program(nc, a, out)
    r = run_bass_kernel_spmd(nc, [{f"in_{k}": v for k, v in arrays.items()}], core_ids=[0])
    return r.results[0]["out_x"]
```
